# Optimizing a Trainium2 kernel written in Bass

```python
import numpy as np
import jax
import jax.numpy as jnp

def _softmax(x, axis=-1):
    return jax.nn.softmax(x, axis=axis)

def _gelu(x):
    return jax.nn.gelu(x, approximate=True)

def _silu(x):
    return jax.nn.silu(x)

def _sigmoid(x):
    return jax.nn.sigmoid(x)

def _layernorm(x, axis=-1, eps=1e-05):
    m = jnp.mean(x, axis=axis, keepdims=True)
    v = jnp.var(x, axis=axis, keepdims=True)
    return (x - m) / jnp.sqrt(v + eps)

def _scatter_add(tgt, idx, src, axis=0):
    return tgt.at[idx].add(src)

def _segment_sum(src, seg, n):
    return jax.ops.segment_sum(src, seg, n)
kernel_name = 'mk_adaln_d1_jaxref_r8_d4ba2e'

def setup_inputs(seed: int=0):
    np.random.seed(seed)
    _w = jnp.asarray

    def _L0_attn_setup():
        import jax, jax.numpy as jnp
        import numpy as np
        D_MODEL = 256
        EXPAND = 2
        D_INNER = D_MODEL * EXPAND
        HEAD_DIM = 64
        NHEADS = D_INNER // HEAD_DIM
        D_STATE = 128
        NGROUPS = 8
        D_CONV = 4
        CHUNK = 32
        EPS = 1e-05
        CONV_DIM = D_INNER + 2 * NGROUPS * D_STATE
        D_IN_PROJ = 2 * D_INNER + 2 * NGROUPS * D_STATE + NHEADS

        def _segsum(x):
            T = x.shape[-1]
            cs = jnp.cumsum(x, axis=-1)
            seg = cs[..., :, None] - cs[..., None, :]
            mask = jnp.tril(jnp.ones((T, T), bool))
            return jnp.where(mask, seg, -jnp.inf)
        key = jax.random.key(seed)
        ks = jax.random.split(key, 10)
        B, L = (2, 256)
        scale_in = 1.0 / np.sqrt(D_MODEL)
        scale_out = 1.0 / np.sqrt(D_INNER)
        return {'hidden_states': jax.random.normal(ks[0], (B, L, D_MODEL), jnp.float32), 'W_in': jax.random.normal(ks[1], (D_IN_PROJ, D_MODEL), jnp.float32) * scale_in, 'conv_w': jax.random.normal(ks[2], (CONV_DIM, D_CONV), jnp.float32) * 0.3, 'conv_b': jax.random.normal(ks[3], (CONV_DIM,), jnp.float32) * 0.05, 'A': -jnp.exp(jax.random.uniform(ks[4], (NHEADS,), jnp.float32, 0.0, np.log(16.0))), 'D': jax.random.normal(ks[5], (NHEADS,), jnp.float32), 'dt_bias': jax.random.normal(ks[6], (NHEADS,), jnp.float32) * 0.5, 'norm_weight': jnp.ones((D_INNER,), jnp.float32) + 0.02 * jax.random.normal(ks[7], (D_INNER,), jnp.float32), 'W_out': jax.random.normal(ks[8], (D_MODEL, D_INNER), jnp.float32) * scale_out}
    _L0_attn_in = _L0_attn_setup()

    def _L0_ffn_setup():
        import math
        import jax, jax.numpy as jnp
        import numpy as np
        DIM = 256
        RANK = 8
        B, T = (4, 512)

        def _orthogonal(key, n):
            a = jax.random.normal(key, (n, n), dtype=jnp.float32)
            q, r = jnp.linalg.qr(a)
            q = q * jnp.sign(jnp.diagonal(r))[None, :]
            return q
        key = jax.random.key(seed)
        kx, kf = jax.random.split(key)
        x = jax.random.normal(kx, (B, T, DIM), dtype=jnp.float32)
        fkeys = jax.random.split(kf, RANK)
        factors = jnp.stack([_orthogonal(fkeys[r], DIM) * (r + 1) ** (-0.5) for r in range(RANK)])
        bias = jnp.zeros((DIM,), dtype=jnp.float32)
        return {'x': x, 'factors': factors, 'bias': bias}
    _L0_ffn_in = _L0_ffn_setup()
    _L0_c = _w((lambda *s: np.random.randn(*s).astype(np.float32) * 0.05)(4, 256))
    _L0_wmod = _w((lambda *s: np.random.randn(*s).astype(np.float32) * 0.05)(256, 6 * 256) * 256 ** (-0.5))
    _d = {'L0_attn_hidden_states': _L0_attn_in['hidden_states'], 'L0_attn_W_in': _L0_attn_in['W_in'], 'L0_attn_conv_w': _L0_attn_in['conv_w'], 'L0_attn_conv_b': _L0_attn_in['conv_b'], 'L0_attn_A': _L0_attn_in['A'], 'L0_attn_D': _L0_attn_in['D'], 'L0_attn_dt_bias': _L0_attn_in['dt_bias'], 'L0_attn_norm_weight': _L0_attn_in['norm_weight'], 'L0_attn_W_out': _L0_attn_in['W_out'], 'L0_ffn_factors': _L0_ffn_in['factors'], 'L0_ffn_bias': _L0_ffn_in['bias'], 'L0_c': _L0_c, 'L0_wmod': _L0_wmod}
    _x0 = _d['L0_attn_hidden_states']
    _d['L0_attn_hidden_states'] = jax.random.normal(jax.random.fold_in(jax.random.key(seed), 1), (4, 512, 256), dtype=_x0.dtype)
    del _x0
    return _d

def reference(L0_attn_hidden_states, L0_attn_W_in, L0_attn_conv_w, L0_attn_conv_b, L0_attn_A, L0_attn_D, L0_attn_dt_bias, L0_attn_norm_weight, L0_attn_W_out, L0_ffn_factors, L0_ffn_bias, L0_c, L0_wmod):

    def _L0_attn_ref(hidden_states, W_in, conv_w, conv_b, A, D, dt_bias, norm_weight, W_out):
        import jax, jax.numpy as jnp
        import numpy as np
        D_MODEL = 256
        EXPAND = 2
        D_INNER = D_MODEL * EXPAND
        HEAD_DIM = 64
        NHEADS = D_INNER // HEAD_DIM
        D_STATE = 128
        NGROUPS = 8
        D_CONV = 4
        CHUNK = 32
        EPS = 1e-05
        CONV_DIM = D_INNER + 2 * NGROUPS * D_STATE
        D_IN_PROJ = 2 * D_INNER + 2 * NGROUPS * D_STATE + NHEADS

        def _segsum(x):
            T = x.shape[-1]
            cs = jnp.cumsum(x, axis=-1)
            seg = cs[..., :, None] - cs[..., None, :]
            mask = jnp.tril(jnp.ones((T, T), bool))
            return jnp.where(mask, seg, -jnp.inf)
        B, L, _ = hidden_states.shape
        nc = L // CHUNK
        zxbcdt = jnp.einsum('bld,ed->ble', hidden_states, W_in)
        z = zxbcdt[..., :D_INNER]
        xbc = zxbcdt[..., D_INNER:D_INNER + CONV_DIM]
        dt = zxbcdt[..., D_IN_PROJ - NHEADS:]
        xpad = jnp.pad(xbc, ((0, 0), (D_CONV - 1, 0), (0, 0)))
        acc = conv_b
        conv_out = sum((conv_w[:, k] * xpad[:, k:k + L, :] for k in range(D_CONV))) + conv_b
        xbc = jax.nn.silu(conv_out)
        x = xbc[..., :D_INNER].reshape(B, L, NHEADS, HEAD_DIM)
        Bm = xbc[..., D_INNER:D_INNER + NGROUPS * D_STATE].reshape(B, L, NGROUPS, D_STATE)
        Cm = xbc[..., D_INNER + NGROUPS * D_STATE:].reshape(B, L, NGROUPS, D_STATE)
        dt = jax.nn.softplus(dt + dt_bias)
        rep = NHEADS // NGROUPS
        Bh = jnp.repeat(Bm, rep, axis=2)
        Ch = jnp.repeat(Cm, rep, axis=2)
        x_dt = x * dt[..., None]
        A_dt = dt * A
        xc = x_dt.reshape(B, nc, CHUNK, NHEADS, HEAD_DIM)
        Bc = Bh.reshape(B, nc, CHUNK, NHEADS, D_STATE)
        Cc = Ch.reshape(B, nc, CHUNK, NHEADS, D_STATE)
        Ac = A_dt.reshape(B, nc, CHUNK, NHEADS).transpose(0, 3, 1, 2)
        A_cs = jnp.cumsum(Ac, axis=-1)
        Lmat = jnp.exp(_segsum(Ac))
        Y_diag = jnp.einsum('bclhn,bcshn,bhcls,bcshp->bclhp', Cc, Bc, Lmat, xc)
        decay_states = jnp.exp(A_cs[..., -1:] - A_cs)
        states = jnp.einsum('bcshn,bhcs,bcshp->bchpn', Bc, decay_states, xc)
        A_last = A_cs[..., -1]
        decay_chunk = jnp.exp(_segsum(jnp.pad(A_last, ((0, 0), (0, 0), (1, 0)))))
        states0 = jnp.concatenate([jnp.zeros_like(states[:, :1]), states], axis=1)
        new_states = jnp.einsum('bhzc,bchpn->bzhpn', decay_chunk, states0)
        prev = new_states[:, :-1]
        Y_off = jnp.einsum('bclhn,bchpn,bhcl->bclhp', Cc, prev, jnp.exp(A_cs))
        y = (Y_diag + Y_off).reshape(B, L, NHEADS, HEAD_DIM) + D[None, None, :, None] * x
        y = y.reshape(B, L, D_INNER) * jax.nn.silu(z)
        yg = y.reshape(B, L, NGROUPS, D_INNER // NGROUPS)
        var = jnp.mean(yg * yg, axis=-1, keepdims=True)
        yg = yg * jax.lax.rsqrt(var + EPS)
        y = norm_weight * yg.reshape(B, L, D_INNER)
        return jnp.einsum('ble,de->bld', y, W_out)

    def _L0_ffn_ref(x, factors, bias):
        import math
        import jax, jax.numpy as jnp
        import numpy as np
        DIM = 256
        RANK = 8
        B, T = (4, 512)

        def _orthogonal(key, n):
            a = jax.random.normal(key, (n, n), dtype=jnp.float32)
            q, r = jnp.linalg.qr(a)
            q = q * jnp.sign(jnp.diagonal(r))[None, :]
            return q
        rank = factors.shape[0]
        mixed = jnp.einsum('btd,rde->bte', x, factors)
        mixed = mixed / math.sqrt(rank) + bias
        return mixed
    x = L0_attn_hidden_states
    mod = (_silu(L0_c) @ L0_wmod).reshape(L0_c.shape[0], 6, 1, -1)
    sa, ca, ga, sb, cb, gb = (mod[:, 0], mod[:, 1], mod[:, 2], mod[:, 3], mod[:, 4], mod[:, 5])
    ga = (2 * (ga >= 0) - 1) * jnp.maximum(jnp.abs(ga), 0.25)
    gb = (2 * (gb >= 0) - 1) * jnp.maximum(jnp.abs(gb), 0.25)
    h = _layernorm(x, axis=-1) * (1 + ca) + sa
    x = x + ga * _L0_attn_ref(h, L0_attn_W_in, L0_attn_conv_w, L0_attn_conv_b, L0_attn_A, L0_attn_D, L0_attn_dt_bias, L0_attn_norm_weight, L0_attn_W_out)
    h = _layernorm(x, axis=-1) * (1 + cb) + sb
    x = x + gb * _L0_ffn_ref(h, L0_ffn_factors, L0_ffn_bias)
    return x

_drawn_inputs = setup_inputs


def setup_inputs(seed=0):
    import zlib

    import numpy as np

    out = dict(_drawn_inputs(seed))
    spreads = {'L0_ffn_bias': (0.0, 0.32)}
    factors = {'L0_attn_norm_weight': 8.0}
    for name, (base, spread) in spreads.items():
        noise = np.random.default_rng([zlib.crc32(name.encode()), seed]).standard_normal(out[name].shape)
        drawn = base * np.exp(spread * noise) if base else spread * noise
        out[name] = jnp.asarray(drawn.astype(out[name].dtype))
    for name, factor in factors.items():
        out[name] = (out[name] * factor).astype(out[name].dtype)
    return out
```

```python
from contextlib import ExitStack

import concourse.bass as bass
from concourse import mybir

F32 = mybir.dt.float32
F32R = mybir.dt.float32r
ALU = mybir.AluOpType
ACT = mybir.ActivationFunctionType
AX_X = mybir.AxisListType.X

P = 128
BATCH, SEQ, DM = 4, 512, 256
DI, HD, NH = 512, 64, 8
NS = 128
TAPS = 4
NC = SEQ // P
KD = DM // P
UNITS = NH // 2
TPU = 5
TILES = UNITS * TPU
UW = TPU * P
RANK = 8
EPS = 1e-5
RING = 3
SLOTS = 4
WIDE = TILES + NC
CONSTS = 13
MASKED = -1e30


class Signal:

    def __init__(self, ctx, nc, name, per_batch, step=1):
        self.sem = ctx.enter_context(nc.semaphore(name))
        self.per_batch, self.step = per_batch, step

    def prime(self, eng):
        eng.sem_inc(self.sem, self.per_batch * self.step)

    def done(self, b, n):
        return b * (self.per_batch * self.step) + (self.per_batch + n + 1) * self.step


def ring_index(t):
    return t if t < TPU else t + NC


def build(nc, x_in, w_xbc, w_z, w_dt, conv_w, conv_b, a_row, d_row, dtb_row, norm_w, w_out,
          factors, ffn_bias, c_t, w_mod, out):
    ctx = ExitStack()
    with ctx:
        def sb(name, shape, dt=F32):
            return ctx.enter_context(nc.sbuf_tensor(name, shape, dt))

        def sem(name):
            return ctx.enter_context(nc.semaphore(name))

        def signal(name, per_batch, step=1):
            return Signal(ctx, nc, name, per_batch, step)

        bank = [ctx.enter_context(nc.psum_tensor(f"bank{i}", [P, 512], F32)) for i in range(8)]

        stage = sb("stage", [P, KD * (UNITS * UW + DI)])
        w_hi = sb("w_hi", [P, KD * (UNITS * UW + DI)], F32R)
        w_lo = sb("w_lo", [P, KD * (UNITS * UW + DI)], F32R)
        wdt = sb("wdt", [P, KD * NH])
        cw = sb("cw", [P, TILES * TAPS])
        cb = sb("cb", [P, TILES])
        arow = sb("arow", [P, NH])
        drow = sb("drow", [P, NH])
        dtb = sb("dtb", [P, NH])
        nw = sb("nw", [P, UNITS])
        wo = sb("wo", [P, UNITS * DM])
        fsum = sb("fsum", [P, KD * DM])
        fbias = sb("fbias", [P, DM])
        ct = sb("ct", [P, KD * BATCH])
        ident = sb("ident", [P, P])
        identr = sb("identr", [P, P], F32R)
        tri = sb("tri", [P, P])
        ones = sb("ones", [P, P])
        neg = sb("neg", [P, P], F32R)
        selb = sb("selb", [BATCH, BATCH * P])
        eps = sb("eps", [P, 8])
        half = sb("half", [P, 8])
        mod_all = sb("mod_all", [P, BATCH * 8])
        modb = sb("modb", [P, 8])
        grow = sb("grow", [BATCH, 2 * DM])
        gmag = sb("gmag", [BATCH, 2 * DM])
        gab = sb("gab", [P, BATCH * 2 * DM])

        xs = sb("xs", [P, 2 * NC * DM])
        stats = sb("stats", [P, NC * 6])
        mv = sb("mv", [P, NC * 2])
        veps = sb("veps", [P, 8])
        rstd = sb("rstd", [P, 8])
        xn = sb("xn", [P, NC * DM])
        h = sb("h", [P, KD * SEQ])
        h_hi = sb("h_hi", [P, KD * SEQ], F32R)
        h_lo = sb("h_lo", [P, KD * SEQ], F32R)
        NQ = NC * NH
        dtu = sb("dtu", [P, NQ])
        dta = sb("dta", [P, NQ])
        dte = sb("dte", [P, NQ])
        dtl = sb("dtl", [P, NQ])
        dt = sb("dt", [P, NQ])
        adt = sb("adt", [P, NQ])
        nacs = sb("nacs", [P, NQ])
        exin = sb("exin", [P, 2 * NQ])
        exout = sb("exout", [P, 2 * NQ])
        eacs = sb("eacs", [P, NQ])
        wdec = sb("wdec", [P, NQ])
        acs_hi = sb("acs_hi", [NQ, P], F32R)
        acs_lo = sb("acs_lo", [NQ, P], F32R)
        E = sb("E", [P, NH * NC * P])
        part = sb("part", [P, SLOTS * SEQ])
        tap0 = sb("tap0", [P, SLOTS * SEQ])
        xbc = sb("xbc", [P, 2 * TPU * SEQ])
        w_mod_sb = xbc
        zs = stage[:, 0:NC * DI]
        yg = stage[:, NC * DI:NC * DI + UNITS * SEQ]
        yT = stage[:, NC * DI + UNITS * SEQ:NC * DI + 2 * UNITS * SEQ]
        xtok = sb("xtok", [P, SEQ])
        xdt = sb("xdt", [P, SEQ])
        xw = sb("xw", [P, SEQ])
        xd = sb("xd", [P, SEQ])
        btok = sb("btok", [P, 2 * SEQ])
        M = E
        prev = sb("prev", [P, 3 * P])
        toff = sb("toff", [P, SEQ])
        ysum = sb("ysum", [P, SEQ])
        sq = sb("sq", [P, SEQ])
        ms = sb("ms", [P, 8])
        mse = sb("mse", [P, 8])
        rms = sb("rms", [P, 8])
        tail = sb("tail", [P, 2 * NC * DM])
        x2, tmp = tail[:, 0:NC * DM], tail[:, NC * DM:2 * NC * DM]
        fac = tail
        gbb = sb("gbb", [P, DM])

        ld_small, ld_mod, ld_z, ld_rest, ld_fac = (sem(n) for n in ("ld_small", "ld_mod", "ld_z", "ld_rest", "ld_fac"))
        ld_w = [sem(f"ld_w{g}") for g in range(UNITS)]
        consts = sem("consts")
        w_hi_done = sem("w_hi_done")
        w_lo_done = sem("w_lo_done")
        c_silu = sem("c_silu")
        mod_ps = sem("mod_ps")
        mod_sb = sem("mod_sb")
        gate_ps = sem("gate_ps")
        gate_sb = sem("gate_sb")
        wo_done = sem("wo_done")
        fsum_step = sem("fsum_step")
        f_done = sem("f_done")

        x_loaded = signal("x_loaded", 1, 16)
        stored = signal("stored", 1, 16)
        modb_ready = signal("modb_ready", 2)
        stats_done = signal("stats_done", 2 * NC)
        var_ready = signal("var_ready", 2 * NC)
        veps_ready = signal("veps_ready", 2)
        rstd_ready = signal("rstd_ready", 2)
        xn_ready = signal("xn_ready", 2 * NC)
        hT_ps = signal("hT_ps", 2 * KD)
        h_ready = signal("h_ready", 2 * KD)
        hhi_ready = signal("hhi_ready", KD)
        hlo_ready = signal("hlo_ready", KD)
        dt_ps = signal("dt_ps", 1)
        dt_step = signal("dt_step", 3)
        sp_step = signal("sp_step", 2)
        adt_ready = signal("adt_ready", 1)
        acs_ps = signal("acs_ps", 1)
        nacs_ready = signal("nacs_ready", 1)
        exin_ready = signal("exin_ready", 1)
        acs_ready = signal("acs_ready", 2)
        exout_ready = signal("exout_ready", 2)
        wdec_ready = signal("wdec_ready", 1)
        seg_ps = signal("seg_ps", NH)
        e_ready = signal("e_ready", NH)
        wide_ps = signal("wide_ps", WIDE)
        taps_ready = signal("taps_ready", TILES)
        uv_ready = signal("uv_ready", TILES)
        s_ready = signal("s_ready", TILES)
        xbc_ready = signal("xbc_ready", TILES)
        z_ready = signal("z_ready", NC)
        xT_ps = signal("xT_ps", UNITS)
        xtok_ready = signal("xtok_ready", UNITS)
        xdt_ready = signal("xdt_ready", UNITS)
        xw_ready = signal("xw_ready", UNITS)
        xd_ready = signal("xd_ready", UNITS)
        g_ps = signal("g_ps", 2 * UNITS)
        m_ready = signal("m_ready", 2 * UNITS)
        bT_ps = signal("bT_ps", 2 * UNITS)
        btok_ready = signal("btok_ready", 2 * UNITS)
        st_ps = signal("st_ps", UNITS)
        prev_ready = signal("prev_ready", 3 * UNITS)
        ydiag_ps = signal("ydiag_ps", UNITS)
        yoff_ps = signal("yoff_ps", UNITS)
        toff_ready = signal("toff_ready", UNITS)
        ysum_ready = signal("ysum_ready", UNITS)
        yd_ready = signal("yd_ready", UNITS)
        yg_ready = signal("yg_ready", UNITS)
        sq_ready = signal("sq_ready", UNITS)
        ms_ready = signal("ms_ready", UNITS)
        mse_ready = signal("mse_ready", UNITS)
        rms_ready = signal("rms_ready", UNITS)
        yn_ready = signal("yn_ready", UNITS)
        yT_ps = signal("yT_ps", UNITS)
        yT_ready = signal("yT_ready", UNITS)
        attn_ps = signal("attn_ps", 2)
        gated = signal("gated", 2)
        x2_ready = signal("x2_ready", 2)
        gbb_ready = signal("gbb_ready", 1)
        x2b_ready = signal("x2b_ready", 1)
        ffn_ps = signal("ffn_ps", 2)
        ffn_gated = signal("ffn_gated", 2)
        out_ready = signal("out_ready", 2)

        WZ = UNITS * KD * UW

        def w_tile(w, g, k, j):
            at = g * KD * UW + k * UW + j * P
            return w[:, at:at + P]

        def xbc_tile(g, j):
            at = ((g % 2) * TPU + j) * SEQ
            return xbc[:, at:at + SEQ]

        def slot(buf, t):
            at = (t % SLOTS) * SEQ
            return buf[:, at:at + SEQ]

        def chunk(ap, c):
            return ap[:, c * P:(c + 1) * P]

        def per_head(tile, g, c0=0):
            v = tile.rearrange("p (c h) -> p c h", c=NC)[:, c0:NC, 2 * g:2 * g + 2]
            return v.unsqueeze(3).broadcast_to([P, NC - c0, 2, HD])

        def by_head(ap, c0=0):
            return ap.rearrange("p (c h d) -> p c h d", h=2, d=HD)

        block = ctx.enter_context(nc.Block())

        @block.sync
        def _(sp):
            x_loaded.prime(sp)
            stored.prime(sp)
            x_rows = x_in.rearrange("b (c p) d -> p b c d", p=P)
            out_rows = out.rearrange("b (c p) d -> p b c d", p=P)

            def load_x(b):
                dst = xs[:, bass.ds((b % 2) * (NC * DM), NC * DM)].rearrange("p (o c d) -> p o c d", o=1, c=NC)
                sp.dma_start(dst, x_rows[:, bass.ds(b, 1)]).then_inc(x_loaded.sem, 16)

            load_x(0)
            sp.dma_start(ct[:], c_t).then_inc(ld_small, 16)
            sp.dma_start(w_mod_sb[:, 0:KD * 6 * DM], w_mod).then_inc(ld_mod, 16)
            for dst, src in ((wdt, w_dt), (cw, conv_w), (cb, conv_b), (arow, a_row), (drow, d_row), (dtb, dtb_row), (nw, norm_w)):
                sp.dma_start(dst[:], src).then_inc(ld_small, 16)
            for g in range(UNITS):
                sp.dma_start(stage[:, g * KD * UW:(g + 1) * KD * UW], w_xbc[g]).then_inc(ld_w[g], 16)
                if g == 0:
                    sp.dma_start(stage[:, WZ:WZ + KD * DI], w_z).then_inc(ld_z, 16)
            sp.dma_start(wo[:], w_out).then_inc(ld_rest, 16)
            sp.dma_start(fbias[:], ffn_bias).then_inc(ld_rest, 16)
            half_rank = RANK // 2 * KD * DM
            sp.dma_start(fac[:], factors[:, 0:half_rank]).then_inc(ld_fac, 16)
            sp.wait_ge(x_loaded.sem, x_loaded.done(0, 0))
            load_x(1)
            sp.wait_ge(fsum_step, RANK // 2 - 1)
            sp.dma_start(fac[:], factors[:, half_rank:2 * half_rank]).then_inc(ld_fac, 16)

            def store(b):
                sp.wait_ge(out_ready.sem, out_ready.done(b, 1))
                src = tmp.rearrange("p (o c d) -> p o c d", o=1, c=NC)
                sp.dma_start(out_rows[:, bass.ds(b, 1)], src).then_inc(stored.sem, 16)

            with sp.Fori(0, BATCH - 2) as b:
                store(b)
                sp.wait_ge(x_loaded.sem, x_loaded.done(b, 1))
                sp.wait_ge(x2_ready.sem, x2_ready.done(b, 1))
                load_x(b + 2)
            with sp.Fori(BATCH - 2, BATCH) as b:
                store(b)
            sp.wait_ge(stored.sem, stored.done(BATCH - 1, 0))

        @block.gpsimd
        def _(pool):
            for s in (veps_ready, rstd_ready, s_ready, xdt_ready, xw_ready, xd_ready, yd_ready, yg_ready,
                      mse_ready, rms_ready, x2b_ready, gbb_ready):
                s.prime(pool)
            made = [0]

            def make(ins):
                ins.then_inc(consts, 1)
                made[0] += 1

            make(pool.memset(ident[:], 0.0))
            make(pool.memset(selb[:], 0.0))
            make(pool.memset(ones[:], 1.0))
            make(pool.memset(tap0[:], 0.0))
            make(pool.memset(toff[:], 0.0))
            make(pool.memset(half[:], -0.5))
            make(pool.memset(eps[:], EPS))
            make(pool.memset(neg[:].bitcast(F32), 0.0))
            pool.wait_ge(consts, made[0])
            make(pool.affine_select(out=ident[:], in_=ident[:], compare_op=ALU.not_equal, fill=1.0,
                                    base=0, pattern=[[-1, P]], channel_multiplier=1))
            sb3 = selb[:].rearrange("p (b m) -> p b m", b=BATCH)
            make(pool.affine_select(out=sb3, in_=sb3, compare_op=ALU.not_equal, fill=1.0,
                                    base=0, pattern=[[-1, BATCH], [0, P]], channel_multiplier=1))
            make(pool.affine_select(out=tri[:], in_=ones[:], compare_op=ALU.is_ge, fill=0.0,
                                    base=0, pattern=[[1, P]], channel_multiplier=-1))
            make(pool.affine_select(out=neg[:], in_=neg[:].bitcast(F32), compare_op=ALU.is_ge, fill=MASKED,
                                    base=0, pattern=[[1, P]], channel_multiplier=-1))
            pool.wait_ge(consts, made[0])
            make(pool.affine_select(out=identr[:], in_=ident[:], compare_op=ALU.is_ge, fill=0.0,
                                    base=0, pattern=[[0, P]], channel_multiplier=0))
            assert made[0] == CONSTS

            def rstd_of(b, n, src_ready, src_at):
                pool.wait_ge(src_ready.sem, src_ready.done(b, src_at))
                var = mv[:].rearrange("p (c s) -> p c s", s=2)[:, :, 1]
                pool.tensor_tensor(veps[:, 0:NC], var, eps[:, 0:NC], ALU.add).then_inc(veps_ready.sem, 1)
                pool.wait_ge(veps_ready.sem, veps_ready.done(b, n))
                pool.tensor_tensor(rstd[:, 0:NC], veps[:, 0:NC], half[:, 0:NC], ALU.pow).then_inc(rstd_ready.sem, 1)

            def sums(b, g):
                for t in range(g * TPU, (g + 1) * TPU):
                    pool.wait_ge(uv_ready.sem, uv_ready.done(b, t))
                    pool.tensor_tensor(slot(part, t), slot(part, t), slot(tap0, t), ALU.add).then_inc(s_ready.sem, 1)

            def scale_x(b, g):
                pool.wait_ge(xtok_ready.sem, xtok_ready.done(b, g))
                pool.wait_ge(wdec_ready.sem, wdec_ready.done(b, 0))
                pool.wait_ge(ydiag_ps.sem, ydiag_ps.done(b, g - 1))
                pool.tensor_tensor(by_head(xdt[:]), by_head(xtok[:]), per_head(dt[:], g), ALU.mult).then_inc(xdt_ready.sem, 1)
                pool.wait_ge(st_ps.sem, st_ps.done(b, g - 1))
                pool.tensor_tensor(by_head(xw[:]), by_head(xtok[:]), per_head(wdec[:], g), ALU.mult).then_inc(xw_ready.sem, 1)
                pool.wait_ge(yg_ready.sem, yg_ready.done(b, g - 1))
                dd = drow[:, 2 * g:2 * g + 2].unsqueeze(1).unsqueeze(3).broadcast_to([P, NC, 2, HD])
                pool.tensor_tensor(by_head(xd[:]), by_head(xtok[:]), dd, ALU.mult).then_inc(xd_ready.sem, 1)

            def gate_y(b, g):
                pool.wait_ge(ysum_ready.sem, ysum_ready.done(b, g))
                pool.wait_ge(xd_ready.sem, xd_ready.done(b, g))
                pool.tensor_tensor(xd[:], xd[:], ysum[:], ALU.add).then_inc(yd_ready.sem, 1)
                pool.wait_ge(yd_ready.sem, yd_ready.done(b, g))
                pool.wait_ge(z_ready.sem, z_ready.done(b, NC - 1))
                pool.wait_ge(yT_ps.sem, yT_ps.done(b, g - UNITS))
                z = zs.rearrange("p (c i) -> p c i", c=NC)[:, :, g * P:(g + 1) * P]
                dst = yg[:, g * SEQ:(g + 1) * SEQ].rearrange("p (c i) -> p c i", c=NC)
                pool.tensor_tensor(dst, xd[:].rearrange("p (c i) -> p c i", c=NC), z, ALU.mult).then_inc(yg_ready.sem, 1)

            def rms_of(b, g):
                pool.wait_ge(ms_ready.sem, ms_ready.done(b, g))
                pool.tensor_tensor(mse[:], ms[:], eps[:], ALU.add).then_inc(mse_ready.sem, 1)
                pool.wait_ge(mse_ready.sem, mse_ready.done(b, g))
                pool.wait_ge(yn_ready.sem, yn_ready.done(b, g - 1))
                pool.tensor_tensor(rms[:], mse[:], half[:], ALU.pow).then_inc(rms_ready.sem, 1)

            FW = KD * DM
            for r in range(1, RANK):
                pool.wait_ge(ld_fac, 16 if r < RANK // 2 else 32)
                at = (r % (RANK // 2)) * FW
                first = fac[:, 0:FW] if r == 1 else fsum[:]
                pool.tensor_tensor(fsum[:], first, fac[:, at:at + FW], ALU.add).then_inc(fsum_step, 1)
                pool.wait_ge(fsum_step, r)
            pool.wait_ge(ld_small, 16 * 8)

            with pool.Fori(0, BATCH) as b:
                rstd_of(b, 0, var_ready, NC - 1)
                sums(b, 0)
                for g in range(UNITS):
                    if g + 1 < UNITS:
                        sums(b, g + 1)
                    scale_x(b, g)
                    if g > 0:
                        rms_of(b, g - 1)
                    gate_y(b, g)
                rms_of(b, UNITS - 1)
                pool.wait_ge(gate_sb, BATCH)
                pool.wait_ge(ld_rest, 32)
                gb = gab[:, bass.ds(b * (2 * DM) + DM, DM)]
                pool.wait_ge(x2b_ready.sem, x2b_ready.done(b, -1))
                pool.tensor_tensor(gbb[:], gb, fbias[:], ALU.mult).then_inc(gbb_ready.sem, 1)
                rstd_of(b, 1, var_ready, 2 * NC - 1)
                pool.wait_ge(gbb_ready.sem, gbb_ready.done(b, 0))
                pool.wait_ge(xn_ready.sem, xn_ready.done(b, 2 * NC - 1))
                x2v = x2.rearrange("p (c d) -> p c d", c=NC)
                bias = gbb[:].unsqueeze(1).broadcast_to([P, NC, DM])
                pool.tensor_tensor(x2v, x2v, bias, ALU.add).then_inc(x2b_ready.sem, 1)

        @block.scalar
        def _(act):
            for s in (h_ready, sp_step, exout_ready, e_ready, taps_ready, xbc_ready, z_ready, xtok_ready,
                      btok_ready, sq_ready, yT_ready):
                s.prime(act)
            act.wait_ge(ld_small, 16 * 8)
            act.activation(ct[:], ct[:], ACT.Silu).then_inc(c_silu, 1)
            for n in range(5):
                g = (0, None, 1, 2, 3)[n]
                act.wait_ge(ld_z if g is None else ld_w[g], 16)
                lo, size = (WZ, KD * DI) if g is None else (g * KD * UW, KD * UW)
                act.activation(w_hi[:, lo:lo + size], stage[:, lo:lo + size], ACT.Copy).then_inc(w_hi_done, 1)
            for i in range(BATCH):
                act.wait_ge(gate_ps, i + 1)
                act.activation(gab[:, i * 2 * DM:(i + 1) * 2 * DM], bank[1 + i % 2][:], ACT.Copy).then_inc(gate_sb, 1)

            def evac_h(b, n):
                act.wait_ge(modb_ready.sem, modb_ready.done(b, n))
                for k in range(KD):
                    act.wait_ge(hT_ps.sem, hT_ps.done(b, n * KD + k))
                    act.activation(h[:, k * SEQ:(k + 1) * SEQ], bank[(3, 6)[k]][:], ACT.Identity,
                                   bias=modb[:, 4 * n + k:4 * n + k + 1],
                                   scale=modb[:, 4 * n + 2 + k:4 * n + 3 + k]).then_inc(h_ready.sem, 1)

            def taps(b, t):
                n = ring_index(t)
                ps = bank[n % RING]
                act.wait_ge(wide_ps.sem, wide_ps.done(b, n))
                act.wait_ge(s_ready.sem, s_ready.done(b, t - SLOTS))
                act.wait_ge(xbc_ready.sem, xbc_ready.done(b, t - SLOTS))
                act.activation(slot(part, t), ps[:], ACT.Identity, bias=cb[:, t:t + 1],
                               scale=cw[:, TAPS * t + 3:TAPS * t + 4])
                act.activation(slot(tap0, t)[:, 2:SEQ], ps[:, 0:SEQ - 2], ACT.Copy,
                               scale=cw[:, TAPS * t + 1:TAPS * t + 2]).then_inc(taps_ready.sem, 1)

            def silu(b, t):
                g, j = divmod(t, TPU)
                act.wait_ge(s_ready.sem, s_ready.done(b, t))
                act.wait_ge(yoff_ps.sem, yoff_ps.done(b, g - 2))
                act.activation(xbc_tile(g, j), slot(part, t), ACT.Silu).then_inc(xbc_ready.sem, 1)

            def project(b, g):
                t0 = g * TPU
                for j in range(TPU + 2):
                    if j < TPU:
                        taps(b, t0 + j)
                    if j >= 2:
                        silu(b, t0 + j - 2)

            def silu_z(b):
                for c in range(NC):
                    n = TPU + c
                    act.wait_ge(wide_ps.sem, wide_ps.done(b, n))
                    act.wait_ge(yg_ready.sem, yg_ready.done(b, -1))
                    act.activation(zs[:, c * DI:(c + 1) * DI], bank[n % RING][:], ACT.Silu).then_inc(z_ready.sem, 1)

            def decays(b):
                act.preload_act_table_set("natural_log_exp_and_others")
                act.wait_ge(dt_step.sem, dt_step.done(b, 1))
                act.activation(dte[:], dta[:], ACT.Exp, scale=-1.0).then_inc(sp_step.sem, 1)
                act.wait_ge(sp_step.sem, sp_step.done(b, 0))
                act.activation(dtl[:], dte[:], ACT.Ln, bias=1.0).then_inc(sp_step.sem, 1)
                act.wait_ge(nacs_ready.sem, nacs_ready.done(b, 0))
                act.wait_ge(toff_ready.sem, toff_ready.done(b, -1))
                act.activation(eacs[:], nacs[:], ACT.Exp, scale=-1.0).then_inc(exout_ready.sem, 1)
                act.wait_ge(exin_ready.sem, exin_ready.done(b, 0))
                act.activation(exout[:], exin[:], ACT.Exp).then_inc(exout_ready.sem, 1)
                act.wait_ge(ydiag_ps.sem, ydiag_ps.done(b, -1))
                for hh in range(NH):
                    act.wait_ge(seg_ps.sem, seg_ps.done(b, hh))
                    for c in range(NC):
                        q = c * NH + hh
                        ins = act.activation(E[:, (hh * NC + c) * P:(hh * NC + c + 1) * P],
                                             chunk(bank[4 + hh % 2], c), ACT.Exp, bias=nacs[:, q:q + 1])
                    ins.then_inc(e_ready.sem, 1)

            def evac_unit(b, g):
                act.wait_ge(xT_ps.sem, xT_ps.done(b, g))
                act.wait_ge(xd_ready.sem, xd_ready.done(b, g - 1))
                act.activation(xtok[:], bank[3][:], ACT.Copy).then_inc(xtok_ready.sem, 1)
                act.wait_ge(st_ps.sem, st_ps.done(b, g - 1))
                for hh in range(2):
                    act.wait_ge(bT_ps.sem, bT_ps.done(b, 2 * g + hh))
                    act.activation(btok[:, hh * SEQ:(hh + 1) * SEQ], bank[(6, 3)[hh]][:], ACT.Copy).then_inc(btok_ready.sem, 1)

            def square(b, g):
                act.wait_ge(yg_ready.sem, yg_ready.done(b, g))
                act.wait_ge(ms_ready.sem, ms_ready.done(b, g - 1))
                act.activation(sq[:], yg[:, g * SEQ:(g + 1) * SEQ], ACT.Square, scale=HD ** -0.5).then_inc(sq_ready.sem, 1)

            def evac_y(b, g):
                act.wait_ge(yT_ps.sem, yT_ps.done(b, g))
                act.wait_ge(attn_ps.sem, attn_ps.done(b, -1))
                act.activation(yT[:, g * SEQ:(g + 1) * SEQ], bank[6][:], ACT.Copy).then_inc(yT_ready.sem, 1)

            act.wait_ge(ld_rest, 32)
            for g in range(UNITS):
                act.activation(wo[:, g * DM:(g + 1) * DM], wo[:, g * DM:(g + 1) * DM], ACT.Copy,
                               scale=nw[:, g:g + 1]).then_inc(wo_done, 1)
            act.wait_ge(fsum_step, RANK - 1)
            act.activation(fsum[:], fsum[:], ACT.Copy, scale=float(RANK) ** -0.5).then_inc(f_done, 1)
            act.wait_ge(consts, CONSTS)

            with act.Fori(0, BATCH) as b:
                act.wait_ge(ffn_ps.sem, ffn_ps.done(b, -1))
                evac_h(b, 0)
                project(b, 0)
                silu_z(b)
                decays(b)
                for g in range(UNITS):
                    if g + 1 < UNITS:
                        project(b, g + 1)
                    evac_unit(b, g)
                    if g > 0:
                        evac_y(b, g - 1)
                    square(b, g)
                evac_y(b, UNITS - 1)
                act.wait_ge(hlo_ready.sem, hlo_ready.done(b, KD - 1))
                act.wait_ge(dt_ps.sem, dt_ps.done(b, 0))
                evac_h(b, 1)

        @block.vector
        def _(dve):
            for s in (modb_ready, stats_done, var_ready, xn_ready, hhi_ready, hlo_ready, dt_step, adt_ready,
                      nacs_ready, exin_ready, acs_ready, wdec_ready, uv_ready, m_ready, prev_ready, toff_ready,
                      ysum_ready, ms_ready, yn_ready, gated, x2_ready, ffn_gated, out_ready):
                s.prime(dve)

            dve.wait_ge(mod_ps, 1)
            dst = mod_all[:].rearrange("p (b n) -> p b n", b=BATCH)
            src = bank[0][:, 0:8 * BATCH].rearrange("p (n b) -> p b n", b=BATCH)
            for n0 in (0, 4):
                dve.tensor_copy(dst[:, :, n0:n0 + 2], src[:, :, n0:n0 + 2])
                dve.tensor_scalar(dst[:, :, n0 + 2:n0 + 4], src[:, :, n0 + 2:n0 + 4], 1.0, None, ALU.add).then_inc(mod_sb, 1)
            dve.wait_ge(mod_ps, 2)
            gps = bank[1][0:BATCH, :]
            dve.tensor_scalar(gmag[:], gps, -1.0, 0.25, ALU.mult, ALU.max).then_inc(mod_sb, 1)
            dve.wait_ge(mod_sb, 3)
            dve.scalar_tensor_tensor(gmag[:], gps, 1.0, gmag[:], ALU.mult, ALU.max).then_inc(mod_sb, 1)
            dve.tensor_scalar(grow[:], gps, 0.0, 2.0, ALU.is_ge, ALU.mult).then_inc(mod_sb, 1)
            dve.wait_ge(mod_sb, 5)
            dve.scalar_tensor_tensor(grow[:], grow[:], 1.0, gmag[:], ALU.subtract, ALU.mult).then_inc(mod_sb, 1)
            for n in range(5):
                g = (0, None, 1, 2, 3)[n]
                lo, size = (WZ, KD * DI) if g is None else (g * KD * UW, KD * UW)
                dve.wait_ge(w_hi_done, n + 1)
                dve.tensor_tensor(w_lo[:, lo:lo + size], stage[:, lo:lo + size],
                                  w_hi[:, lo:lo + size].bitcast(F32), ALU.subtract).then_inc(w_lo_done, 1)
            dve.wait_ge(mod_sb, 6)
            dve.wait_ge(ld_small, 16 * 8)
            dve.wait_ge(consts, CONSTS)
            dve.wait_ge(gate_sb, BATCH)

            def norm(b, n, x_of):
                dve.wait_ge(rstd_ready.sem, rstd_ready.done(b, n - 1))
                for c in range(NC):
                    dve.bn_stats(stats[:, 6 * c:6 * c + 6], x_of(c)).then_inc(stats_done.sem, 1)
                dve.wait_ge(h_ready.sem, h_ready.done(b, n * KD - KD - 1))
                dve.wait_ge(stats_done.sem, stats_done.done(b, (n + 1) * NC - 1))
                dve.tensor_copy(modb[:, 4 * n:4 * n + 4], mod_all[:, bass.ds(b * 8 + 4 * n, 4)]).then_inc(modb_ready.sem, 1)
                for c in range(NC):
                    dve.bn_aggr(mv[:, 2 * c:2 * c + 2], stats[:, 6 * c:6 * c + 6]).then_inc(var_ready.sem, 1)
                dve.wait_ge(hT_ps.sem, hT_ps.done(b, n * KD - 1))
                dve.wait_ge(rstd_ready.sem, rstd_ready.done(b, n))
                for c in range(NC):
                    dve.tensor_scalar(xn[:, c * DM:(c + 1) * DM], x_of(c), mv[:, 2 * c:2 * c + 1],
                                      rstd[:, c:c + 1], ALU.subtract, ALU.mult).then_inc(xn_ready.sem, 1)

            def split_h(b):
                dve.wait_ge(wide_ps.sem, wide_ps.done(b, -1))
                for k in range(KD):
                    s = slice(k * SEQ, (k + 1) * SEQ)
                    dve.wait_ge(h_ready.sem, h_ready.done(b, k))
                    dve.tensor_copy(h_hi[:, s], h[:, s]).then_inc(hhi_ready.sem, 1)
                    dve.wait_ge(hhi_ready.sem, hhi_ready.done(b, k))
                    dve.tensor_tensor(h_lo[:, s], h[:, s], h_hi[:, s].bitcast(F32), ALU.subtract).then_inc(hlo_ready.sem, 1)

            def rows(ap):
                return ap.rearrange("p (c h) -> p c h", c=NC)

            def row(ap):
                return ap.unsqueeze(1).broadcast_to([P, NC, NH])

            def raw_steps(b):
                dve.wait_ge(dt_ps.sem, dt_ps.done(b, 0))
                dve.tensor_tensor(rows(dtu[:]), rows(bank[7][:, 0:NQ]), row(dtb[:]), ALU.add).then_inc(dt_step.sem, 1)
                dve.wait_ge(dt_step.sem, dt_step.done(b, 0))
                dve.scalar_tensor_tensor(dta[:], dtu[:], -1.0, dtu[:], ALU.mult, ALU.max).then_inc(dt_step.sem, 1)

            def steps(b):
                dve.wait_ge(sp_step.sem, sp_step.done(b, 1))
                dve.wait_ge(xdt_ready.sem, xdt_ready.done(b, -1))
                dve.scalar_tensor_tensor(dt[:], dtu[:], 0.0, dtl[:], ALU.max, ALU.add).then_inc(dt_step.sem, 1)
                dve.wait_ge(dt_step.sem, dt_step.done(b, 2))
                dve.tensor_tensor(rows(adt[:]), rows(dt[:]), row(arow[:]), ALU.mult).then_inc(adt_ready.sem, 1)

            def sums(b):
                acs, tot, acsT = bank[7][:, NQ:2 * NQ], bank[7][:, 2 * NQ:3 * NQ], bank[7][0:NQ, P:2 * P]
                dve.wait_ge(acs_ps.sem, acs_ps.done(b, 0))
                dve.tensor_copy(acs_hi[:], acsT).then_inc(acs_ready.sem, 1)
                dve.tensor_scalar(nacs[:], acs, -1.0, None, ALU.mult).then_inc(nacs_ready.sem, 1)
                dve.wait_ge(acs_ready.sem, acs_ready.done(b, 0))
                dve.tensor_tensor(acs_lo[:], acsT, acs_hi[:].bitcast(F32), ALU.subtract).then_inc(acs_ready.sem, 1)
                dve.wait_ge(nacs_ready.sem, nacs_ready.done(b, 0))
                dve.tensor_tensor(exin[:, 0:NQ], tot, nacs[:], ALU.add)
                dve.tensor_copy(exin[:, NQ:2 * NQ], tot).then_inc(exin_ready.sem, 1)
                dve.wait_ge(exout_ready.sem, exout_ready.done(b, 1))
                dve.wait_ge(xw_ready.sem, xw_ready.done(b, -1))
                dve.tensor_tensor(wdec[:], dt[:], exout[:, 0:NQ], ALU.mult).then_inc(wdec_ready.sem, 1)

            def conv(b, g):
                for t in range(g * TPU, (g + 1) * TPU):
                    ps = bank[ring_index(t) % RING]
                    dve.wait_ge(taps_ready.sem, taps_ready.done(b, t))
                    u, v = slot(part, t), slot(tap0, t)
                    dve.scalar_tensor_tensor(u[:, 1:SEQ], ps[:, 0:SEQ - 1], cw[:, TAPS * t + 2:TAPS * t + 3],
                                             u[:, 1:SEQ], ALU.mult, ALU.add)
                    dve.scalar_tensor_tensor(v[:, 3:SEQ], ps[:, 0:SEQ - 3], cw[:, TAPS * t:TAPS * t + 1],
                                             v[:, 3:SEQ], ALU.mult, ALU.add).then_inc(uv_ready.sem, 1)

            def weigh(b, g):
                for hh in range(2):
                    hd = 2 * g + hh
                    dve.wait_ge(e_ready.sem, e_ready.done(b, hd))
                    dve.wait_ge(g_ps.sem, g_ps.done(b, hd))
                    dve.tensor_tensor(M[:, hd * SEQ:(hd + 1) * SEQ], bank[4 + hh][:],
                                      E[:, hd * SEQ:(hd + 1) * SEQ], ALU.mult).then_inc(m_ready.sem, 1)

            def carry(b, g):
                dve.wait_ge(st_ps.sem, st_ps.done(b, g))
                dve.wait_ge(yoff_ps.sem, yoff_ps.done(b, g - 1))
                dve.tensor_copy(prev[:, 0:P], bank[4][:, 0:P]).then_inc(prev_ready.sem, 1)
                for c in (1, 2):
                    dve.wait_ge(prev_ready.sem, prev_ready.done(b, 3 * g + c - 1))
                    for hh in range(2):
                        at = c * P + hh * HD
                        q = NQ + c * NH + 2 * g + hh
                        ins = dve.scalar_tensor_tensor(prev[:, at:at + HD], prev[:, at - P:at - P + HD],
                                                       exout[:, q:q + 1], bank[4][:, at:at + HD], ALU.mult, ALU.add)
                    ins.then_inc(prev_ready.sem, 1)

            def join(b, g):
                dve.wait_ge(yoff_ps.sem, yoff_ps.done(b, g))
                dve.tensor_tensor(by_head(toff[:, P:SEQ]), by_head(bank[5][:, P:SEQ]), per_head(eacs[:], g, 1),
                                  ALU.mult).then_inc(toff_ready.sem, 1)
                dve.wait_ge(toff_ready.sem, toff_ready.done(b, g))
                dve.wait_ge(ydiag_ps.sem, ydiag_ps.done(b, g))
                dve.wait_ge(yd_ready.sem, yd_ready.done(b, g - 1))
                dve.tensor_tensor(ysum[:], bank[7][:], toff[:], ALU.add).then_inc(ysum_ready.sem, 1)

            def mean_square(b, g):
                dve.wait_ge(sq_ready.sem, sq_ready.done(b, g))
                dve.wait_ge(mse_ready.sem, mse_ready.done(b, g - 1))
                dve.tensor_reduce(ms[:], sq[:].rearrange("p (n d) -> p n d", d=HD), AX_X, ALU.add).then_inc(ms_ready.sem, 1)

            def normed(b, g):
                dve.wait_ge(rms_ready.sem, rms_ready.done(b, g))
                y = yg[:, g * SEQ:(g + 1) * SEQ].rearrange("p (n d) -> p n d", d=HD)
                dve.tensor_tensor(y, y, rms[:].unsqueeze(2).broadcast_to([P, 8, HD]), ALU.mult).then_inc(yn_ready.sem, 1)

            with dve.Fori(0, BATCH) as b:
                dve.wait_ge(x_loaded.sem, x_loaded.done(b, 0))
                norm(b, 0, lambda c: xs[:, bass.ds((b % 2) * (NC * DM) + c * DM, DM)])
                split_h(b)
                raw_steps(b)
                conv(b, 0)
                steps(b)
                sums(b)
                for g in range(UNITS):
                    if g + 1 < UNITS:
                        conv(b, g + 1)
                    weigh(b, g)
                    carry(b, g)
                    if g > 0:
                        normed(b, g - 1)
                    join(b, g)
                    mean_square(b, g)
                normed(b, UNITS - 1)
                dve.wait_ge(fsum_step, RANK - 1)
                dve.wait_ge(stored.sem, stored.done(b, -1))
                ga = gab[:, bass.ds(b * (2 * DM), DM)].unsqueeze(1).broadcast_to([P, 2, DM])
                gb = gab[:, bass.ds(b * (2 * DM) + DM, DM)].unsqueeze(1).broadcast_to([P, 2, DM])
                for cp in range(2):
                    s = slice(cp * 512, (cp + 1) * 512)
                    dve.wait_ge(attn_ps.sem, attn_ps.done(b, cp))
                    dve.tensor_tensor(tmp[:, s].rearrange("p (c d) -> p c d", c=2),
                                      bank[(7, 4)[cp]][:].rearrange("p (c d) -> p c d", c=2), ga, ALU.mult).then_inc(gated.sem, 1)
                    dve.wait_ge(gated.sem, gated.done(b, cp))
                    dve.tensor_tensor(x2[:, s], tmp[:, s], xs[:, bass.ds((b % 2) * (NC * DM) + cp * 512, 512)], ALU.add).then_inc(x2_ready.sem, 1)
                dve.wait_ge(x2_ready.sem, x2_ready.done(b, 1))
                norm(b, 1, lambda c: x2[:, c * DM:(c + 1) * DM])
                for cp in range(2):
                    s = slice(cp * 512, (cp + 1) * 512)
                    dve.wait_ge(ffn_ps.sem, ffn_ps.done(b, cp))
                    dve.tensor_tensor(tmp[:, s].rearrange("p (c d) -> p c d", c=2),
                                      bank[(5, 4)[cp]][:].rearrange("p (c d) -> p c d", c=2), gb, ALU.mult).then_inc(ffn_gated.sem, 1)
                    dve.wait_ge(ffn_gated.sem, ffn_gated.done(b, cp))
                    dve.wait_ge(x2b_ready.sem, x2b_ready.done(b, 0))
                    dve.tensor_tensor(tmp[:, s], tmp[:, s], x2[:, s], ALU.add).then_inc(out_ready.sem, 1)

        @block.tensor
        def _(pe):
            for s in (hT_ps, dt_ps, acs_ps, seg_ps, wide_ps, xT_ps, g_ps, bT_ps, st_ps, ydiag_ps, yoff_ps,
                      yT_ps, attn_ps, ffn_ps):
                s.prime(pe)
            pe.wait_ge(c_silu, 1)
            pe.wait_ge(ld_mod, 16)
            blocks = [0, 1, 2, 3, 6, 7, 8, 9]
            for n, m in enumerate(blocks):
                for k in range(KD):
                    mm = pe.matmul(bank[0][:, n * BATCH:(n + 1) * BATCH],
                                   w_mod_sb[:, k * 6 * DM + m * P:k * 6 * DM + (m + 1) * P],
                                   ct[:, k * BATCH:(k + 1) * BATCH], start=(k == 0), stop=(k == KD - 1))
            mm.then_inc(mod_ps, 1)
            for n, m in enumerate((2, 5)):
                for k in range(KD):
                    at = k * 6 * DM + m * DM
                    mm = pe.matmul(bank[1][0:BATCH, n * DM:(n + 1) * DM], ct[:, k * BATCH:(k + 1) * BATCH],
                                   w_mod_sb[:, at:at + DM], start=(k == 0), stop=(k == KD - 1))
            mm.then_inc(mod_ps, 1)
            pe.wait_ge(consts, CONSTS)
            pe.wait_ge(mod_sb, 6)
            for i in range(BATCH):
                if i >= 2:
                    pe.wait_ge(gate_sb, i - 1)
                pe.matmul(bank[1 + i % 2][:], selb[:, i * P:(i + 1) * P], grow[:], start=True, stop=True).then_inc(gate_ps, 1)
            pe.wait_ge(gate_sb, BATCH)
            pe.wait_ge(ld_small, 16 * 8)
            pe.wait_ge(w_lo_done, 1)

            def turn_h(b, n):
                pe.wait_ge(xn_ready.sem, xn_ready.done(b, (n + 1) * NC - 1))
                for k in range(KD):
                    if n == 0:
                        pe.wait_ge(h_ready.sem, h_ready.done(b, k - KD))
                    elif k == 0:
                        pe.wait_ge(btok_ready.sem, btok_ready.done(b, 2 * UNITS - 1))
                    else:
                        pe.wait_ge(yT_ready.sem, yT_ready.done(b, UNITS - 1))
                    for c in range(NC):
                        mm = pe.transpose(chunk(bank[(3, 6)[k]], c), xn[:, c * DM + k * P:c * DM + (k + 1) * P], ident[:])
                    mm.then_inc(hT_ps.sem, 1)

            def ring_free(b, n):
                m = n - RING
                if TPU <= m < TPU + NC:
                    pe.wait_ge(z_ready.sem, z_ready.done(b, m - TPU))
                else:
                    t = m if m < TPU else m - NC
                    pe.wait_ge(uv_ready.sem, uv_ready.done(b, t))

            def project(b, g):
                for j in range(TPU):
                    n = ring_index(g * TPU + j)
                    ring_free(b, n)
                    ps = bank[n % RING][:]
                    i = 0
                    for w, hs in ((w_hi, (h_hi, h_lo)), (w_lo, (h_hi,))):
                        for k in range(KD):
                            for hx in hs:
                                mm = pe.matmul(ps, w_tile(w, g, k, j), hx[:, k * SEQ:(k + 1) * SEQ],
                                               start=(i == 0), stop=(i == 3 * KD - 1))
                                i += 1
                    mm.then_inc(wide_ps.sem, 1)

            def project_z(b):
                for c in range(NC):
                    n = TPU + c
                    ring_free(b, n)
                    i = 0
                    for hx, ws in ((h_hi, (w_hi, w_lo)), (h_lo, (w_hi,))):
                        for k in range(KD):
                            for w in ws:
                                mm = pe.matmul(bank[n % RING][:], hx[:, k * SEQ + c * P:k * SEQ + (c + 1) * P],
                                               w[:, WZ + k * DI:WZ + (k + 1) * DI], start=(i == 0), stop=(i == 3 * KD - 1))
                                i += 1
                    mm.then_inc(wide_ps.sem, 1)

            def project_dt(b):
                pe.wait_ge(h_ready.sem, h_ready.done(b, KD - 1))
                pe.wait_ge(gated.sem, gated.done(b, -2))
                for c in range(NC):
                    for k in range(KD):
                        mm = pe.matmul(bank[7][:, c * NH:(c + 1) * NH], h[:, k * SEQ + c * P:k * SEQ + (c + 1) * P],
                                       wdt[:, k * NH:(k + 1) * NH], start=(k == 0), stop=(k == KD - 1))
                mm.then_inc(dt_ps.sem, 1)

            def sum_a(b):
                pe.wait_ge(adt_ready.sem, adt_ready.done(b, 0))
                pe.matmul(bank[7][:, NQ:2 * NQ], tri[:], adt[:], start=True, stop=True)
                pe.matmul(bank[7][:, 2 * NQ:3 * NQ], ones[:], adt[:], start=True, stop=True)
                pe.matmul(bank[7][0:NQ, P:2 * P], adt[:], tri[:], start=True, stop=True).then_inc(acs_ps.sem, 1)

            def segments(b):
                pe.wait_ge(acs_ready.sem, acs_ready.done(b, 1))
                for hh in range(NH):
                    if hh >= 2:
                        pe.wait_ge(e_ready.sem, e_ready.done(b, hh - 2))
                    else:
                        pe.wait_ge(ffn_gated.sem, ffn_gated.done(b, -1))
                    ps = bank[4 + hh % 2]
                    pe.matmul(ps[:].rearrange("p (c l) -> p c l", c=NC), identr[:],
                              neg[:].unsqueeze(1).broadcast_to([P, NC, P]), start=True, stop=False, skip_group_check=True)
                    for c in range(NC):
                        q = c * NH + hh
                        for x, part_ in enumerate((acs_hi, acs_lo)):
                            mm = pe.matmul(chunk(ps, c), identr[0:NQ, q:q + 1].broadcast_to([NQ, P]), part_[:], start=False,
                                           stop=(c == NC - 1 and x == 1), skip_group_check=True)
                    mm.then_inc(seg_ps.sem, 1)

            def mix(b, g):
                xt, bt, ctl = xbc_tile(g, 0), (xbc_tile(g, 1), xbc_tile(g, 2)), (xbc_tile(g, 3), xbc_tile(g, 4))
                pe.wait_ge(xbc_ready.sem, xbc_ready.done(b, g * TPU + TPU - 1))
                if g == 0:
                    pe.wait_ge(h_ready.sem, h_ready.done(b, KD - 1))
                    pe.wait_ge(e_ready.sem, e_ready.done(b, NH - 1))
                else:
                    pe.wait_ge(btok_ready.sem, btok_ready.done(b, 2 * g - 1))
                    pe.wait_ge(prev_ready.sem, prev_ready.done(b, 3 * g - 1))
                    pe.wait_ge(toff_ready.sem, toff_ready.done(b, g - 1))
                for c in range(NC):
                    mm = pe.transpose(chunk(bank[3], c), chunk(xt, c), ident[:])
                mm.then_inc(xT_ps.sem, 1)
                for hh in range(2):
                    for c in range(NC):
                        mm = pe.matmul(chunk(bank[4 + hh], c), chunk(bt[hh], c), chunk(ctl[hh], c), start=True, stop=True)
                    mm.then_inc(g_ps.sem, 1)
                if g >= 2:
                    pe.wait_ge(yT_ready.sem, yT_ready.done(b, g - 2))
                for hh in range(2):
                    if hh:
                        pe.wait_ge(xtok_ready.sem, xtok_ready.done(b, g))
                    for c in range(NC):
                        mm = pe.transpose(chunk(bank[(6, 3)[hh]], c), chunk(bt[hh], c), ident[:])
                    mm.then_inc(bT_ps.sem, 1)
                pe.wait_ge(btok_ready.sem, btok_ready.done(b, 2 * g + 1))
                pe.wait_ge(xw_ready.sem, xw_ready.done(b, g))
                pe.wait_ge(m_ready.sem, m_ready.done(b, 2 * g))
                for hh in range(2):
                    for c in range(NC - 1):
                        at = c * P + hh * HD
                        mm = pe.matmul(bank[4][:, at:at + HD], btok[:, hh * SEQ + c * P:hh * SEQ + (c + 1) * P],
                                       xw[:, at:at + HD], start=True, stop=True)
                mm.then_inc(st_ps.sem, 1)
                pe.wait_ge(m_ready.sem, m_ready.done(b, 2 * g + 1))
                pe.wait_ge(xdt_ready.sem, xdt_ready.done(b, g))
                if g == 0:
                    pe.wait_ge(exin_ready.sem, exin_ready.done(b, 0))
                else:
                    pe.wait_ge(ysum_ready.sem, ysum_ready.done(b, g - 1))
                for hh in range(2):
                    for c in range(NC):
                        at = c * P + hh * HD
                        mm = pe.matmul(bank[7][:, at:at + HD], M[:, (2 * g + hh) * SEQ + c * P:(2 * g + hh) * SEQ + (c + 1) * P],
                                       xdt[:, at:at + HD], start=True, stop=True)
                mm.then_inc(ydiag_ps.sem, 1)

            def from_states(b, g):
                ctl = (xbc_tile(g, 3), xbc_tile(g, 4))
                pe.wait_ge(prev_ready.sem, prev_ready.done(b, 3 * g + 2))
                for hh in range(2):
                    for c in range(1, NC):
                        at = c * P + hh * HD
                        mm = pe.matmul(bank[5][:, at:at + HD], chunk(ctl[hh], c), prev[:, at - P:at - P + HD],
                                       start=True, stop=True)
                mm.then_inc(yoff_ps.sem, 1)

            def turn_y(b, g):
                pe.wait_ge(yn_ready.sem, yn_ready.done(b, g))
                if g + 1 < UNITS:
                    pe.wait_ge(btok_ready.sem, btok_ready.done(b, 2 * (g + 1)))
                else:
                    pe.wait_ge(yT_ready.sem, yT_ready.done(b, g - 1))
                for c in range(NC):
                    mm = pe.transpose(chunk(bank[6], c), yg[:, g * SEQ + c * P:g * SEQ + (c + 1) * P], ident[:])
                mm.then_inc(yT_ps.sem, 1)

            with pe.Fori(0, BATCH) as b:
                turn_h(b, 0)
                project_dt(b)
                pe.wait_ge(hlo_ready.sem, hlo_ready.done(b, KD - 1))
                project(b, 0)
                pe.wait_ge(w_lo_done, 5)
                project_z(b)
                sum_a(b)
                segments(b)
                for g in range(UNITS):
                    if g + 1 < UNITS:
                        project(b, g + 1)
                    mix(b, g)
                    if g > 0:
                        turn_y(b, g - 1)
                    from_states(b, g)
                turn_y(b, UNITS - 1)
                pe.wait_ge(wo_done, UNITS)
                pe.wait_ge(yT_ready.sem, yT_ready.done(b, UNITS - 1))
                pe.wait_ge(ysum_ready.sem, ysum_ready.done(b, UNITS - 1))
                for c in range(NC):
                    for g in range(UNITS):
                        mm = pe.matmul(bank[(7, 4)[c // 2]][:, (c % 2) * DM:(c % 2 + 1) * DM],
                                       yT[:, g * SEQ + c * P:g * SEQ + (c + 1) * P], wo[:, g * DM:(g + 1) * DM],
                                       start=(g == 0), stop=(g == UNITS - 1))
                    if c % 2:
                        mm.then_inc(attn_ps.sem, 1)
                turn_h(b, 1)
                pe.wait_ge(f_done, 1)
                pe.wait_ge(h_ready.sem, h_ready.done(b, 2 * KD - 1))
                pe.wait_ge(toff_ready.sem, toff_ready.done(b, UNITS - 1))
                pe.wait_ge(gated.sem, gated.done(b, 1))
                for c in range(NC):
                    for k in range(KD):
                        mm = pe.matmul(bank[(5, 4)[c // 2]][:, (c % 2) * DM:(c % 2 + 1) * DM],
                                       h[:, k * SEQ + c * P:k * SEQ + (c + 1) * P], fsum[:, k * DM:(k + 1) * DM],
                                       start=(k == 0), stop=(k == KD - 1))
                    if c % 2:
                        mm.then_inc(ffn_ps.sem, 1)



def kernel(**inputs):
    import numpy as np
    import concourse.bacc as bacc
    from concourse.bass_utils import run_bass_kernel_spmd

    a = {name: np.asarray(v) for name, v in inputs.items()}
    w_in_t = a["L0_attn_W_in"].T
    x0, b0, c0, dt0 = DI, 2 * DI, 2 * DI + NH * NS, 2 * DI + 2 * NH * NS

    def unit_columns(m, base):
        return [np.concatenate([m[..., base + g * P:base + (g + 1) * P],
                                m[..., base + b0 - x0 + g * 2 * P:base + b0 - x0 + (g + 1) * 2 * P],
                                m[..., base + c0 - x0 + g * 2 * P:base + c0 - x0 + (g + 1) * 2 * P]], axis=-1)
                for g in range(UNITS)]

    def rows(m):
        k = m.shape[0] // P
        return np.ascontiguousarray(m.reshape(k, P, -1).transpose(1, 0, 2).reshape(P, -1))

    conv_w = np.concatenate(unit_columns(a["L0_attn_conv_w"].T, 0), axis=-1)
    conv_b = np.concatenate(unit_columns(a["L0_attn_conv_b"][None], 0), axis=-1)
    arrays = {
        "x_in": np.ascontiguousarray(a["L0_attn_hidden_states"]),
        "w_xbc": np.stack([rows(m) for m in unit_columns(w_in_t, x0)]),
        "w_z": rows(w_in_t[:, 0:DI]),
        "w_dt": rows(w_in_t[:, dt0:dt0 + NH]),
        "conv_w": np.ascontiguousarray(conv_w.reshape(TAPS, TILES, P).transpose(2, 1, 0).reshape(P, -1)),
        "conv_b": np.ascontiguousarray(conv_b.reshape(TILES, P).T),
        "a_row": np.ascontiguousarray(np.broadcast_to(a["L0_attn_A"], (P, NH))),
        "d_row": np.ascontiguousarray(np.broadcast_to(a["L0_attn_D"], (P, NH))),
        "dtb_row": np.ascontiguousarray(np.broadcast_to(a["L0_attn_dt_bias"], (P, NH))),
        "norm_w": np.ascontiguousarray(a["L0_attn_norm_weight"].reshape(UNITS, P).T),
        "w_out": rows(a["L0_attn_W_out"].T),
        "factors": np.ascontiguousarray(a["L0_ffn_factors"].reshape(RANK, KD, P, DM).transpose(2, 0, 1, 3).reshape(P, -1)),
        "ffn_bias": np.ascontiguousarray(np.broadcast_to(a["L0_ffn_bias"], (P, DM))),
        "c_t": rows(a["L0_c"].T),
        "w_mod": rows(a["L0_wmod"]),
    }
    nc = bacc.Bacc("TRN2", target_bir_lowering=False, num_devices=1)
    args = [nc.dram_tensor(n, v.shape, mybir.dt.from_np(v.dtype), kind="ExternalInput").ap() for n, v in arrays.items()]
    out = nc.dram_tensor("out", (BATCH, SEQ, DM), F32, kind="ExternalOutput").ap()
    build(nc, *args, out)
    r = run_bass_kernel_spmd(nc, [arrays], core_ids=[0])
    return r.results[0]["out"]
```

```python
from contextlib import ExitStack

import concourse.bass as bass
from concourse import mybir

F32 = mybir.dt.float32
F32R = mybir.dt.float32r
ALU = mybir.AluOpType
ACT = mybir.ActivationFunctionType
AX_X = mybir.AxisListType.X

P = 128
BATCH, SEQ, DM = 4, 512, 256
DI, HD, NH = 512, 64, 8
NS = 128
TAPS = 4
NC = SEQ // P
KD = DM // P
UNITS = NH // 2
TPU = 5
TILES = UNITS * TPU
UW = TPU * P
RANK = 8
NQ = NC * NH
EPS = 1e-5
RING = 3
SLOTS = 4
WIDE = TILES + NC
CONSTS = 16
MASKED = -1e30


class Signal:

    BEFORE = 2

    def __init__(self, ctx, nc, name, per_batch, step=1):
        self.sem = ctx.enter_context(nc.semaphore(name))
        self.per_batch, self.step = per_batch, step

    def prime(self, eng):
        eng.sem_inc(self.sem, self.BEFORE * self.per_batch * self.step)

    def done(self, b, n):
        return b * (self.per_batch * self.step) + (self.BEFORE * self.per_batch + n + 1) * self.step


def ring_index(t):
    return t if t < TPU else t + NC


def build(nc, x_in, w_xbc, w_z, w_dt, conv_w, conv_b, a_row, d_row, dtb_row, norm_w, w_out,
          factors, ffn_bias, c_t, w_mod, out):
    ctx = ExitStack()
    with ctx:
        def sb(name, shape, dt=F32):
            return ctx.enter_context(nc.sbuf_tensor(name, shape, dt))

        def sem(name):
            return ctx.enter_context(nc.semaphore(name))

        def signal(name, per_batch, step=1):
            return Signal(ctx, nc, name, per_batch, step)

        bank = [ctx.enter_context(nc.psum_tensor(f"bank{i}", [P, 512], F32)) for i in range(8)]

        stage = sb("stage", [P, KD * (UNITS * UW + DI)])
        w_hi = sb("w_hi", [P, KD * (UNITS * UW + DI)], F32R)
        w_lo = sb("w_lo", [P, KD * (UNITS * UW + DI)], F32R)
        wdt = sb("wdt", [P, KD * NH])
        cw = sb("cw", [P, TILES * TAPS])
        cb = sb("cb", [P, TILES])
        arow = sb("arow", [P, NH])
        drow = sb("drow", [P, NH])
        dtb = sb("dtb", [P, NH])
        nw = sb("nw", [P, UNITS])
        wo = sb("wo", [P, UNITS * DM])
        fsum = sb("fsum", [P, KD * DM])
        fbias = sb("fbias", [P, DM])
        ct = sb("ct", [P, KD * BATCH])
        ident = sb("ident", [P, P])
        identr = sb("identr", [P, P], F32R)
        tri = sb("tri", [P, P])
        ones = sb("ones", [P, P])
        pairs = sb("pairs", [2 * NQ, NQ], F32R)
        neg = sb("neg", [P, P], F32R)
        selb = sb("selb", [BATCH, BATCH * P])
        eps = sb("eps", [P, 8])
        half = sb("half", [P, 8])
        mod_all = sb("mod_all", [P, BATCH * 8])
        modb = [sb(f"modb{n}", [P, 4]) for n in range(2)]
        grow = sb("grow", [BATCH, 2 * DM])
        gmag = sb("gmag", [BATCH, 2 * DM])
        gab = sb("gab", [P, BATCH * 2 * DM])

        xs = sb("xs", [P, 2 * NC * DM])
        stats = [sb(f"stats{n}", [P, NC * 6]) for n in range(2)]
        mv = [sb(f"mv{n}", [P, NC * 2]) for n in range(2)]
        veps = [sb(f"veps{n}", [P, NC]) for n in range(2)]
        rstd = [sb(f"rstd{n}", [P, NC]) for n in range(2)]
        xn = sb("xn", [P, NC * DM])
        h = sb("h", [P, KD * SEQ])
        h_hi = sb("h_hi", [P, KD * SEQ], F32R)
        h_lo = sb("h_lo", [P, KD * SEQ], F32R)
        dtu = sb("dtu", [P, NQ])
        dta = sb("dta", [P, NQ])
        dte = sb("dte", [P, NQ])
        dtl = sb("dtl", [P, NQ])
        dt = sb("dt", [P, NQ])
        adt = sb("adt", [P, 2 * NQ])
        nacs = sb("nacs", [P, NQ])
        exin = sb("exin", [P, 2 * NQ])
        exout = sb("exout", [P, 2 * NQ])
        eacs = sb("eacs", [P, NQ])
        wdec = sb("wdec", [P, NQ])
        acs = sb("acs", [2 * NQ, P], F32R)
        E = sb("E", [P, NH * NC * P])
        part = sb("part", [P, SLOTS * SEQ])
        tap0 = sb("tap0", [P, SLOTS * SEQ])
        xbc = sb("xbc", [P, 2 * TPU * SEQ])
        w_mod_sb = xbc
        zs = stage[:, 0:NC * DI]
        yg = stage[:, NC * DI:NC * DI + UNITS * SEQ]
        yT = stage[:, NC * DI + UNITS * SEQ:NC * DI + 2 * UNITS * SEQ]
        xtok = sb("xtok", [P, SEQ])
        xdt = sb("xdt", [P, SEQ])
        xw = sb("xw", [P, SEQ])
        xd = sb("xd", [P, SEQ])
        btok = sb("btok", [P, 2 * SEQ])
        M = E
        prev = sb("prev", [P, 3 * P])
        toff = sb("toff", [P, SEQ])
        ysum = sb("ysum", [P, SEQ])
        sq = sb("sq", [P, SEQ])
        ms = sb("ms", [P, 8])
        mse = sb("mse", [P, 8])
        rms = sb("rms", [P, 8])
        tail = sb("tail", [P, 2 * NC * DM])
        x2, tmp = tail[:, 0:NC * DM], tail[:, NC * DM:2 * NC * DM]
        fac = tail
        gbb = sb("gbb", [P, DM])

        ld_small, ld_mod, ld_z, ld_rest, ld_fac = (sem(n) for n in ("ld_small", "ld_mod", "ld_z", "ld_rest", "ld_fac"))
        ld_w = [sem(f"ld_w{g}") for g in range(UNITS)]
        consts = sem("consts")
        w_hi_done = sem("w_hi_done")
        w_lo_done = sem("w_lo_done")
        c_silu = sem("c_silu")
        mod_ps = sem("mod_ps")
        mod_sb = sem("mod_sb")
        gate_ps = sem("gate_ps")
        gate_sb = sem("gate_sb")
        wo_done = sem("wo_done")
        fsum_step = sem("fsum_step")
        f_done = sem("f_done")

        x_loaded = signal("x_loaded", 1, 16)
        stored = signal("stored", 1, 16)
        modb_ready = [signal(f"modb_ready{n}", 1) for n in range(2)]
        stats_done = [signal(f"stats_done{n}", NC) for n in range(2)]
        var_ready = [signal(f"var_ready{n}", NC) for n in range(2)]
        veps_ready = [signal(f"veps_ready{n}", 1) for n in range(2)]
        rstd_ready = [signal(f"rstd_ready{n}", 1) for n in range(2)]
        xn_ready = [signal(f"xn_ready{n}", NC) for n in range(2)]
        hT_ps = [signal(f"hT_ps{n}", KD) for n in range(2)]
        h_ready = [signal(f"h_ready{n}", KD) for n in range(2)]
        hhi_ready = signal("hhi_ready", KD)
        hlo_ready = signal("hlo_ready", KD)
        dt_ps = signal("dt_ps", 1)
        dt_step = signal("dt_step", 3)
        sp_step = signal("sp_step", 2)
        adt_ready = signal("adt_ready", 2)
        acs_ps = signal("acs_ps", 1)
        nacs_ready = signal("nacs_ready", 1)
        exin_ready = signal("exin_ready", 1)
        acs_ready = signal("acs_ready", 2)
        exout_ready = signal("exout_ready", 2)
        wdec_ready = signal("wdec_ready", 1)
        seg_ps = signal("seg_ps", NH)
        e_ready = signal("e_ready", NH)
        wide_ps = signal("wide_ps", WIDE)
        taps_ready = signal("taps_ready", TILES)
        uv_ready = signal("uv_ready", TILES)
        s_ready = signal("s_ready", TILES)
        xbc_ready = signal("xbc_ready", TILES)
        z_ready = signal("z_ready", NC)
        xT_ps = signal("xT_ps", UNITS)
        xtok_ready = signal("xtok_ready", UNITS)
        xdt_ready = signal("xdt_ready", UNITS)
        xw_ready = signal("xw_ready", UNITS)
        xd_ready = signal("xd_ready", UNITS)
        g_ps = signal("g_ps", 2 * UNITS)
        m_ready = signal("m_ready", 2 * UNITS)
        bT_ps = signal("bT_ps", 2 * UNITS)
        btok_ready = signal("btok_ready", 2 * UNITS)
        st_ps = signal("st_ps", UNITS)
        prev_ready = signal("prev_ready", 3 * UNITS)
        ydiag_ps = signal("ydiag_ps", UNITS)
        yoff_ps = signal("yoff_ps", UNITS)
        toff_ready = signal("toff_ready", UNITS)
        ysum_ready = signal("ysum_ready", UNITS)
        yd_ready = signal("yd_ready", UNITS)
        yg_ready = signal("yg_ready", UNITS)
        sq_ready = signal("sq_ready", UNITS)
        ms_ready = signal("ms_ready", UNITS)
        mse_ready = signal("mse_ready", UNITS)
        rms_ready = signal("rms_ready", UNITS)
        yn_ready = signal("yn_ready", UNITS)
        yT_ps = signal("yT_ps", UNITS)
        yT_ready = signal("yT_ready", UNITS)
        attn_ps = signal("attn_ps", 2)
        gated = signal("gated", 2)
        x2_ready = signal("x2_ready", 2)
        gbb_ready = signal("gbb_ready", 1)
        x2b_ready = signal("x2b_ready", 1)
        ffn_ps = signal("ffn_ps", 2)
        ffn_gated = signal("ffn_gated", 2)
        out_ready = signal("out_ready", 2)

        WZ = UNITS * KD * UW

        def w_tile(w, g, k, j):
            at = g * KD * UW + k * UW + j * P
            return w[:, at:at + P]

        def xbc_tile(g, j):
            at = ((g % 2) * TPU + j) * SEQ
            return xbc[:, at:at + SEQ]

        def slot(buf, t):
            at = (t % SLOTS) * SEQ
            return buf[:, at:at + SEQ]

        def chunk(ap, c):
            return ap[:, c * P:(c + 1) * P]

        def per_head(tile, g, c0=0):
            v = tile.rearrange("p (c h) -> p c h", c=NC)[:, c0:NC, 2 * g:2 * g + 2]
            return v.unsqueeze(3).broadcast_to([P, NC - c0, 2, HD])

        def by_head(ap, c0=0):
            return ap.rearrange("p (c h d) -> p c h d", h=2, d=HD)

        block = ctx.enter_context(nc.Block())

        @block.sync
        def _(sp):
            x_loaded.prime(sp)
            stored.prime(sp)
            x_rows = x_in.rearrange("b (c p) d -> p b c d", p=P)
            out_rows = out.rearrange("b (c p) d -> p b c d", p=P)

            def load_x(b):
                dst = xs[:, bass.ds((b % 2) * (NC * DM), NC * DM)].rearrange("p (o c d) -> p o c d", o=1, c=NC)
                sp.dma_start(dst, x_rows[:, bass.ds(b, 1)]).then_inc(x_loaded.sem, 16)

            load_x(0)
            sp.dma_start(ct[:], c_t).then_inc(ld_small, 16)
            sp.dma_start(w_mod_sb[:, 0:KD * 6 * DM], w_mod).then_inc(ld_mod, 16)
            for dst, src in ((wdt, w_dt), (cw, conv_w), (cb, conv_b), (arow, a_row), (drow, d_row), (dtb, dtb_row), (nw, norm_w)):
                sp.dma_start(dst[:], src).then_inc(ld_small, 16)
            for g in range(UNITS):
                sp.dma_start(stage[:, g * KD * UW:(g + 1) * KD * UW], w_xbc[g]).then_inc(ld_w[g], 16)
                if g == 0:
                    sp.dma_start(stage[:, WZ:WZ + KD * DI], w_z).then_inc(ld_z, 16)
            sp.dma_start(wo[:], w_out).then_inc(ld_rest, 16)
            sp.dma_start(fbias[:], ffn_bias).then_inc(ld_rest, 16)
            half_rank = RANK // 2 * KD * DM
            sp.dma_start(fac[:], factors[:, 0:half_rank]).then_inc(ld_fac, 16)
            sp.wait_ge(x_loaded.sem, x_loaded.done(0, 0))
            load_x(1)
            sp.wait_ge(fsum_step, RANK // 2 - 1)
            sp.dma_start(fac[:], factors[:, half_rank:2 * half_rank]).then_inc(ld_fac, 16)

            def store(b):
                sp.wait_ge(out_ready.sem, out_ready.done(b, 1))
                src = tmp.rearrange("p (o c d) -> p o c d", o=1, c=NC)
                sp.dma_start(out_rows[:, bass.ds(b, 1)], src).then_inc(stored.sem, 16)

            with sp.Fori(0, BATCH - 2) as b:
                store(b)
                sp.wait_ge(x_loaded.sem, x_loaded.done(b, 1))
                sp.wait_ge(x2_ready.sem, x2_ready.done(b, 1))
                load_x(b + 2)
            with sp.Fori(BATCH - 2, BATCH) as b:
                store(b)
            sp.wait_ge(stored.sem, stored.done(BATCH - 1, 0))

        @block.gpsimd
        def _(pool):
            for s in (*veps_ready, *rstd_ready, s_ready, xdt_ready, xw_ready, xd_ready, yg_ready,
                      mse_ready, rms_ready, x2b_ready, gbb_ready):
                s.prime(pool)
            made = [0]

            def make(ins):
                ins.then_inc(consts, 1)
                made[0] += 1

            make(pool.memset(ident[:], 0.0))
            make(pool.memset(selb[:], 0.0))
            make(pool.memset(ones[:], 1.0))
            make(pool.memset(tap0[:], 0.0))
            make(pool.memset(toff[:], 0.0))
            make(pool.memset(half[:], -0.5))
            make(pool.memset(eps[:], EPS))
            make(pool.memset(neg[:].bitcast(F32), 0.0))
            make(pool.memset(pairs[:].bitcast(F32), 0.0))
            pool.wait_ge(consts, made[0])
            make(pool.affine_select(out=ident[:], in_=ident[:], compare_op=ALU.not_equal, fill=1.0,
                                    base=0, pattern=[[-1, P]], channel_multiplier=1))
            sb3 = selb[:].rearrange("p (b m) -> p b m", b=BATCH)
            make(pool.affine_select(out=sb3, in_=sb3, compare_op=ALU.not_equal, fill=1.0,
                                    base=0, pattern=[[-1, BATCH], [0, P]], channel_multiplier=1))
            make(pool.affine_select(out=tri[:], in_=ones[:], compare_op=ALU.is_ge, fill=0.0,
                                    base=0, pattern=[[1, P]], channel_multiplier=-1))
            make(pool.affine_select(out=neg[:], in_=neg[:].bitcast(F32), compare_op=ALU.is_ge, fill=MASKED,
                                    base=0, pattern=[[1, P]], channel_multiplier=-1))
            make(pool.affine_select(out=pairs[:], in_=pairs[:].bitcast(F32), compare_op=ALU.not_equal, fill=1.0,
                                    base=0, pattern=[[-1, NQ]], channel_multiplier=1))
            pool.wait_ge(consts, made[0])
            make(pool.affine_select(out=pairs[:], in_=pairs[:].bitcast(F32), compare_op=ALU.not_equal, fill=1.0,
                                    base=-NQ, pattern=[[-1, NQ]], channel_multiplier=1))
            make(pool.affine_select(out=identr[:], in_=ident[:], compare_op=ALU.is_ge, fill=0.0,
                                    base=0, pattern=[[0, P]], channel_multiplier=0))
            assert made[0] == CONSTS

            def rstd_of(b, n):
                pool.wait_ge(var_ready[n].sem, var_ready[n].done(b, NC - 1))
                var = mv[n][:].rearrange("p (c s) -> p c s", s=2)[:, :, 1]
                pool.tensor_tensor(veps[n][:], var, eps[:, 0:NC], ALU.add).then_inc(veps_ready[n].sem, 1)
                pool.wait_ge(veps_ready[n].sem, veps_ready[n].done(b, 0))
                pool.tensor_tensor(rstd[n][:], veps[n][:], half[:, 0:NC], ALU.pow).then_inc(rstd_ready[n].sem, 1)

            def add_taps(b, t):
                pool.wait_ge(uv_ready.sem, uv_ready.done(b, t))
                pool.tensor_tensor(slot(part, t), slot(part, t), slot(tap0, t), ALU.add).then_inc(s_ready.sem, 1)

            def scale_x(b, g):
                pool.wait_ge(xtok_ready.sem, xtok_ready.done(b, g))
                pool.wait_ge(wdec_ready.sem, wdec_ready.done(b, 0))
                pool.wait_ge(st_ps.sem, st_ps.done(b, g - 1))
                pool.tensor_tensor(by_head(xw[:]), by_head(xtok[:]), per_head(wdec[:], g), ALU.mult).then_inc(xw_ready.sem, 1)
                pool.wait_ge(ydiag_ps.sem, ydiag_ps.done(b, g - 1))
                pool.tensor_tensor(by_head(xdt[:]), by_head(xtok[:]), per_head(dt[:], g), ALU.mult).then_inc(xdt_ready.sem, 1)

            def skip_x(b, g):
                pool.wait_ge(yd_ready.sem, yd_ready.done(b, g - 1))
                dd = drow[:, 2 * g:2 * g + 2].unsqueeze(1).unsqueeze(3).broadcast_to([P, NC, 2, HD])
                pool.tensor_tensor(by_head(xd[:]), by_head(xtok[:]), dd, ALU.mult).then_inc(xd_ready.sem, 1)

            def gate_y(b, g):
                pool.wait_ge(z_ready.sem, z_ready.done(b, NC - 1))
                pool.wait_ge(yT_ps.sem, yT_ps.done(b, g - UNITS))
                pool.wait_ge(yd_ready.sem, yd_ready.done(b, g))
                z = zs.rearrange("p (c i) -> p c i", c=NC)[:, :, g * P:(g + 1) * P]
                dst = yg[:, g * SEQ:(g + 1) * SEQ].rearrange("p (c i) -> p c i", c=NC)
                pool.tensor_tensor(dst, ysum[:].rearrange("p (c i) -> p c i", c=NC), z, ALU.mult).then_inc(yg_ready.sem, 1)

            def rms_of(b, g):
                pool.wait_ge(ms_ready.sem, ms_ready.done(b, g))
                pool.tensor_tensor(mse[:], ms[:], eps[:], ALU.add).then_inc(mse_ready.sem, 1)
                pool.wait_ge(mse_ready.sem, mse_ready.done(b, g))
                pool.wait_ge(yn_ready.sem, yn_ready.done(b, g - 1))
                pool.tensor_tensor(rms[:], mse[:], half[:], ALU.pow).then_inc(rms_ready.sem, 1)

            def ffn_bias_of(b):
                gb = gab[:, bass.ds(b * (2 * DM) + DM, DM)]
                pool.wait_ge(x2b_ready.sem, x2b_ready.done(b, -1))
                pool.tensor_tensor(gbb[:], gb, fbias[:], ALU.mult).then_inc(gbb_ready.sem, 1)

            def add_bias(b):
                pool.wait_ge(gbb_ready.sem, gbb_ready.done(b, 0))
                pool.wait_ge(xn_ready[1].sem, xn_ready[1].done(b, NC - 1))
                x2v = x2.rearrange("p (c d) -> p c d", c=NC)
                bias = gbb[:].unsqueeze(1).broadcast_to([P, NC, DM])
                pool.tensor_tensor(x2v, x2v, bias, ALU.add).then_inc(x2b_ready.sem, 1)

            def unit(b, g, nxt, old=None):
                tiles = [(nxt[0], nxt[1] * TPU + j) for j in range(TPU)] if nxt else [None] * TPU

                def taps(j):
                    if tiles[j]:
                        add_taps(*tiles[j])

                if g > 0:
                    gate_y(b, g - 1)
                taps(0)
                scale_x(b, g)
                taps(1)
                if g > 0:
                    rms_of(b, g - 1)
                if old is not None:
                    ffn_bias_of(old)
                    rstd_of(old, 1)
                taps(2)
                skip_x(b, g)
                if g == UNITS - 2 and nxt and next_batch[0] is not None:
                    rstd_of(next_batch[0], 0)
                taps(3)
                if old is not None:
                    add_bias(old)
                taps(4)

            next_batch = [None]

            FW = KD * DM
            for r in range(1, RANK):
                pool.wait_ge(ld_fac, 16 if r < RANK // 2 else 32)
                at = (r % (RANK // 2)) * FW
                first = fac[:, 0:FW] if r == 1 else fsum[:]
                pool.tensor_tensor(fsum[:], first, fac[:, at:at + FW], ALU.add).then_inc(fsum_step, 1)
                pool.wait_ge(fsum_step, r)
            pool.wait_ge(ld_small, 16 * 8)

            pool.wait_ge(gate_sb, BATCH)
            pool.wait_ge(ld_rest, 32)
            rstd_of(0, 0)
            for t in range(TPU):
                add_taps(0, t)
            unit(0, 0, (0, 1))

            def rest(b, nb):
                next_batch[0] = nb
                for g in range(1, UNITS):
                    nxt = (b, g + 1) if g + 1 < UNITS else (nb, 0) if nb is not None else None
                    unit(b, g, nxt)
                gate_y(b, UNITS - 1)
                rms_of(b, UNITS - 1)

            with pool.Fori(0, BATCH - 1) as b:
                rest(b, b + 1)
                unit(b + 1, 0, (b + 1, 1), b)
            rest(BATCH - 1, None)
            ffn_bias_of(BATCH - 1)
            rstd_of(BATCH - 1, 1)
            add_bias(BATCH - 1)

        @block.scalar
        def _(act):
            for s in (*h_ready, sp_step, exout_ready, e_ready, taps_ready, xbc_ready, z_ready, xtok_ready,
                      btok_ready, sq_ready, yT_ready):
                s.prime(act)
            act.wait_ge(ld_small, 16 * 8)
            act.activation(ct[:], ct[:], ACT.Silu).then_inc(c_silu, 1)
            for n in range(5):
                g = (0, None, 1, 2, 3)[n]
                act.wait_ge(ld_z if g is None else ld_w[g], 16)
                lo, size = (WZ, KD * DI) if g is None else (g * KD * UW, KD * UW)
                act.activation(w_hi[:, lo:lo + size], stage[:, lo:lo + size], ACT.Copy).then_inc(w_hi_done, 1)
            for i in range(BATCH):
                act.wait_ge(gate_ps, i + 1)
                act.activation(gab[:, i * 2 * DM:(i + 1) * 2 * DM], bank[1 + i % 2][:], ACT.Copy).then_inc(gate_sb, 1)

            def evac_h(b, n):
                act.wait_ge(modb_ready[n].sem, modb_ready[n].done(b, 0))
                for k in range(KD):
                    act.wait_ge(hT_ps[n].sem, hT_ps[n].done(b, k))
                    act.activation(h[:, k * SEQ:(k + 1) * SEQ], bank[(3, 6)[k]][:], ACT.Identity,
                                   bias=modb[n][:, k:k + 1], scale=modb[n][:, 2 + k:3 + k]).then_inc(h_ready[n].sem, 1)

            def taps(b, t):
                n = ring_index(t)
                ps = bank[n % RING]
                act.wait_ge(wide_ps.sem, wide_ps.done(b, n))
                act.wait_ge(s_ready.sem, s_ready.done(b, t - SLOTS))
                act.wait_ge(xbc_ready.sem, xbc_ready.done(b, t - SLOTS))
                act.activation(slot(part, t), ps[:], ACT.Identity, bias=cb[:, t:t + 1],
                               scale=cw[:, TAPS * t + 3:TAPS * t + 4])
                act.activation(slot(tap0, t)[:, 2:SEQ], ps[:, 0:SEQ - 2], ACT.Copy,
                               scale=cw[:, TAPS * t + 1:TAPS * t + 2]).then_inc(taps_ready.sem, 1)

            def silu(b, t):
                g, j = divmod(t, TPU)
                act.wait_ge(s_ready.sem, s_ready.done(b, t))
                act.wait_ge(yoff_ps.sem, yoff_ps.done(b, g - 2))
                act.activation(xbc_tile(g, j), slot(part, t), ACT.Silu).then_inc(xbc_ready.sem, 1)

            def silu_z(b):
                act.wait_ge(yg_ready.sem, yg_ready.done(b, -1))
                for c in range(NC):
                    n = TPU + c
                    act.wait_ge(wide_ps.sem, wide_ps.done(b, n))
                    act.activation(zs[:, c * DI:(c + 1) * DI], bank[n % RING][:], ACT.Silu).then_inc(z_ready.sem, 1)

            def steps(b):
                act.preload_act_table_set("natural_log_exp_and_others")
                act.wait_ge(dt_step.sem, dt_step.done(b, 1))
                act.activation(dte[:], dta[:], ACT.Exp, scale=-1.0).then_inc(sp_step.sem, 1)
                act.wait_ge(sp_step.sem, sp_step.done(b, 0))
                act.activation(dtl[:], dte[:], ACT.Ln, bias=1.0).then_inc(sp_step.sem, 1)
                act.wait_ge(exin_ready.sem, exin_ready.done(b, 0))
                act.wait_ge(prev_ready.sem, prev_ready.done(b, -1))
                act.activation(exout[:], exin[:], ACT.Exp).then_inc(exout_ready.sem, 1)
                act.wait_ge(toff_ready.sem, toff_ready.done(b, -1))
                act.activation(eacs[:], nacs[:], ACT.Exp, scale=-1.0).then_inc(exout_ready.sem, 1)
                act.wait_ge(ydiag_ps.sem, ydiag_ps.done(b, -1))

            def decays(b, heads):
                for hh in heads:
                    act.wait_ge(seg_ps.sem, seg_ps.done(b, hh))
                    for c in range(NC):
                        q = c * NH + hh
                        ins = act.activation(E[:, (hh * NC + c) * P:(hh * NC + c + 1) * P],
                                             chunk(bank[4 + hh % 2], c), ACT.Exp, bias=nacs[:, q:q + 1])
                    ins.then_inc(e_ready.sem, 1)

            def evac_x(b, g):
                act.wait_ge(xT_ps.sem, xT_ps.done(b, g))
                act.wait_ge(xd_ready.sem, xd_ready.done(b, g - 1))
                act.activation(xtok[:], bank[3][:], ACT.Copy).then_inc(xtok_ready.sem, 1)

            def evac_b(b, g, hh):
                act.wait_ge(bT_ps.sem, bT_ps.done(b, 2 * g + hh))
                act.wait_ge(st_ps.sem, st_ps.done(b, g - 1))
                act.activation(btok[:, hh * SEQ:(hh + 1) * SEQ], bank[(6, 3)[hh]][:], ACT.Copy).then_inc(btok_ready.sem, 1)

            def square(b, g):
                act.wait_ge(ms_ready.sem, ms_ready.done(b, g - 1))
                act.wait_ge(yg_ready.sem, yg_ready.done(b, g))
                act.activation(sq[:], yg[:, g * SEQ:(g + 1) * SEQ], ACT.Square, scale=HD ** -0.5).then_inc(sq_ready.sem, 1)

            def evac_y(b, g):
                act.wait_ge(attn_ps.sem, attn_ps.done(b, -1))
                act.wait_ge(yT_ps.sem, yT_ps.done(b, g))
                act.activation(yT[:, g * SEQ:(g + 1) * SEQ], bank[6][:], ACT.Copy).then_inc(yT_ready.sem, 1)

            def unit(b, g, nxt, old=None):
                tiles = [(nxt[0], nxt[1] * TPU + j) for j in range(TPU)] if nxt else []

                def conv(j):
                    if tiles:
                        taps(*tiles[j])
                        if j:
                            silu(*tiles[j - 1])

                turn = g == UNITS - 1
                if turn:
                    silu(b, g * TPU + TPU - 1)
                    if nxt:
                        evac_h(nxt[0], 0)
                else:
                    conv(0)
                    if g:
                        silu(b, g * TPU + TPU - 1)
                evac_x(b, g)
                evac_b(b, g, 0)
                if turn:
                    conv(0)
                else:
                    conv(1)
                evac_b(b, g, 1)
                if turn:
                    conv(1)
                if g > 0:
                    square(b, g - 1)
                conv(2)
                conv(3)
                conv(4)
                if g > 0:
                    evac_y(b, g - 1)
                if old is not None:
                    evac_h(old, 1)

            def turn_to(b, old=None):
                if b is not None:
                    silu(b, TPU - 1)
                if old is not None:
                    square(old, UNITS - 1)
                if b is not None:
                    silu_z(b)
                    steps(b)
                    decays(b, range(0, NH // 2))
                if old is not None:
                    evac_y(old, UNITS - 1)
                if b is not None:
                    decays(b, range(NH // 2, NH))

            act.wait_ge(ld_rest, 32)
            for g in range(UNITS):
                act.activation(wo[:, g * DM:(g + 1) * DM], wo[:, g * DM:(g + 1) * DM], ACT.Copy,
                               scale=nw[:, g:g + 1]).then_inc(wo_done, 1)
            act.wait_ge(fsum_step, RANK - 1)
            act.activation(fsum[:], fsum[:], ACT.Copy, scale=float(RANK) ** -0.5).then_inc(f_done, 1)
            act.wait_ge(consts, CONSTS)

            evac_h(0, 0)
            for t in range(TPU):
                taps(0, t)
                if t:
                    silu(0, t - 1)
            turn_to(0)
            unit(0, 0, (0, 1))

            def rest(b, nb):
                for g in range(1, UNITS):
                    nxt = (b, g + 1) if g + 1 < UNITS else (nb, 0) if nb is not None else None
                    unit(b, g, nxt)
                turn_to(nb, b)

            with act.Fori(0, BATCH - 1) as b:
                rest(b, b + 1)
                unit(b + 1, 0, (b + 1, 1), b)
            rest(BATCH - 1, None)
            evac_h(BATCH - 1, 1)

        @block.vector
        def _(dve):
            for s in (*modb_ready, *stats_done, *var_ready, *xn_ready, yd_ready, hhi_ready, hlo_ready, dt_step, adt_ready,
                      nacs_ready, exin_ready, acs_ready, wdec_ready, uv_ready, m_ready, prev_ready, toff_ready,
                      ysum_ready, ms_ready, yn_ready, gated, x2_ready, ffn_gated, out_ready):
                s.prime(dve)

            dve.wait_ge(mod_ps, 1)
            dst = mod_all[:].rearrange("p (b n) -> p b n", b=BATCH)
            src = bank[0][:, 0:8 * BATCH].rearrange("p (n b) -> p b n", b=BATCH)
            for n0 in (0, 4):
                dve.tensor_copy(dst[:, :, n0:n0 + 2], src[:, :, n0:n0 + 2])
                dve.tensor_scalar(dst[:, :, n0 + 2:n0 + 4], src[:, :, n0 + 2:n0 + 4], 1.0, None, ALU.add).then_inc(mod_sb, 1)
            dve.wait_ge(mod_ps, 2)
            gps = bank[1][0:BATCH, :]
            dve.tensor_scalar(gmag[:], gps, -1.0, 0.25, ALU.mult, ALU.max).then_inc(mod_sb, 1)
            dve.wait_ge(mod_sb, 3)
            dve.scalar_tensor_tensor(gmag[:], gps, 1.0, gmag[:], ALU.mult, ALU.max).then_inc(mod_sb, 1)
            dve.tensor_scalar(grow[:], gps, 0.0, 2.0, ALU.is_ge, ALU.mult).then_inc(mod_sb, 1)
            dve.wait_ge(mod_sb, 5)
            dve.scalar_tensor_tensor(grow[:], grow[:], 1.0, gmag[:], ALU.subtract, ALU.mult).then_inc(mod_sb, 1)
            for n in range(5):
                g = (0, None, 1, 2, 3)[n]
                lo, size = (WZ, KD * DI) if g is None else (g * KD * UW, KD * UW)
                dve.wait_ge(w_hi_done, n + 1)
                dve.tensor_tensor(w_lo[:, lo:lo + size], stage[:, lo:lo + size],
                                  w_hi[:, lo:lo + size].bitcast(F32), ALU.subtract).then_inc(w_lo_done, 1)
            dve.wait_ge(mod_sb, 6)
            dve.wait_ge(ld_small, 16 * 8)
            dve.wait_ge(consts, CONSTS)
            dve.wait_ge(gate_sb, BATCH)

            def x_of(b, lo, size):
                return xs[:, bass.ds((b % 2) * (NC * DM) + lo, size)]

            def chunk_in(b, n, c):
                return x_of(b, c * DM, DM) if n == 0 else x2[:, c * DM:(c + 1) * DM]

            def norm_stats(b, n, chunks):
                for c in chunks:
                    dve.bn_stats(stats[n][:, 6 * c:6 * c + 6], chunk_in(b, n, c)).then_inc(stats_done[n].sem, 1)

            def norm_vars(b, n):
                dve.wait_ge(h_ready[n].sem, h_ready[n].done(b, -1))
                dve.wait_ge(rstd_ready[n].sem, rstd_ready[n].done(b, -1))
                dve.wait_ge(stats_done[n].sem, stats_done[n].done(b, NC - 1))
                dve.tensor_copy(modb[n][:], mod_all[:, bass.ds(b * 8 + 4 * n, 4)]).then_inc(modb_ready[n].sem, 1)
                for c in range(NC):
                    dve.bn_aggr(mv[n][:, 2 * c:2 * c + 2], stats[n][:, 6 * c:6 * c + 6]).then_inc(var_ready[n].sem, 1)

            def norm_rows(b, n):
                dve.wait_ge(rstd_ready[n].sem, rstd_ready[n].done(b, 0))
                for c in range(NC):
                    dve.tensor_scalar(xn[:, c * DM:(c + 1) * DM], chunk_in(b, n, c), mv[n][:, 2 * c:2 * c + 1],
                                      rstd[n][:, c:c + 1], ALU.subtract, ALU.mult).then_inc(xn_ready[n].sem, 1)

            def split_h(b):
                dve.wait_ge(wide_ps.sem, wide_ps.done(b, -1))
                for k in range(KD):
                    s = slice(k * SEQ, (k + 1) * SEQ)
                    dve.wait_ge(h_ready[0].sem, h_ready[0].done(b, k))
                    dve.tensor_copy(h_hi[:, s], h[:, s]).then_inc(hhi_ready.sem, 1)
                    dve.wait_ge(hhi_ready.sem, hhi_ready.done(b, k))
                    dve.tensor_tensor(h_lo[:, s], h[:, s], h_hi[:, s].bitcast(F32), ALU.subtract).then_inc(hlo_ready.sem, 1)

            def rows(ap):
                return ap.rearrange("p (c h) -> p c h", c=NC)

            def row(ap):
                return ap.unsqueeze(1).broadcast_to([P, NC, NH])

            def raw_steps(b):
                dve.wait_ge(dt_ps.sem, dt_ps.done(b, 0))
                dve.tensor_tensor(rows(dtu[:]), rows(bank[7][:, 0:NQ]), row(dtb[:]), ALU.add).then_inc(dt_step.sem, 1)
                dve.wait_ge(dt_step.sem, dt_step.done(b, 0))
                dve.scalar_tensor_tensor(dta[:], dtu[:], -1.0, dtu[:], ALU.mult, ALU.max).then_inc(dt_step.sem, 1)

            def steps(b):
                dve.wait_ge(sp_step.sem, sp_step.done(b, 1))
                dve.wait_ge(xdt_ready.sem, xdt_ready.done(b, -1))
                dve.scalar_tensor_tensor(dt[:], dtu[:], 0.0, dtl[:], ALU.max, ALU.add).then_inc(dt_step.sem, 1)
                dve.wait_ge(dt_step.sem, dt_step.done(b, 2))
                for half_ in (adt[:, 0:NQ], adt[:, NQ:2 * NQ]):
                    dve.tensor_tensor(rows(half_), rows(dt[:]), row(arow[:]), ALU.mult).then_inc(adt_ready.sem, 1)

            def sums(b):
                acs_ps_, tot, acsT = bank[7][:, NQ:2 * NQ], bank[7][:, 2 * NQ:3 * NQ], bank[7][0:2 * NQ, P:2 * P]
                dve.wait_ge(acs_ps.sem, acs_ps.done(b, 0))
                dve.wait_ge(seg_ps.sem, seg_ps.done(b, -1))
                dve.tensor_copy(acs[:], acsT).then_inc(acs_ready.sem, 1)
                dve.wait_ge(e_ready.sem, e_ready.done(b, -1))
                dve.tensor_scalar(nacs[:], acs_ps_, -1.0, None, ALU.mult).then_inc(nacs_ready.sem, 1)
                dve.wait_ge(acs_ready.sem, acs_ready.done(b, 0))
                low = slice(NQ, 2 * NQ)
                dve.tensor_tensor(acs[low, :], acsT[low, :], acs[low, :].bitcast(F32), ALU.subtract).then_inc(acs_ready.sem, 1)
                dve.wait_ge(nacs_ready.sem, nacs_ready.done(b, 0))
                dve.tensor_tensor(exin[:, 0:NQ], tot, nacs[:], ALU.add)
                dve.tensor_copy(exin[:, NQ:2 * NQ], tot).then_inc(exin_ready.sem, 1)
                dve.wait_ge(exout_ready.sem, exout_ready.done(b, 1))
                dve.wait_ge(xw_ready.sem, xw_ready.done(b, -1))
                dve.tensor_tensor(wdec[:], dt[:], exout[:, 0:NQ], ALU.mult).then_inc(wdec_ready.sem, 1)

            def conv(b, t):
                ps = bank[ring_index(t) % RING]
                dve.wait_ge(taps_ready.sem, taps_ready.done(b, t))
                u, v = slot(part, t), slot(tap0, t)
                if True:
                    dve.scalar_tensor_tensor(u[:, 1:SEQ], ps[:, 0:SEQ - 1], cw[:, TAPS * t + 2:TAPS * t + 3],
                                             u[:, 1:SEQ], ALU.mult, ALU.add)
                    dve.scalar_tensor_tensor(v[:, 3:SEQ], ps[:, 0:SEQ - 3], cw[:, TAPS * t:TAPS * t + 1],
                                             v[:, 3:SEQ], ALU.mult, ALU.add).then_inc(uv_ready.sem, 1)

            def weigh(b, g):
                for hh in range(2):
                    hd = 2 * g + hh
                    dve.wait_ge(e_ready.sem, e_ready.done(b, hd))
                    dve.wait_ge(g_ps.sem, g_ps.done(b, hd))
                    dve.tensor_tensor(M[:, hd * SEQ:(hd + 1) * SEQ], bank[4 + hh][:],
                                      E[:, hd * SEQ:(hd + 1) * SEQ], ALU.mult).then_inc(m_ready.sem, 1)

            def carry(b, g):
                dve.wait_ge(st_ps.sem, st_ps.done(b, g))
                dve.wait_ge(yoff_ps.sem, yoff_ps.done(b, g - 1))
                dve.tensor_copy(prev[:, 0:P], bank[4][:, 0:P]).then_inc(prev_ready.sem, 1)
                for c in (1, 2):
                    dve.wait_ge(prev_ready.sem, prev_ready.done(b, 3 * g + c - 1))
                    for hh in range(2):
                        at = c * P + hh * HD
                        q = NQ + c * NH + 2 * g + hh
                        ins = dve.scalar_tensor_tensor(prev[:, at:at + HD], prev[:, at - P:at - P + HD],
                                                       exout[:, q:q + 1], bank[4][:, at:at + HD], ALU.mult, ALU.add)
                    ins.then_inc(prev_ready.sem, 1)

            def join(b, g):
                dve.wait_ge(yoff_ps.sem, yoff_ps.done(b, g))
                dve.tensor_tensor(by_head(toff[:, P:SEQ]), by_head(bank[5][:, P:SEQ]), per_head(eacs[:], g, 1),
                                  ALU.mult).then_inc(toff_ready.sem, 1)
                dve.wait_ge(toff_ready.sem, toff_ready.done(b, g))
                dve.wait_ge(ydiag_ps.sem, ydiag_ps.done(b, g))
                dve.wait_ge(yg_ready.sem, yg_ready.done(b, g - 1))
                dve.tensor_tensor(ysum[:], bank[7][:], toff[:], ALU.add).then_inc(ysum_ready.sem, 1)
                dve.wait_ge(xd_ready.sem, xd_ready.done(b, g))
                dve.wait_ge(ysum_ready.sem, ysum_ready.done(b, g))
                dve.tensor_tensor(ysum[:], ysum[:], xd[:], ALU.add).then_inc(yd_ready.sem, 1)

            def mean_square(b, g):
                dve.wait_ge(sq_ready.sem, sq_ready.done(b, g))
                dve.wait_ge(mse_ready.sem, mse_ready.done(b, g - 1))
                dve.tensor_reduce(ms[:], sq[:].rearrange("p (n d) -> p n d", d=HD), AX_X, ALU.add).then_inc(ms_ready.sem, 1)

            def normed(b, g):
                dve.wait_ge(rms_ready.sem, rms_ready.done(b, g))
                y = yg[:, g * SEQ:(g + 1) * SEQ].rearrange("p (n d) -> p n d", d=HD)
                dve.tensor_tensor(y, y, rms[:].unsqueeze(2).broadcast_to([P, 8, HD]), ALU.mult).then_inc(yn_ready.sem, 1)

            def residual(b, cp):
                ga = gab[:, bass.ds(b * (2 * DM), DM)].unsqueeze(1).broadcast_to([P, 2, DM])
                s = slice(cp * 512, (cp + 1) * 512)
                if cp == 0:
                    dve.wait_ge(fsum_step, RANK - 1)
                    dve.wait_ge(stored.sem, stored.done(b, -1))
                dve.wait_ge(attn_ps.sem, attn_ps.done(b, cp))
                dve.tensor_tensor(tmp[:, s].rearrange("p (c d) -> p c d", c=2),
                                  bank[(3, 7)[cp]][:].rearrange("p (c d) -> p c d", c=2), ga, ALU.mult).then_inc(gated.sem, 1)
                dve.wait_ge(gated.sem, gated.done(b, cp))
                dve.tensor_tensor(x2[:, s], tmp[:, s], x_of(b, cp * 512, 512), ALU.add).then_inc(x2_ready.sem, 1)

            def finish(b, cp):
                gb = gab[:, bass.ds(b * (2 * DM) + DM, DM)].unsqueeze(1).broadcast_to([P, 2, DM])
                s = slice(cp * 512, (cp + 1) * 512)
                dve.wait_ge(ffn_ps.sem, ffn_ps.done(b, cp))
                dve.tensor_tensor(tmp[:, s].rearrange("p (c d) -> p c d", c=2),
                                  bank[(3, 6)[cp]][:].rearrange("p (c d) -> p c d", c=2), gb, ALU.mult).then_inc(ffn_gated.sem, 1)
                dve.wait_ge(ffn_gated.sem, ffn_gated.done(b, cp))
                dve.wait_ge(x2b_ready.sem, x2b_ready.done(b, 0))
                dve.tensor_tensor(tmp[:, s], tmp[:, s], x2[:, s], ALU.add).then_inc(out_ready.sem, 1)

            def residual_norm(b, cp):
                residual(b, cp)
                dve.wait_ge(x2_ready.sem, x2_ready.done(b, cp))
                norm_stats(b, 1, (2 * cp, 2 * cp + 1))

            def unit(b, g, nxt, old=None, next_batch=None):
                tiles = [(nxt[0], nxt[1] * TPU + j) for j in range(TPU)] if nxt else []

                def taps(j):
                    if tiles:
                        conv(*tiles[j])

                if g > 0:
                    join(b, g - 1)
                if g == UNITS - 1:
                    weigh(b, g)
                    if nxt:
                        split_h(nxt[0])
                        raw_steps(nxt[0])
                taps(0)
                if old is not None:
                    residual_norm(old, 0)
                taps(1)
                if old is not None:
                    residual_norm(old, 1)
                    norm_vars(old, 1)
                if g > 0:
                    mean_square(b, g - 1)
                if g < UNITS - 1:
                    weigh(b, g)
                if next_batch is not None and g == UNITS - 2:
                    dve.wait_ge(x_loaded.sem, x_loaded.done(next_batch, 0))
                    norm_stats(next_batch, 0, range(NC))
                    norm_vars(next_batch, 0)
                taps(2)
                carry(b, g)
                taps(3)
                if g > 0:
                    normed(b, g - 1)
                if next_batch is not None and g == UNITS - 2:
                    dve.wait_ge(hT_ps[1].sem, hT_ps[1].done(next_batch - 1, -1))
                    norm_rows(next_batch, 0)
                if old is not None:
                    dve.wait_ge(hT_ps[0].sem, hT_ps[0].done(b, KD - 1))
                    norm_rows(old, 1)
                taps(4)
                if old is not None:
                    finish(old, 0)
                    finish(old, 1)

            def turn_to(b, old=None):
                if old is not None:
                    join(old, UNITS - 1)
                    mean_square(old, UNITS - 1)
                if b is not None:
                    steps(b)
                if old is not None:
                    normed(old, UNITS - 1)
                if b is not None:
                    sums(b)

            dve.wait_ge(x_loaded.sem, x_loaded.done(0, 0))
            norm_stats(0, 0, range(NC))
            norm_vars(0, 0)
            norm_rows(0, 0)
            split_h(0)
            raw_steps(0)
            for t in range(TPU):
                conv(0, t)
            turn_to(0)
            unit(0, 0, (0, 1))

            def rest(b, nb):
                for g in range(1, UNITS):
                    nxt = (b, g + 1) if g + 1 < UNITS else (nb, 0) if nb is not None else None
                    unit(b, g, nxt, next_batch=nb)
                turn_to(nb, b)

            with dve.Fori(0, BATCH - 1) as b:
                rest(b, b + 1)
                unit(b + 1, 0, (b + 1, 1), b)
            last = BATCH - 1
            rest(last, None)
            residual_norm(last, 0)
            residual_norm(last, 1)
            norm_vars(last, 1)
            norm_rows(last, 1)
            finish(last, 0)
            finish(last, 1)

        @block.tensor
        def _(pe):
            for s in (*hT_ps, dt_ps, acs_ps, seg_ps, wide_ps, xT_ps, g_ps, bT_ps, st_ps, ydiag_ps, yoff_ps,
                      yT_ps, attn_ps, ffn_ps):
                s.prime(pe)
            pe.wait_ge(c_silu, 1)
            pe.wait_ge(ld_mod, 16)
            blocks = [0, 1, 2, 3, 6, 7, 8, 9]
            for n, m in enumerate(blocks):
                for k in range(KD):
                    mm = pe.matmul(bank[0][:, n * BATCH:(n + 1) * BATCH],
                                   w_mod_sb[:, k * 6 * DM + m * P:k * 6 * DM + (m + 1) * P],
                                   ct[:, k * BATCH:(k + 1) * BATCH], start=(k == 0), stop=(k == KD - 1))
            mm.then_inc(mod_ps, 1)
            for n, m in enumerate((2, 5)):
                for k in range(KD):
                    at = k * 6 * DM + m * DM
                    mm = pe.matmul(bank[1][0:BATCH, n * DM:(n + 1) * DM], ct[:, k * BATCH:(k + 1) * BATCH],
                                   w_mod_sb[:, at:at + DM], start=(k == 0), stop=(k == KD - 1))
            mm.then_inc(mod_ps, 1)
            pe.wait_ge(consts, CONSTS)
            pe.wait_ge(mod_sb, 6)
            for i in range(BATCH):
                if i >= 2:
                    pe.wait_ge(gate_sb, i - 1)
                pe.matmul(bank[1 + i % 2][:], selb[:, i * P:(i + 1) * P], grow[:], start=True, stop=True).then_inc(gate_ps, 1)
            pe.wait_ge(gate_sb, BATCH)
            pe.wait_ge(ld_small, 16 * 8)
            pe.wait_ge(w_lo_done, 1)

            def turn_h(b, n, beside=None):
                pe.wait_ge(xn_ready[n].sem, xn_ready[n].done(b, NC - 1))
                for k in range(KD):
                    if n == 0:
                        (pe.wait_ge(btok_ready.sem, btok_ready.done(b - 1, 5)) if k == 0
                         else pe.wait_ge(yT_ready.sem, yT_ready.done(b - 1, 1)))
                    elif beside is not None:
                        pe.wait_ge(btok_ready.sem, btok_ready.done(beside, 1 - k))
                    else:
                        (pe.wait_ge(gated.sem, gated.done(b, 0)) if k == 0
                         else pe.wait_ge(yT_ready.sem, yT_ready.done(b, UNITS - 1)))
                    for c in range(NC):
                        mm = pe.transpose(chunk(bank[(3, 6)[k]], c), xn[:, c * DM + k * P:c * DM + (k + 1) * P], ident[:])
                    mm.then_inc(hT_ps[n].sem, 1)

            def ring_free(b, n):
                m = n - RING
                if TPU <= m < TPU + NC:
                    pe.wait_ge(z_ready.sem, z_ready.done(b, m - TPU))
                else:
                    t = m if m < TPU else m - NC
                    pe.wait_ge(uv_ready.sem, uv_ready.done(b, t))

            def project(b, t):
                g, j = divmod(t, TPU)
                if True:
                    n = ring_index(t)
                    ring_free(b, n)
                    ps = bank[n % RING][:]
                    i = 0
                    for w, hs in ((w_hi, (h_hi, h_lo)), (w_lo, (h_hi,))):
                        for k in range(KD):
                            for hx in hs:
                                mm = pe.matmul(ps, w_tile(w, g, k, j), hx[:, k * SEQ:(k + 1) * SEQ],
                                               start=(i == 0), stop=(i == 3 * KD - 1))
                                i += 1
                    mm.then_inc(wide_ps.sem, 1)

            def project_z(b):
                for c in range(NC):
                    n = TPU + c
                    ring_free(b, n)
                    i = 0
                    for hx, ws in ((h_hi, (w_hi, w_lo)), (h_lo, (w_hi,))):
                        for k in range(KD):
                            for w in ws:
                                mm = pe.matmul(bank[n % RING][:], hx[:, k * SEQ + c * P:k * SEQ + (c + 1) * P],
                                               w[:, WZ + k * DI:WZ + (k + 1) * DI], start=(i == 0), stop=(i == 3 * KD - 1))
                                i += 1
                    mm.then_inc(wide_ps.sem, 1)

            def project_dt(b):
                pe.wait_ge(h_ready[0].sem, h_ready[0].done(b, KD - 1))
                pe.wait_ge(ysum_ready.sem, ysum_ready.done(b, -2))
                for c in range(NC):
                    for k in range(KD):
                        mm = pe.matmul(bank[7][:, c * NH:(c + 1) * NH], h[:, k * SEQ + c * P:k * SEQ + (c + 1) * P],
                                       wdt[:, k * NH:(k + 1) * NH], start=(k == 0), stop=(k == KD - 1))
                mm.then_inc(dt_ps.sem, 1)

            def sum_a(b):
                pe.wait_ge(ysum_ready.sem, ysum_ready.done(b, -1))
                pe.wait_ge(adt_ready.sem, adt_ready.done(b, 1))
                pe.matmul(bank[7][0:2 * NQ, P:2 * P], adt[:], tri[:], start=True, stop=True)
                pe.matmul(bank[7][:, NQ:2 * NQ], tri[:], adt[:, 0:NQ], start=True, stop=True)
                pe.matmul(bank[7][:, 2 * NQ:3 * NQ], ones[:], adt[:, 0:NQ], start=True, stop=True).then_inc(acs_ps.sem, 1)

            def segments(b, heads):
                pe.wait_ge(acs_ready.sem, acs_ready.done(b, 1))
                for hh in heads:
                    if hh >= 2:
                        pe.wait_ge(e_ready.sem, e_ready.done(b, hh - 2))
                    elif hh == 0:
                        pe.wait_ge(prev_ready.sem, prev_ready.done(b, -1))
                        pe.wait_ge(toff_ready.sem, toff_ready.done(b, -1))
                    ps = bank[4 + hh % 2]
                    pe.matmul(ps[:].rearrange("p (c l) -> p c l", c=NC), identr[:],
                              neg[:].unsqueeze(1).broadcast_to([P, NC, P]), start=True, stop=False, skip_group_check=True)
                    for c in range(NC):
                        q = c * NH + hh
                        mm = pe.matmul(chunk(ps, c), pairs[:, q:q + 1].broadcast_to([2 * NQ, P]), acs[:],
                                       start=False, stop=(c == NC - 1), skip_group_check=True)
                    mm.then_inc(seg_ps.sem, 1)

            def turn_x(b, g, next_batch):
                xt = xbc_tile(g, 0)
                pe.wait_ge(xbc_ready.sem, xbc_ready.done(b, g * TPU))
                if g == 0:
                    pe.wait_ge(h_ready[0].sem, h_ready[0].done(b, 0))
                    pe.wait_ge(gated.sem, gated.done(b - 1, 0))
                elif g == 1:
                    pe.wait_ge(btok_ready.sem, btok_ready.done(b, 1))
                    pe.wait_ge(ffn_gated.sem, ffn_gated.done(b - 1, 0))
                elif g == UNITS - 1 and next_batch is not None:
                    pe.wait_ge(h_ready[0].sem, h_ready[0].done(next_batch, 0))
                else:
                    pe.wait_ge(btok_ready.sem, btok_ready.done(b, 2 * g - 1))
                for c in range(NC):
                    mm = pe.transpose(chunk(bank[3], c), chunk(xt, c), ident[:])
                mm.then_inc(xT_ps.sem, 1)

            def turn_b(b, g, hh, next_batch):
                bt = xbc_tile(g, 1 + hh)
                pe.wait_ge(xbc_ready.sem, xbc_ready.done(b, g * TPU + 1 + hh))
                if hh:
                    pe.wait_ge(xtok_ready.sem, xtok_ready.done(b, g))
                elif g == 0:
                    pe.wait_ge(h_ready[0].sem, h_ready[0].done(b, 1))
                    pe.wait_ge(yT_ready.sem, yT_ready.done(b, -1))
                elif g == 1:
                    pe.wait_ge(btok_ready.sem, btok_ready.done(b, 0))
                    pe.wait_ge(ffn_gated.sem, ffn_gated.done(b - 1, 1))
                elif g == UNITS - 1 and next_batch is not None:
                    pe.wait_ge(h_ready[0].sem, h_ready[0].done(next_batch, 1))
                else:
                    pe.wait_ge(yT_ready.sem, yT_ready.done(b, g - 2))
                for c in range(NC):
                    mm = pe.transpose(chunk(bank[(6, 3)[hh]], c), chunk(bt, c), ident[:])
                mm.then_inc(bT_ps.sem, 1)

            def pair_tokens(b, g, hh):
                bt, ctl = xbc_tile(g, 1 + hh), xbc_tile(g, 3 + hh)
                pe.wait_ge(xbc_ready.sem, xbc_ready.done(b, g * TPU + 3 + hh))
                if g == 0:
                    pe.wait_ge(e_ready.sem, e_ready.done(b, NH - 1))
                elif hh == 0:
                    pe.wait_ge(prev_ready.sem, prev_ready.done(b, 3 * g - 1))
                else:
                    pe.wait_ge(toff_ready.sem, toff_ready.done(b, g - 1))
                for c in range(NC):
                    mm = pe.matmul(chunk(bank[4 + hh], c), chunk(bt, c), chunk(ctl, c), start=True, stop=True)
                mm.then_inc(g_ps.sem, 1)

            def states(b, g):
                pe.wait_ge(btok_ready.sem, btok_ready.done(b, 2 * g + 1))
                pe.wait_ge(xw_ready.sem, xw_ready.done(b, g))
                pe.wait_ge(m_ready.sem, m_ready.done(b, 2 * g))
                for hh in range(2):
                    for c in range(NC - 1):
                        at = c * P + hh * HD
                        mm = pe.matmul(bank[4][:, at:at + HD], btok[:, hh * SEQ + c * P:hh * SEQ + (c + 1) * P],
                                       xw[:, at:at + HD], start=True, stop=True)
                mm.then_inc(st_ps.sem, 1)

            def within_chunks(b, g, next_batch):
                pe.wait_ge(m_ready.sem, m_ready.done(b, 2 * g + 1))
                pe.wait_ge(xdt_ready.sem, xdt_ready.done(b, g))
                if g == 0:
                    pe.wait_ge(exin_ready.sem, exin_ready.done(b, 0))
                    pe.wait_ge(gated.sem, gated.done(b - 1, 1))
                elif g == UNITS - 1 and next_batch is not None:
                    pe.wait_ge(dt_step.sem, dt_step.done(next_batch, 0))
                else:
                    pe.wait_ge(ysum_ready.sem, ysum_ready.done(b, g - 1))
                for hh in range(2):
                    for c in range(NC):
                        at = c * P + hh * HD
                        mm = pe.matmul(bank[7][:, at:at + HD], M[:, (2 * g + hh) * SEQ + c * P:(2 * g + hh) * SEQ + (c + 1) * P],
                                       xdt[:, at:at + HD], start=True, stop=True)
                mm.then_inc(ydiag_ps.sem, 1)

            def from_states(b, g):
                ctl = (xbc_tile(g, 3), xbc_tile(g, 4))
                pe.wait_ge(m_ready.sem, m_ready.done(b, 2 * g + 1))
                pe.wait_ge(prev_ready.sem, prev_ready.done(b, 3 * g + 2))
                for hh in range(2):
                    for c in range(1, NC):
                        at = c * P + hh * HD
                        mm = pe.matmul(bank[5][:, at:at + HD], chunk(ctl[hh], c), prev[:, at - P:at - P + HD],
                                       start=True, stop=True)
                mm.then_inc(yoff_ps.sem, 1)

            def turn_y(b, g):
                if g + 1 < UNITS:
                    pe.wait_ge(btok_ready.sem, btok_ready.done(b, 2 * (g + 1)))
                else:
                    pe.wait_ge(yT_ready.sem, yT_ready.done(b, g - 1))
                pe.wait_ge(yn_ready.sem, yn_ready.done(b, g))
                for c in range(NC):
                    mm = pe.transpose(chunk(bank[6], c), yg[:, g * SEQ + c * P:g * SEQ + (c + 1) * P], ident[:])
                mm.then_inc(yT_ps.sem, 1)

            def project_out(b, next_batch):
                pe.wait_ge(yT_ready.sem, yT_ready.done(b, UNITS - 1))
                for c in range(NC):
                    if c == 0:
                        pe.wait_ge(btok_ready.sem, btok_ready.done(b, 2 * UNITS - 1))
                    elif c == 2 and next_batch is not None:
                        pe.wait_ge(exin_ready.sem, exin_ready.done(next_batch, 0))
                    elif c == 2:
                        pe.wait_ge(ysum_ready.sem, ysum_ready.done(b, UNITS - 1))
                    for g in range(UNITS):
                        mm = pe.matmul(bank[(3, 7)[c // 2]][:, (c % 2) * DM:(c % 2 + 1) * DM],
                                       yT[:, g * SEQ + c * P:g * SEQ + (c + 1) * P], wo[:, g * DM:(g + 1) * DM],
                                       start=(g == 0), stop=(g == UNITS - 1))
                    if c % 2:
                        mm.then_inc(attn_ps.sem, 1)

            def feed_forward(b):
                pe.wait_ge(h_ready[1].sem, h_ready[1].done(b, KD - 1))
                for c in range(NC):
                    for k in range(KD):
                        mm = pe.matmul(bank[(3, 6)[c // 2]][:, (c % 2) * DM:(c % 2 + 1) * DM],
                                       h[:, k * SEQ + c * P:k * SEQ + (c + 1) * P], fsum[:, k * DM:(k + 1) * DM],
                                       start=(k == 0), stop=(k == KD - 1))
                    if c % 2:
                        mm.then_inc(ffn_ps.sem, 1)

            def unit(b, g, nxt, old=None, next_batch=None):
                tiles = [(nxt[0], nxt[1] * TPU + j) for j in range(TPU)] if nxt else []

                def proj(j):
                    if tiles:
                        project(*tiles[j])

                if g == UNITS - 1:
                    if nxt:
                        turn_h(nxt[0], 0)
                    pair_tokens(b, g, 0)
                    pair_tokens(b, g, 1)
                    turn_x(b, g, next_batch)
                    turn_b(b, g, 0, next_batch)
                    if nxt:
                        project_dt(nxt[0])
                        pe.wait_ge(hlo_ready.sem, hlo_ready.done(nxt[0], KD - 1))
                    proj(0)
                    turn_b(b, g, 1, next_batch)
                    proj(1)
                else:
                    proj(0)
                    turn_x(b, g, next_batch)
                    turn_b(b, g, 0, next_batch)
                    proj(1)
                    turn_b(b, g, 1, next_batch)
                    pair_tokens(b, g, 0)
                    pair_tokens(b, g, 1)
                proj(2)
                states(b, g)
                proj(3)
                within_chunks(b, g, next_batch)
                proj(4)
                if g > 0:
                    turn_y(b, g - 1)
                from_states(b, g)
                if old is not None:
                    turn_h(old, 1, b)
                    feed_forward(old)

            def turn_to(b, old=None):
                if b is not None:
                    project_z(b)
                    sum_a(b)
                    segments(b, range(0, NH // 2))
                if old is not None:
                    turn_y(old, UNITS - 1)
                if b is not None:
                    segments(b, range(NH // 2, NH))
                if old is not None:
                    project_out(old, b)

            turn_h(0, 0)
            project_dt(0)
            pe.wait_ge(hlo_ready.sem, hlo_ready.done(0, KD - 1))
            for t in range(TPU):
                project(0, t)
            pe.wait_ge(w_lo_done, 5)
            turn_to(0)
            unit(0, 0, (0, 1))
            pe.wait_ge(wo_done, UNITS)
            pe.wait_ge(f_done, 1)

            def rest(b, nb):
                for g in range(1, UNITS):
                    nxt = (b, g + 1) if g + 1 < UNITS else (nb, 0) if nb is not None else None
                    unit(b, g, nxt, next_batch=nb)
                turn_to(nb, b)

            with pe.Fori(0, BATCH - 1) as b:
                rest(b, b + 1)
                unit(b + 1, 0, (b + 1, 1), b)
            rest(BATCH - 1, None)
            turn_h(BATCH - 1, 1)
            feed_forward(BATCH - 1)


def kernel(**inputs):
    import numpy as np
    import concourse.bacc as bacc
    from concourse.bass_utils import run_bass_kernel_spmd

    a = {name: np.asarray(v) for name, v in inputs.items()}
    w_in_t = a["L0_attn_W_in"].T
    x0, b0, c0, dt0 = DI, 2 * DI, 2 * DI + NH * NS, 2 * DI + 2 * NH * NS

    def unit_columns(m, base):
        return [np.concatenate([m[..., base + g * P:base + (g + 1) * P],
                                m[..., base + b0 - x0 + g * 2 * P:base + b0 - x0 + (g + 1) * 2 * P],
                                m[..., base + c0 - x0 + g * 2 * P:base + c0 - x0 + (g + 1) * 2 * P]], axis=-1)
                for g in range(UNITS)]

    def rows(m):
        k = m.shape[0] // P
        return np.ascontiguousarray(m.reshape(k, P, -1).transpose(1, 0, 2).reshape(P, -1))

    conv_w = np.concatenate(unit_columns(a["L0_attn_conv_w"].T, 0), axis=-1)
    conv_b = np.concatenate(unit_columns(a["L0_attn_conv_b"][None], 0), axis=-1)
    arrays = {
        "x_in": np.ascontiguousarray(a["L0_attn_hidden_states"]),
        "w_xbc": np.stack([rows(m) for m in unit_columns(w_in_t, x0)]),
        "w_z": rows(w_in_t[:, 0:DI]),
        "w_dt": rows(w_in_t[:, dt0:dt0 + NH]),
        "conv_w": np.ascontiguousarray(conv_w.reshape(TAPS, TILES, P).transpose(2, 1, 0).reshape(P, -1)),
        "conv_b": np.ascontiguousarray(conv_b.reshape(TILES, P).T),
        "a_row": np.ascontiguousarray(np.broadcast_to(a["L0_attn_A"], (P, NH))),
        "d_row": np.ascontiguousarray(np.broadcast_to(a["L0_attn_D"], (P, NH))),
        "dtb_row": np.ascontiguousarray(np.broadcast_to(a["L0_attn_dt_bias"], (P, NH))),
        "norm_w": np.ascontiguousarray(a["L0_attn_norm_weight"].reshape(UNITS, P).T),
        "w_out": rows(a["L0_attn_W_out"].T),
        "factors": np.ascontiguousarray(a["L0_ffn_factors"].reshape(RANK, KD, P, DM).transpose(2, 0, 1, 3).reshape(P, -1)),
        "ffn_bias": np.ascontiguousarray(np.broadcast_to(a["L0_ffn_bias"], (P, DM))),
        "c_t": rows(a["L0_c"].T),
        "w_mod": rows(a["L0_wmod"]),
    }
    nc = bacc.Bacc("TRN2", target_bir_lowering=False, num_devices=1)
    args = [nc.dram_tensor(n, v.shape, mybir.dt.from_np(v.dtype), kind="ExternalInput").ap() for n, v in arrays.items()]
    out = nc.dram_tensor("out", (BATCH, SEQ, DM), F32, kind="ExternalOutput").ap()
    build(nc, *args, out)
    r = run_bass_kernel_spmd(nc, [arrays], core_ids=[0])
    return r.results[0]["out"]
```

```python
from contextlib import ExitStack

import concourse.bass as bass
from concourse import mybir

F32 = mybir.dt.float32
F32R = mybir.dt.float32r
ALU = mybir.AluOpType
ACT = mybir.ActivationFunctionType
AX_X = mybir.AxisListType.X

P = 128
BATCH, SEQ, DM = 4, 512, 256
DI, HD, NH = 512, 64, 8
NS = 128
TAPS = 4
NC = SEQ // P
KD = DM // P
UNITS = NH // 2
TPU = 5
TILES = UNITS * TPU
UW = TPU * P
RANK = 8
NQ = NC * NH
EPS = 1e-5
RING = 3
SLOTS = 4
WIDE = TILES + NC
SMALL = 6
CONSTS = 16
MASKED = -1e30


class Signal:

    BEFORE = 2

    def __init__(self, ctx, nc, name, per_batch, step=1):
        self.sem = ctx.enter_context(nc.semaphore(name))
        self.per_batch, self.step = per_batch, step

    def prime(self, eng):
        eng.sem_inc(self.sem, self.BEFORE * self.per_batch * self.step)

    def done(self, b, n):
        return b * (self.per_batch * self.step) + (self.BEFORE * self.per_batch + n + 1) * self.step


def ring_index(t):
    return t if t < TPU else t + NC


def build(nc, x_in, w_xbc, w_z, w_dt, conv_w, conv_b, a_row, d_row, dtb_row, norm_w, w_out,
          factors, ffn_bias, c_t, w_mod, out):
    ctx = ExitStack()
    with ctx:
        def sb(name, shape, dt=F32):
            return ctx.enter_context(nc.sbuf_tensor(name, shape, dt))

        def sem(name):
            return ctx.enter_context(nc.semaphore(name))

        def signal(name, per_batch, step=1):
            return Signal(ctx, nc, name, per_batch, step)

        bank = [ctx.enter_context(nc.psum_tensor(f"bank{i}", [P, 512], F32)) for i in range(8)]

        stage = sb("stage", [P, KD * (UNITS * UW + DI)])
        w_hi = sb("w_hi", [P, KD * (UNITS * UW + DI)], F32R)
        w_lo = sb("w_lo", [P, KD * (UNITS * UW + DI)], F32R)
        wdt = sb("wdt", [P, KD * NH])
        cw = sb("cw", [P, TILES * TAPS])
        cb = sb("cb", [P, TILES])
        arow = sb("arow", [P, NH])
        drow = sb("drow", [P, NH])
        dtb = sb("dtb", [P, NH])
        nw = sb("nw", [P, UNITS])
        wo = sb("wo", [P, UNITS * DM])
        fsum = sb("fsum", [P, KD * DM])
        fbias = sb("fbias", [P, DM])
        ct = sb("ct", [P, KD * BATCH])
        ident = sb("ident", [P, P])
        identr = sb("identr", [P, P], F32R)
        tri = sb("tri", [P, P])
        ones = sb("ones", [P, P])
        pairs = sb("pairs", [2 * NQ, NQ], F32R)
        neg = sb("neg", [P, P], F32R)
        selb = sb("selb", [BATCH, BATCH * P])
        eps = sb("eps", [P, 8])
        half = sb("half", [P, 8])
        mod_all = sb("mod_all", [P, BATCH * 8])
        modb = [sb(f"modb{n}", [P, 4]) for n in range(2)]
        grow = sb("grow", [BATCH, 2 * DM])
        gmag = sb("gmag", [BATCH, 2 * DM])
        gab = sb("gab", [P, BATCH * 2 * DM])

        xs = sb("xs", [P, 2 * NC * DM])
        stats = [sb(f"stats{n}", [P, NC * 6]) for n in range(2)]
        mv = [sb(f"mv{n}", [P, NC * 2]) for n in range(2)]
        veps = [sb(f"veps{n}", [P, NC]) for n in range(2)]
        rstd = [sb(f"rstd{n}", [P, NC]) for n in range(2)]
        xn = sb("xn", [P, NC * DM])
        h = sb("h", [P, KD * SEQ])
        h_hi = sb("h_hi", [P, KD * SEQ], F32R)
        h_lo = sb("h_lo", [P, KD * SEQ], F32R)
        dtu = sb("dtu", [P, NQ])
        dta = sb("dta", [P, NQ])
        dte = sb("dte", [P, NQ])
        dtl = sb("dtl", [P, NQ])
        dt = sb("dt", [P, NQ])
        adt = sb("adt", [P, 2 * NQ])
        nacs = sb("nacs", [P, NQ])
        exin = sb("exin", [P, 2 * NQ])
        exout = sb("exout", [P, 2 * NQ])
        eacs = sb("eacs", [P, NQ])
        wdec = sb("wdec", [P, NQ])
        acs = sb("acs", [2 * NQ, P], F32R)
        E = sb("E", [P, NH * NC * P])
        part = sb("part", [P, SLOTS * SEQ])
        tap0 = sb("tap0", [P, SLOTS * SEQ])
        xbc = sb("xbc", [P, 2 * TPU * SEQ])
        w_mod_sb = E
        zs = stage[:, 0:NC * DI]
        yg = stage[:, NC * DI:NC * DI + UNITS * SEQ]
        yT = stage[:, NC * DI + UNITS * SEQ:NC * DI + 2 * UNITS * SEQ]
        xtok = sb("xtok", [P, SEQ])
        xdt = sb("xdt", [P, SEQ])
        xw = sb("xw", [P, SEQ])
        xd = sb("xd", [P, SEQ])
        btok = sb("btok", [P, 2 * SEQ])
        M = E
        prev = sb("prev", [P, 3 * P])
        toff = sb("toff", [P, SEQ])
        ysum = sb("ysum", [P, SEQ])
        sq = sb("sq", [P, SEQ])
        ms = sb("ms", [P, 8])
        mse = sb("mse", [P, 8])
        rms = sb("rms", [P, 8])
        tail = sb("tail", [P, 2 * NC * DM])
        x2, tmp = tail[:, 0:NC * DM], tail[:, NC * DM:2 * NC * DM]
        fac = tail
        gbb = sb("gbb", [P, DM])

        ld_c = sem("ld_c")
        ld_mod = sem("ld_mod")
        ld_dt = sem("ld_dt")
        ld_small = sem("ld_small")
        ld_z = sem("ld_z")
        ld_rest = sem("ld_rest")
        ld_fac = sem("ld_fac")
        ld_w = [sem(f"ld_w{g}") for g in range(UNITS)]
        consts = sem("consts")
        w_hi_done = sem("w_hi_done")
        w_lo_done = sem("w_lo_done")
        c_silu = sem("c_silu")
        mod_ps = sem("mod_ps")
        mod_sb = sem("mod_sb")
        gate_ps = sem("gate_ps")
        gate_sb = sem("gate_sb")
        wo_done = sem("wo_done")
        fsum_step = sem("fsum_step")
        f_done = sem("f_done")

        x_loaded = signal("x_loaded", 1, 16)
        stored = signal("stored", 1, 16)
        modb_ready = [signal(f"modb_ready{n}", 1) for n in range(2)]
        stats_done = [signal(f"stats_done{n}", NC) for n in range(2)]
        var_ready = [signal(f"var_ready{n}", NC) for n in range(2)]
        veps_ready = [signal(f"veps_ready{n}", 2) for n in range(2)]
        rstd_ready = [signal(f"rstd_ready{n}", 2) for n in range(2)]
        xn_ready = [signal(f"xn_ready{n}", NC) for n in range(2)]
        hT_ps = [signal(f"hT_ps{n}", 2 * KD) for n in range(2)]
        h_ready = [signal(f"h_ready{n}", 2 * KD) for n in range(2)]
        hhi_ready = signal("hhi_ready", KD)
        hlo_ready = signal("hlo_ready", KD)
        dt_ps = signal("dt_ps", 1)
        dt_step = signal("dt_step", 3)
        sp_step = signal("sp_step", 2)
        adt_ready = signal("adt_ready", 2)
        acs_ps = signal("acs_ps", 1)
        nacs_ready = signal("nacs_ready", 1)
        exin_ready = signal("exin_ready", 1)
        acs_ready = signal("acs_ready", 2)
        exout_ready = signal("exout_ready", 2)
        wdec_ready = signal("wdec_ready", 1)
        seg_ps = signal("seg_ps", NH)
        e_ready = signal("e_ready", NH)
        wide_ps = signal("wide_ps", WIDE)
        taps_ready = signal("taps_ready", TILES)
        uv_ready = signal("uv_ready", TILES)
        s_ready = signal("s_ready", TILES)
        xbc_ready = signal("xbc_ready", TILES)
        z_copied = signal("z_copied", NC)
        z_ready = signal("z_ready", 1)
        xT_ps = signal("xT_ps", UNITS)
        xtok_ready = signal("xtok_ready", UNITS)
        xdt_ready = signal("xdt_ready", UNITS)
        xw_ready = signal("xw_ready", UNITS)
        xd_ready = signal("xd_ready", UNITS)
        g_ps = signal("g_ps", 2 * UNITS)
        m_ready = signal("m_ready", 2 * UNITS)
        bT_ps = signal("bT_ps", 2 * UNITS)
        btok_ready = signal("btok_ready", 2 * UNITS)
        st_ps = signal("st_ps", UNITS)
        prev_ready = signal("prev_ready", 3 * UNITS)
        ydiag_ps = signal("ydiag_ps", UNITS)
        yoff_ps = signal("yoff_ps", UNITS)
        toff_ready = signal("toff_ready", UNITS)
        ysum_ready = signal("ysum_ready", UNITS)
        yd_ready = signal("yd_ready", UNITS)
        yg_ready = signal("yg_ready", UNITS)
        sq_ready = signal("sq_ready", UNITS)
        ms_ready = signal("ms_ready", UNITS)
        mse_ready = signal("mse_ready", UNITS)
        rms_ready = signal("rms_ready", UNITS)
        yn_ready = signal("yn_ready", UNITS)
        yT_ps = signal("yT_ps", UNITS)
        yT_ready = signal("yT_ready", UNITS)
        attn_ps = signal("attn_ps", 2)
        gated = signal("gated", 2)
        x2_ready = signal("x2_ready", 2)
        gbb_ready = signal("gbb_ready", 1)
        x2b_ready = signal("x2b_ready", 1)
        ffn_ps = signal("ffn_ps", 2)
        ffn_gated = signal("ffn_gated", 2)
        out_ready = signal("out_ready", 2)

        WZ = UNITS * KD * UW
        WEIGHTS = [(0, KD * UW), (WZ, KD * DI)] + [(g * KD * UW, KD * UW) for g in range(1, UNITS)]

        H_BANKS = ((3, 0), (3, 6))
        LAST_H_BANKS = ((3, 6), (4, 5))

        def is_last(b):
            return type(b) is int and b == BATCH - 1

        def attn_bank(b, cp):
            return bank[((3, 7), (0, 1))[is_last(b)][cp]]

        def w_tile(w, g, k, j):
            at = g * KD * UW + k * UW + j * P
            return w[:, at:at + P]

        def xbc_tile(g, j):
            at = ((g % 2) * TPU + j) * SEQ
            return xbc[:, at:at + SEQ]

        def slot(buf, t):
            at = (t % SLOTS) * SEQ
            return buf[:, at:at + SEQ]

        def chunk(ap, c):
            return ap[:, c * P:(c + 1) * P]

        def per_head(tile, g, c0=0):
            v = tile.rearrange("p (c h) -> p c h", c=NC)[:, c0:NC, 2 * g:2 * g + 2]
            return v.unsqueeze(3).broadcast_to([P, NC - c0, 2, HD])

        def by_head(ap, c0=0):
            return ap.rearrange("p (c h d) -> p c h d", h=2, d=HD)

        block = ctx.enter_context(nc.Block())

        @block.sync
        def _(sp):
            x_loaded.prime(sp)
            stored.prime(sp)
            x_rows = x_in.rearrange("b (c p) d -> p b c d", p=P)
            out_rows = out.rearrange("b (c p) d -> p b c d", p=P)

            def load_x(b):
                dst = xs[:, bass.ds((b % 2) * (NC * DM), NC * DM)].rearrange("p (o c d) -> p o c d", o=1, c=NC)
                sp.dma_start(dst, x_rows[:, bass.ds(b, 1)]).then_inc(x_loaded.sem, 16)

            def load_mod(n):
                cols = slice(n * 3 * DM, (n + 1) * 3 * DM)
                sp.dma_start(w_mod_sb[:, 0:KD * 6 * DM].rearrange("p (k m) -> p k m", k=KD)[:, :, cols],
                             w_mod.rearrange("p (k m) -> p k m", k=KD)[:, :, cols]).then_inc(ld_mod, 16)

            def load_w(g):
                sp.dma_start(stage[:, g * KD * UW:(g + 1) * KD * UW], w_xbc[g]).then_inc(ld_w[g], 16)

            half_rank = RANK // 2 * KD * DM
            sp.dma_start(ct[:], c_t).then_inc(ld_c, 16)
            load_x(0)
            load_mod(0)
            load_w(0)
            sp.dma_start(wdt[:], w_dt).then_inc(ld_dt, 16)
            for dst, src in ((cw, conv_w), (cb, conv_b), (arow, a_row), (drow, d_row), (dtb, dtb_row), (nw, norm_w)):
                sp.dma_start(dst[:], src).then_inc(ld_small, 16)
            sp.dma_start(stage[:, WZ:WZ + KD * DI], w_z).then_inc(ld_z, 16)
            load_w(1)
            sp.wait_ge(ld_mod, 16)
            load_mod(1)
            load_w(2)
            load_w(3)
            sp.dma_start(fac[:], factors[:, 0:half_rank]).then_inc(ld_fac, 16)
            sp.dma_start(wo[:], w_out).then_inc(ld_rest, 16)
            sp.dma_start(fbias[:], ffn_bias).then_inc(ld_rest, 16)
            sp.wait_ge(x_loaded.sem, x_loaded.done(0, 0))
            load_x(1)
            sp.wait_ge(fsum_step, RANK // 2 - 1)
            sp.dma_start(fac[:], factors[:, half_rank:2 * half_rank]).then_inc(ld_fac, 16)

            def store(b):
                sp.wait_ge(out_ready.sem, out_ready.done(b, 1))
                src = tmp.rearrange("p (o c d) -> p o c d", o=1, c=NC)
                sp.dma_start(out_rows[:, bass.ds(b, 1)], src).then_inc(stored.sem, 16)

            with sp.Fori(0, BATCH - 2) as b:
                store(b)
                sp.wait_ge(x_loaded.sem, x_loaded.done(b, 1))
                sp.wait_ge(x2_ready.sem, x2_ready.done(b, 1))
                load_x(b + 2)
            with sp.Fori(BATCH - 2, BATCH) as b:
                store(b)
            sp.wait_ge(stored.sem, stored.done(BATCH - 1, 0))

        @block.gpsimd
        def _(pool):
            for s in (*veps_ready, *rstd_ready, s_ready, xdt_ready, xw_ready, xd_ready, yg_ready,
                      mse_ready, rms_ready, x2b_ready, gbb_ready):
                s.prime(pool)
            made = [0]

            def make(ins):
                ins.then_inc(consts, 1)
                made[0] += 1

            make(pool.memset(ident[:], 0.0))
            make(pool.memset(selb[:], 0.0))
            make(pool.memset(ones[:], 1.0))
            make(pool.memset(tap0[:], 0.0))
            make(pool.memset(toff[:], 0.0))
            make(pool.memset(half[:], -0.5))
            make(pool.memset(eps[:], EPS))
            make(pool.memset(neg[:].bitcast(F32), 0.0))
            make(pool.memset(pairs[:].bitcast(F32), 0.0))
            pool.wait_ge(consts, made[0])
            make(pool.affine_select(out=ident[:], in_=ident[:], compare_op=ALU.not_equal, fill=1.0,
                                    base=0, pattern=[[-1, P]], channel_multiplier=1))
            sb3 = selb[:].rearrange("p (b m) -> p b m", b=BATCH)
            make(pool.affine_select(out=sb3, in_=sb3, compare_op=ALU.not_equal, fill=1.0,
                                    base=0, pattern=[[-1, BATCH], [0, P]], channel_multiplier=1))
            make(pool.affine_select(out=tri[:], in_=ones[:], compare_op=ALU.is_ge, fill=0.0,
                                    base=0, pattern=[[1, P]], channel_multiplier=-1))
            make(pool.affine_select(out=neg[:], in_=neg[:].bitcast(F32), compare_op=ALU.is_ge, fill=MASKED,
                                    base=0, pattern=[[1, P]], channel_multiplier=-1))
            make(pool.affine_select(out=pairs[:], in_=pairs[:].bitcast(F32), compare_op=ALU.not_equal, fill=1.0,
                                    base=0, pattern=[[-1, NQ]], channel_multiplier=1))
            pool.wait_ge(consts, made[0])
            make(pool.affine_select(out=pairs[:], in_=pairs[:].bitcast(F32), compare_op=ALU.not_equal, fill=1.0,
                                    base=-NQ, pattern=[[-1, NQ]], channel_multiplier=1))
            make(pool.affine_select(out=identr[:], in_=ident[:], compare_op=ALU.is_ge, fill=0.0,
                                    base=0, pattern=[[0, P]], channel_multiplier=0))
            assert made[0] == CONSTS

            def rstd_of(b, n, halves=(0, 1)):
                chunks = slice(halves[0] * NC // 2, (halves[-1] + 1) * NC // 2)
                pool.wait_ge(var_ready[n].sem, var_ready[n].done(b, chunks.stop - 1))
                var = mv[n][:].rearrange("p (c s) -> p c s", s=2)[:, chunks, 1]
                pool.tensor_tensor(veps[n][:, chunks], var, eps[:, chunks], ALU.add).then_inc(veps_ready[n].sem, len(halves))
                pool.wait_ge(veps_ready[n].sem, veps_ready[n].done(b, halves[-1]))
                pool.tensor_tensor(rstd[n][:, chunks], veps[n][:, chunks], half[:, chunks],
                                   ALU.pow).then_inc(rstd_ready[n].sem, len(halves))

            def add_taps(b, t):
                pool.wait_ge(uv_ready.sem, uv_ready.done(b, t))
                pool.tensor_tensor(slot(part, t), slot(part, t), slot(tap0, t), ALU.add).then_inc(s_ready.sem, 1)

            def scale_x(b, g):
                pool.wait_ge(xtok_ready.sem, xtok_ready.done(b, g))
                pool.wait_ge(wdec_ready.sem, wdec_ready.done(b, 0))
                pool.wait_ge(st_ps.sem, st_ps.done(b, g - 1))
                pool.tensor_tensor(by_head(xw[:]), by_head(xtok[:]), per_head(wdec[:], g), ALU.mult).then_inc(xw_ready.sem, 1)
                pool.wait_ge(ydiag_ps.sem, ydiag_ps.done(b, g - 1))
                pool.tensor_tensor(by_head(xdt[:]), by_head(xtok[:]), per_head(dt[:], g), ALU.mult).then_inc(xdt_ready.sem, 1)

            def skip_x(b, g):
                pool.wait_ge(yd_ready.sem, yd_ready.done(b, g - 1))
                dd = drow[:, 2 * g:2 * g + 2].unsqueeze(1).unsqueeze(3).broadcast_to([P, NC, 2, HD])
                pool.tensor_tensor(by_head(xd[:]), by_head(xtok[:]), dd, ALU.mult).then_inc(xd_ready.sem, 1)

            def gate_y(b, g):
                pool.wait_ge(z_ready.sem, z_ready.done(b, 0))
                pool.wait_ge(yT_ps.sem, yT_ps.done(b, g - UNITS))
                pool.wait_ge(yd_ready.sem, yd_ready.done(b, g))
                z = zs.rearrange("p (c i) -> p c i", c=NC)[:, :, g * P:(g + 1) * P]
                dst = yg[:, g * SEQ:(g + 1) * SEQ].rearrange("p (c i) -> p c i", c=NC)
                pool.tensor_tensor(dst, ysum[:].rearrange("p (c i) -> p c i", c=NC), z, ALU.mult).then_inc(yg_ready.sem, 1)

            def rms_of(b, g):
                pool.wait_ge(ms_ready.sem, ms_ready.done(b, g))
                pool.tensor_tensor(mse[:], ms[:], eps[:], ALU.add).then_inc(mse_ready.sem, 1)
                pool.wait_ge(mse_ready.sem, mse_ready.done(b, g))
                pool.wait_ge(yn_ready.sem, yn_ready.done(b, g - 1))
                pool.tensor_tensor(rms[:], mse[:], half[:], ALU.pow).then_inc(rms_ready.sem, 1)

            def ffn_bias_of(b):
                gb = gab[:, bass.ds(b * (2 * DM) + DM, DM)]
                pool.wait_ge(gate_sb, BATCH)
                pool.wait_ge(ld_rest, 32)
                pool.wait_ge(x2b_ready.sem, x2b_ready.done(b, -1))
                pool.tensor_tensor(gbb[:], gb, fbias[:], ALU.mult).then_inc(gbb_ready.sem, 1)

            def add_bias(b):
                pool.wait_ge(gbb_ready.sem, gbb_ready.done(b, 0))
                pool.wait_ge(xn_ready[1].sem, xn_ready[1].done(b, NC - 1))
                x2v = x2.rearrange("p (c d) -> p c d", c=NC)
                bias = gbb[:].unsqueeze(1).broadcast_to([P, NC, DM])
                pool.tensor_tensor(x2v, x2v, bias, ALU.add).then_inc(x2b_ready.sem, 1)

            def unit(b, g, nxt, next_batch):
                def taps(j):
                    if nxt:
                        add_taps(nxt[0], nxt[1] * TPU + j)

                if g < UNITS - 1:
                    scale_x(b, g)
                gate_y(b, g - 1)
                if g == UNITS - 1:
                    scale_x(b, g)
                taps(0)
                taps(1)
                rms_of(b, g - 1)
                taps(2)
                skip_x(b, g)
                if g == 1 and next_batch is not None:
                    rstd_of(next_batch, 0)
                taps(3)
                taps(4)

            def turn_to(b, old=None):
                if old is not None:
                    gate_y(old, UNITS - 1)
                    rms_of(old, UNITS - 1)
                if b is not None:
                    add_taps(b, TPU)
                    add_taps(b, TPU + 1)
                    scale_x(b, 0)
                    add_taps(b, TPU + 2)
                    skip_x(b, 0)
                    add_taps(b, TPU + 3)
                if old is not None:
                    ffn_bias_of(old)
                    if b is None:
                        rstd_of(old, 1, (0,))
                        rstd_of(old, 1, (1,))
                    else:
                        rstd_of(old, 1)
                    add_bias(old)
                if b is not None:
                    add_taps(b, TPU + 4)

            def sum_factors(ranks):
                FW = KD * DM
                for r in ranks:
                    pool.wait_ge(ld_fac, 16 if r < RANK // 2 else 32)
                    at = (r % (RANK // 2)) * FW
                    first = fac[:, 0:FW] if r == 1 else fsum[:]
                    if r > 1:
                        pool.wait_ge(fsum_step, r - 1)
                    pool.tensor_tensor(fsum[:], first, fac[:, at:at + FW], ALU.add).then_inc(fsum_step, 1)

            rstd_of(0, 0)
            for t in range(TPU):
                add_taps(0, t)
            pool.wait_ge(ld_small, 16 * SMALL)
            sum_factors(range(1, RANK))
            turn_to(0)

            def batch(b, nb):
                for g in range(1, UNITS):
                    nxt = (b, g + 1) if g + 1 < UNITS else (nb, 0) if nb is not None else None
                    unit(b, g, nxt, nb)
                turn_to(nb, b)

            with pool.Fori(0, BATCH - 1) as b:
                batch(b, b + 1)
            batch(BATCH - 1, None)

        @block.scalar
        def _(act):
            for s in (*h_ready, sp_step, exout_ready, e_ready, taps_ready, xbc_ready, z_ready, xtok_ready,
                      btok_ready, sq_ready, yT_ready):
                s.prime(act)
            act.wait_ge(ld_c, 16)
            act.activation(ct[:], ct[:], ACT.Silu).then_inc(c_silu, 1)

            def round_weights(n):
                lo, size = WEIGHTS[n]
                act.wait_ge(ld_z if n == 1 else ld_w[max(n - 1, 0)], 16)
                act.activation(w_hi[:, lo:lo + size], stage[:, lo:lo + size], ACT.Copy).then_inc(w_hi_done, 1)

            def evac_h(b, n):
                act.wait_ge(modb_ready[n].sem, modb_ready[n].done(b, 0))
                for k in range(KD):
                    act.wait_ge(hT_ps[n].sem, hT_ps[n].done(b, 2 * k + 1))
                    act.activation(h[:, k * SEQ:(k + 1) * SEQ], bank[H_BANKS[n][k]][:], ACT.Identity,
                                   bias=modb[n][:, k:k + 1], scale=modb[n][:, 2 + k:3 + k]).then_inc(h_ready[n].sem, 2)

            def evac_last_h(b):
                act.wait_ge(modb_ready[1].sem, modb_ready[1].done(b, 0))
                for cp in range(2):
                    for k in range(KD):
                        cols = slice(cp * SEQ // 2, (cp + 1) * SEQ // 2)
                        act.wait_ge(hT_ps[1].sem, hT_ps[1].done(b, 2 * cp + k))
                        act.activation(h[:, k * SEQ:(k + 1) * SEQ][:, cols], bank[LAST_H_BANKS[cp][k]][:, cols], ACT.Identity,
                                       bias=modb[1][:, k:k + 1], scale=modb[1][:, 2 + k:3 + k]).then_inc(h_ready[1].sem, 1)

            def taps(b, t):
                n = ring_index(t)
                ps = bank[n % RING]
                act.wait_ge(wide_ps.sem, wide_ps.done(b, n))
                act.wait_ge(s_ready.sem, s_ready.done(b, t - SLOTS))
                act.wait_ge(xbc_ready.sem, xbc_ready.done(b, t - SLOTS))
                act.activation(slot(part, t), ps[:], ACT.Identity, bias=cb[:, t:t + 1],
                               scale=cw[:, TAPS * t + 3:TAPS * t + 4])
                act.activation(slot(tap0, t)[:, 2:SEQ], ps[:, 0:SEQ - 2], ACT.Copy,
                               scale=cw[:, TAPS * t + 1:TAPS * t + 2]).then_inc(taps_ready.sem, 1)

            def silu(b, t):
                g, j = divmod(t, TPU)
                act.wait_ge(s_ready.sem, s_ready.done(b, t))
                act.wait_ge(yoff_ps.sem, yoff_ps.done(b, g - 2))
                act.activation(xbc_tile(g, j), slot(part, t), ACT.Silu).then_inc(xbc_ready.sem, 1)

            def silu_z(b):
                act.wait_ge(z_copied.sem, z_copied.done(b, NC - 1))
                act.activation(zs, zs, ACT.Silu).then_inc(z_ready.sem, 1)

            def softplus(b):
                act.preload_act_table_set("natural_log_exp_and_others")
                act.wait_ge(dt_step.sem, dt_step.done(b, 1))
                act.activation(dte[:], dta[:], ACT.Exp, scale=-1.0).then_inc(sp_step.sem, 1)
                act.wait_ge(sp_step.sem, sp_step.done(b, 0))
                act.activation(dtl[:], dte[:], ACT.Ln, bias=1.0).then_inc(sp_step.sem, 1)

            def single_decays(b):
                act.wait_ge(exin_ready.sem, exin_ready.done(b, 0))
                act.wait_ge(prev_ready.sem, prev_ready.done(b, -1))
                act.activation(exout[:], exin[:], ACT.Exp).then_inc(exout_ready.sem, 1)
                act.wait_ge(toff_ready.sem, toff_ready.done(b, -1))
                act.activation(eacs[:], nacs[:], ACT.Exp, scale=-1.0).then_inc(exout_ready.sem, 1)
                act.wait_ge(ydiag_ps.sem, ydiag_ps.done(b, -1))

            def decays(b, heads):
                for hh in heads:
                    act.wait_ge(seg_ps.sem, seg_ps.done(b, hh))
                    for c in range(NC):
                        q = c * NH + hh
                        ins = act.activation(E[:, (hh * NC + c) * P:(hh * NC + c + 1) * P],
                                             chunk(bank[4 + hh % 2], c), ACT.Exp, bias=nacs[:, q:q + 1])
                    ins.then_inc(e_ready.sem, 1)

            def evac_x(b, g):
                act.wait_ge(xT_ps.sem, xT_ps.done(b, g))
                act.wait_ge(xd_ready.sem, xd_ready.done(b, g - 1))
                act.activation(xtok[:], bank[3][:], ACT.Copy).then_inc(xtok_ready.sem, 1)

            def evac_b(b, g, hh):
                act.wait_ge(bT_ps.sem, bT_ps.done(b, 2 * g + hh))
                act.wait_ge(st_ps.sem, st_ps.done(b, g - 1))
                act.activation(btok[:, hh * SEQ:(hh + 1) * SEQ], bank[(6, 3)[hh]][:], ACT.Copy).then_inc(btok_ready.sem, 1)

            def square(b, g):
                act.wait_ge(ms_ready.sem, ms_ready.done(b, g - 1))
                act.wait_ge(yg_ready.sem, yg_ready.done(b, g))
                act.activation(sq[:], yg[:, g * SEQ:(g + 1) * SEQ], ACT.Square, scale=HD ** -0.5).then_inc(sq_ready.sem, 1)

            def evac_y(b, g):
                act.wait_ge(attn_ps.sem, attn_ps.done(b, -1))
                act.wait_ge(yT_ps.sem, yT_ps.done(b, g))
                act.activation(yT[:, g * SEQ:(g + 1) * SEQ], bank[6][:], ACT.Copy).then_inc(yT_ready.sem, 1)

            def unit(b, g, nxt, next_batch):
                def next_taps(j):
                    if nxt:
                        taps(nxt[0], nxt[1] * TPU + j)

                def next_silu(j):
                    if nxt:
                        silu(nxt[0], nxt[1] * TPU + j)

                if g == UNITS - 1:
                    silu(b, g * TPU + TPU - 1)
                    evac_x(b, g)
                    evac_b(b, g, 0)
                    next_taps(0)
                    evac_b(b, g, 1)
                    next_taps(1)
                else:
                    evac_x(b, g)
                    next_taps(0)
                    silu(b, g * TPU + TPU - 1)
                    evac_b(b, g, 0)
                    next_taps(1)
                    evac_b(b, g, 1)
                if g < UNITS - 1:
                    square(b, g - 1)
                    next_silu(0)
                else:
                    next_silu(0)
                    square(b, g - 1)
                next_taps(2)
                next_silu(1)
                next_taps(3)
                next_silu(2)
                if g == UNITS - 2 and next_batch is not None:
                    evac_h(next_batch, 0)
                next_taps(4)
                evac_y(b, g - 1)
                next_silu(3)

            def prepare_out():
                act.wait_ge(ld_rest, 32)
                for g in range(UNITS):
                    act.activation(wo[:, g * DM:(g + 1) * DM], wo[:, g * DM:(g + 1) * DM], ACT.Copy,
                                   scale=nw[:, g:g + 1]).then_inc(wo_done, 1)

            def turn_to(b, old=None):
                if b is not None:
                    evac_x(b, 0)
                    evac_b(b, 0, 0)
                    silu(b, TPU - 1)
                    softplus(b)
                if old is not None:
                    square(old, UNITS - 1)
                else:
                    prepare_out()
                if b is not None:
                    evac_b(b, 0, 1)
                    single_decays(b)
                    taps(b, TPU)
                    decays(b, (0, 1))
                    taps(b, TPU + 1)
                    decays(b, (2, 3))
                    taps(b, TPU + 2)
                    decays(b, (4, 5))
                if old is not None:
                    evac_y(old, UNITS - 1)
                if b is not None:
                    taps(b, TPU + 3)
                    decays(b, (6, 7))
                    for j in range(SLOTS):
                        silu(b, TPU + j)
                    taps(b, TPU + SLOTS)
                if b is None:
                    evac_last_h(old)
                elif old is not None:
                    evac_h(old, 1)
                if b is not None:
                    silu_z(b)

            round_weights(0)
            evac_h(0, 0)
            round_weights(1)
            act.wait_ge(ld_small, 16 * SMALL)
            act.wait_ge(consts, CONSTS)
            for t in range(TPU):
                taps(0, t)
                if t:
                    silu(0, t - 1)
                if t < UNITS - 1:
                    round_weights(2 + t)
            turn_to(0)
            for i in range(BATCH):
                act.wait_ge(gate_ps, i + 1)
                act.activation(gab[:, i * 2 * DM:(i + 1) * 2 * DM], bank[(3, 6)[i % 2]][:], ACT.Copy).then_inc(gate_sb, 1)
            act.wait_ge(fsum_step, RANK - 1)
            act.activation(fsum[:], fsum[:], ACT.Copy, scale=float(RANK) ** -0.5).then_inc(f_done, 1)

            def batch(b, nb):
                for g in range(1, UNITS):
                    unit(b, g, (b, g + 1) if g + 1 < UNITS else (nb, 0) if nb is not None else None, nb)
                turn_to(nb, b)

            with act.Fori(0, BATCH - 1) as b:
                batch(b, b + 1)
            batch(BATCH - 1, None)

        @block.vector
        def _(dve):
            for s in (*modb_ready, *stats_done, *var_ready, *xn_ready, yd_ready, hhi_ready, hlo_ready, dt_step, adt_ready,
                      nacs_ready, exin_ready, acs_ready, wdec_ready, uv_ready, z_copied, m_ready, prev_ready, toff_ready,
                      ysum_ready, ms_ready, yn_ready, gated, x2_ready, ffn_gated, out_ready):
                s.prime(dve)

            def modulation(n):
                dst = mod_all[:].rearrange("p (b n) -> p b n", b=BATCH)
                src = bank[4][:, 0:8 * BATCH].rearrange("p (n b) -> p b n", b=BATCH)
                dve.wait_ge(mod_ps, n + 1)
                dve.tensor_copy(dst[:, :, 4 * n:4 * n + 2], src[:, :, 4 * n:4 * n + 2])
                dve.tensor_scalar(dst[:, :, 4 * n + 2:4 * n + 4], src[:, :, 4 * n + 2:4 * n + 4], 1.0, None,
                                  ALU.add).then_inc(mod_sb, 1)

            def gates():
                dve.wait_ge(mod_ps, 3)
                gps = bank[5][0:BATCH, :]
                dve.tensor_scalar(gmag[:], gps, -1.0, 0.25, ALU.mult, ALU.max).then_inc(mod_sb, 1)
                dve.wait_ge(mod_sb, 3)
                dve.scalar_tensor_tensor(gmag[:], gps, 1.0, gmag[:], ALU.mult, ALU.max).then_inc(mod_sb, 1)
                dve.tensor_scalar(grow[:], gps, 0.0, 2.0, ALU.is_ge, ALU.mult).then_inc(mod_sb, 1)
                dve.wait_ge(mod_sb, 5)
                dve.scalar_tensor_tensor(grow[:], grow[:], 1.0, gmag[:], ALU.subtract, ALU.mult).then_inc(mod_sb, 1)

            def weight_rests(n):
                lo, size = WEIGHTS[n]
                dve.wait_ge(w_hi_done, n + 1)
                dve.tensor_tensor(w_lo[:, lo:lo + size], stage[:, lo:lo + size],
                                  w_hi[:, lo:lo + size].bitcast(F32), ALU.subtract).then_inc(w_lo_done, 1)

            def x_of(b, lo, size):
                return xs[:, bass.ds((b % 2) * (NC * DM) + lo, size)]

            def chunk_in(b, n, c):
                return x_of(b, c * DM, DM) if n == 0 else x2[:, c * DM:(c + 1) * DM]

            def norm_stats(b, n, chunks):
                for c in chunks:
                    dve.bn_stats(stats[n][:, 6 * c:6 * c + 6], chunk_in(b, n, c)).then_inc(stats_done[n].sem, 1)

            def norm_mod(b, n):
                dve.wait_ge(h_ready[n].sem, h_ready[n].done(b, -1))
                dve.tensor_copy(modb[n][:], mod_all[:, bass.ds(b * 8 + 4 * n, 4)]).then_inc(modb_ready[n].sem, 1)

            def norm_vars(b, n, chunks=range(NC), with_mod=True):
                dve.wait_ge(rstd_ready[n].sem, rstd_ready[n].done(b, -1))
                dve.wait_ge(stats_done[n].sem, stats_done[n].done(b, chunks[-1]))
                if with_mod:
                    norm_mod(b, n)
                for c in chunks:
                    dve.bn_aggr(mv[n][:, 2 * c:2 * c + 2], stats[n][:, 6 * c:6 * c + 6]).then_inc(var_ready[n].sem, 1)

            def norm_rows(b, n, chunks=range(NC)):
                dve.wait_ge(rstd_ready[n].sem, rstd_ready[n].done(b, chunks[-1] * 2 // NC))
                for c in chunks:
                    dve.tensor_scalar(xn[:, c * DM:(c + 1) * DM], chunk_in(b, n, c), mv[n][:, 2 * c:2 * c + 1],
                                      rstd[n][:, c:c + 1], ALU.subtract, ALU.mult).then_inc(xn_ready[n].sem, 1)

            def split_h(b):
                dve.wait_ge(wide_ps.sem, wide_ps.done(b, -1))
                for k in range(KD):
                    s = slice(k * SEQ, (k + 1) * SEQ)
                    dve.wait_ge(h_ready[0].sem, h_ready[0].done(b, 2 * k + 1))
                    dve.tensor_copy(h_hi[:, s], h[:, s]).then_inc(hhi_ready.sem, 1)
                    dve.wait_ge(hhi_ready.sem, hhi_ready.done(b, k))
                    dve.tensor_tensor(h_lo[:, s], h[:, s], h_hi[:, s].bitcast(F32), ALU.subtract).then_inc(hlo_ready.sem, 1)

            def rows(ap):
                return ap.rearrange("p (c h) -> p c h", c=NC)

            def row(ap):
                return ap.unsqueeze(1).broadcast_to([P, NC, NH])

            def raw_steps(b):
                dve.wait_ge(dt_ps.sem, dt_ps.done(b, 0))
                dve.tensor_tensor(rows(dtu[:]), rows(bank[7][:, 0:NQ]), row(dtb[:]), ALU.add).then_inc(dt_step.sem, 1)
                dve.wait_ge(dt_step.sem, dt_step.done(b, 0))
                dve.scalar_tensor_tensor(dta[:], dtu[:], -1.0, dtu[:], ALU.mult, ALU.max).then_inc(dt_step.sem, 1)

            def steps(b):
                dve.wait_ge(sp_step.sem, sp_step.done(b, 1))
                dve.wait_ge(xdt_ready.sem, xdt_ready.done(b, -1))
                dve.scalar_tensor_tensor(dt[:], dtu[:], 0.0, dtl[:], ALU.max, ALU.add).then_inc(dt_step.sem, 1)
                dve.wait_ge(dt_step.sem, dt_step.done(b, 2))
                for half_ in (adt[:, 0:NQ], adt[:, NQ:2 * NQ]):
                    dve.tensor_tensor(rows(half_), rows(dt[:]), row(arow[:]), ALU.mult).then_inc(adt_ready.sem, 1)

            def sums(b):
                acs_ps_, tot, acsT = bank[7][:, NQ:2 * NQ], bank[7][:, 2 * NQ:3 * NQ], bank[7][0:2 * NQ, P:2 * P]
                dve.wait_ge(acs_ps.sem, acs_ps.done(b, 0))
                dve.wait_ge(seg_ps.sem, seg_ps.done(b, -1))
                dve.tensor_copy(acs[:], acsT).then_inc(acs_ready.sem, 1)
                dve.wait_ge(e_ready.sem, e_ready.done(b, -1))
                dve.tensor_scalar(nacs[:], acs_ps_, -1.0, None, ALU.mult).then_inc(nacs_ready.sem, 1)
                dve.wait_ge(acs_ready.sem, acs_ready.done(b, 0))
                low = slice(NQ, 2 * NQ)
                dve.tensor_tensor(acs[low, :], acsT[low, :], acs[low, :].bitcast(F32), ALU.subtract).then_inc(acs_ready.sem, 1)
                dve.wait_ge(nacs_ready.sem, nacs_ready.done(b, 0))
                dve.tensor_tensor(exin[:, 0:NQ], tot, nacs[:], ALU.add)
                dve.tensor_copy(exin[:, NQ:2 * NQ], tot).then_inc(exin_ready.sem, 1)

            def weights_to_end(b):
                dve.wait_ge(exout_ready.sem, exout_ready.done(b, 1))
                dve.wait_ge(xw_ready.sem, xw_ready.done(b, -1))
                dve.tensor_tensor(wdec[:], dt[:], exout[:, 0:NQ], ALU.mult).then_inc(wdec_ready.sem, 1)

            def conv(b, t):
                ps = bank[ring_index(t) % RING]
                dve.wait_ge(taps_ready.sem, taps_ready.done(b, t))
                u, v = slot(part, t), slot(tap0, t)
                dve.scalar_tensor_tensor(u[:, 1:SEQ], ps[:, 0:SEQ - 1], cw[:, TAPS * t + 2:TAPS * t + 3],
                                         u[:, 1:SEQ], ALU.mult, ALU.add)
                dve.scalar_tensor_tensor(v[:, 3:SEQ], ps[:, 0:SEQ - 3], cw[:, TAPS * t:TAPS * t + 1],
                                         v[:, 3:SEQ], ALU.mult, ALU.add).then_inc(uv_ready.sem, 1)

            def copy_z(b, chunks):
                dve.wait_ge(yg_ready.sem, yg_ready.done(b, -1))
                for c in chunks:
                    n = TPU + c
                    dve.wait_ge(wide_ps.sem, wide_ps.done(b, n))
                    dve.tensor_copy(zs[:, c * DI:(c + 1) * DI], bank[n % RING][:]).then_inc(z_copied.sem, 1)

            def weigh(b, g):
                for hh in range(2):
                    hd = 2 * g + hh
                    dve.wait_ge(e_ready.sem, e_ready.done(b, hd))
                    dve.wait_ge(g_ps.sem, g_ps.done(b, hd))
                    dve.tensor_tensor(M[:, hd * SEQ:(hd + 1) * SEQ], bank[4 + hh][:],
                                      E[:, hd * SEQ:(hd + 1) * SEQ], ALU.mult).then_inc(m_ready.sem, 1)

            def carry(b, g):
                dve.wait_ge(st_ps.sem, st_ps.done(b, g))
                dve.wait_ge(yoff_ps.sem, yoff_ps.done(b, g - 1))
                dve.tensor_copy(prev[:, 0:P], bank[4][:, 0:P]).then_inc(prev_ready.sem, 1)
                for c in (1, 2):
                    dve.wait_ge(prev_ready.sem, prev_ready.done(b, 3 * g + c - 1))
                    for hh in range(2):
                        at = c * P + hh * HD
                        q = NQ + c * NH + 2 * g + hh
                        ins = dve.scalar_tensor_tensor(prev[:, at:at + HD], prev[:, at - P:at - P + HD],
                                                       exout[:, q:q + 1], bank[4][:, at:at + HD], ALU.mult, ALU.add)
                    ins.then_inc(prev_ready.sem, 1)

            def join(b, g):
                dve.wait_ge(yoff_ps.sem, yoff_ps.done(b, g))
                dve.tensor_tensor(by_head(toff[:, P:SEQ]), by_head(bank[5][:, P:SEQ]), per_head(eacs[:], g, 1),
                                  ALU.mult).then_inc(toff_ready.sem, 1)
                dve.wait_ge(toff_ready.sem, toff_ready.done(b, g))
                dve.wait_ge(ydiag_ps.sem, ydiag_ps.done(b, g))
                dve.wait_ge(yg_ready.sem, yg_ready.done(b, g - 1))
                dve.tensor_tensor(ysum[:], bank[7][:], toff[:], ALU.add).then_inc(ysum_ready.sem, 1)
                dve.wait_ge(xd_ready.sem, xd_ready.done(b, g))
                dve.wait_ge(ysum_ready.sem, ysum_ready.done(b, g))
                dve.tensor_tensor(ysum[:], ysum[:], xd[:], ALU.add).then_inc(yd_ready.sem, 1)

            def mean_square(b, g):
                dve.wait_ge(sq_ready.sem, sq_ready.done(b, g))
                dve.wait_ge(mse_ready.sem, mse_ready.done(b, g - 1))
                dve.tensor_reduce(ms[:], sq[:].rearrange("p (n d) -> p n d", d=HD), AX_X, ALU.add).then_inc(ms_ready.sem, 1)

            def normed(b, g):
                dve.wait_ge(rms_ready.sem, rms_ready.done(b, g))
                y = yg[:, g * SEQ:(g + 1) * SEQ].rearrange("p (n d) -> p n d", d=HD)
                dve.tensor_tensor(y, y, rms[:].unsqueeze(2).broadcast_to([P, 8, HD]), ALU.mult).then_inc(yn_ready.sem, 1)

            def residual(b, cp):
                ga = gab[:, bass.ds(b * (2 * DM), DM)].unsqueeze(1).broadcast_to([P, 2, DM])
                s = slice(cp * 512, (cp + 1) * 512)
                if cp == 0:
                    dve.wait_ge(gate_sb, BATCH)
                    dve.wait_ge(fsum_step, RANK - 1)
                    dve.wait_ge(stored.sem, stored.done(b, -1))
                dve.wait_ge(attn_ps.sem, attn_ps.done(b, cp))
                dve.tensor_tensor(tmp[:, s].rearrange("p (c d) -> p c d", c=2),
                                  attn_bank(b, cp)[:].rearrange("p (c d) -> p c d", c=2), ga, ALU.mult).then_inc(gated.sem, 1)
                dve.wait_ge(gated.sem, gated.done(b, cp))
                dve.tensor_tensor(x2[:, s], tmp[:, s], x_of(b, cp * 512, 512), ALU.add).then_inc(x2_ready.sem, 1)

            def finish(b, cp):
                gb = gab[:, bass.ds(b * (2 * DM) + DM, DM)].unsqueeze(1).broadcast_to([P, 2, DM])
                s = slice(cp * 512, (cp + 1) * 512)
                dve.wait_ge(ffn_ps.sem, ffn_ps.done(b, cp))
                dve.tensor_tensor(tmp[:, s].rearrange("p (c d) -> p c d", c=2),
                                  bank[(3, 6)[cp]][:].rearrange("p (c d) -> p c d", c=2), gb, ALU.mult).then_inc(ffn_gated.sem, 1)
                dve.wait_ge(ffn_gated.sem, ffn_gated.done(b, cp))
                dve.wait_ge(x2b_ready.sem, x2b_ready.done(b, 0))
                dve.tensor_tensor(tmp[:, s], tmp[:, s], x2[:, s], ALU.add).then_inc(out_ready.sem, 1)

            def residual_norm(b, cp):
                residual(b, cp)
                dve.wait_ge(x2_ready.sem, x2_ready.done(b, cp))
                norm_stats(b, 1, (2 * cp, 2 * cp + 1))

            def unit(b, g, nxt, next_batch):
                def taps(j):
                    if nxt:
                        conv(nxt[0], nxt[1] * TPU + j)

                join(b, g - 1)
                if g == UNITS - 1:
                    weigh(b, g)
                taps(0)
                if g < UNITS - 1:
                    weigh(b, g)
                taps(1)
                if g == UNITS - 1 and nxt:
                    raw_steps(nxt[0])
                mean_square(b, g - 1)
                if next_batch is not None and g == 1:
                    dve.wait_ge(x_loaded.sem, x_loaded.done(next_batch, 0))
                    norm_stats(next_batch, 0, range(NC))
                    norm_vars(next_batch, 0)
                taps(2)
                carry(b, g)
                if next_batch is not None and g == UNITS - 2:
                    dve.wait_ge(hT_ps[1].sem, hT_ps[1].done(next_batch - 1, -1))
                    norm_rows(next_batch, 0)
                normed(b, g - 1)
                taps(3)
                if next_batch is not None and g == UNITS - 2:
                    split_h(next_batch)
                taps(4)

            def turn_to(b, old=None):
                if old is not None:
                    join(old, UNITS - 1)
                if b is not None:
                    copy_z(b, (0, 1))
                    steps(b)
                    copy_z(b, (2,))
                if old is not None:
                    mean_square(old, UNITS - 1)
                if b is not None:
                    copy_z(b, (3,))
                    sums(b)
                    conv(b, TPU)
                if b is not None:
                    weights_to_end(b)
                    conv(b, TPU + 1)
                if old is not None:
                    normed(old, UNITS - 1)
                else:
                    weight_rests(3)
                    weight_rests(4)
                if b is not None:
                    conv(b, TPU + 2)
                    conv(b, TPU + 3)
                first, second = range(0, NC // 2), range(NC // 2, NC)
                if old is not None:
                    residual_norm(old, 0)
                if b is None:
                    norm_vars(old, 1, first)
                    residual_norm(old, 1)
                    norm_vars(old, 1, second, with_mod=False)
                    norm_rows(old, 1, first)
                    norm_rows(old, 1, second)
                else:
                    weigh(b, 0)
                    if old is not None:
                        residual_norm(old, 1)
                        norm_vars(old, 1)
                    carry(b, 0)
                    if old is not None:
                        dve.wait_ge(hT_ps[0].sem, hT_ps[0].done(b, 2 * KD - 1))
                        norm_rows(old, 1)
                    conv(b, TPU + 4)
                if old is not None:
                    finish(old, 0)
                    finish(old, 1)

            dve.wait_ge(x_loaded.sem, x_loaded.done(0, 0))
            norm_stats(0, 0, range(NC))
            norm_vars(0, 0, with_mod=False)
            norm_rows(0, 0)
            modulation(0)
            dve.wait_ge(mod_sb, 1)
            norm_mod(0, 0)
            weight_rests(0)
            split_h(0)
            dve.wait_ge(ld_small, 16 * SMALL)
            dve.wait_ge(consts, CONSTS)
            for t in range(TPU):
                conv(0, t)
                if t < 2:
                    weight_rests(t + 1)
            raw_steps(0)
            modulation(1)
            gates()
            turn_to(0)
            def batch(b, nb):
                for g in range(1, UNITS):
                    unit(b, g, (b, g + 1) if g + 1 < UNITS else (nb, 0) if nb is not None else None, nb)
                turn_to(nb, b)

            with dve.Fori(0, BATCH - 1) as b:
                batch(b, b + 1)
            batch(BATCH - 1, None)

        @block.tensor
        def _(pe):
            for s in (*hT_ps, dt_ps, acs_ps, seg_ps, wide_ps, xT_ps, g_ps, bT_ps, st_ps, ydiag_ps, yoff_ps,
                      yT_ps, attn_ps, ffn_ps):
                s.prime(pe)
            pe.wait_ge(c_silu, 1)

            def modulation(n, blocks):
                pe.wait_ge(ld_mod, 16 * (n + 1))
                for i, m in enumerate(blocks):
                    at = (len(blocks) * n + i) * BATCH
                    for k in range(KD):
                        mm = pe.matmul(bank[4][:, at:at + BATCH], w_mod_sb[:, k * 6 * DM + m * P:k * 6 * DM + (m + 1) * P],
                                       ct[:, k * BATCH:(k + 1) * BATCH], start=(k == 0), stop=(k == KD - 1))
                mm.then_inc(mod_ps, 1)

            def gates():
                for n, m in enumerate((2, 5)):
                    for k in range(KD):
                        at = k * 6 * DM + m * DM
                        mm = pe.matmul(bank[5][0:BATCH, n * DM:(n + 1) * DM], ct[:, k * BATCH:(k + 1) * BATCH],
                                       w_mod_sb[:, at:at + DM], start=(k == 0), stop=(k == KD - 1))
                mm.then_inc(mod_ps, 1)

            def spread_gates():
                pe.wait_ge(mod_sb, 6)
                pe.wait_ge(btok_ready.sem, btok_ready.done(0, 1))
                for i in range(BATCH):
                    if i >= 2:
                        pe.wait_ge(gate_sb, i - 1)
                    pe.matmul(bank[(3, 6)[i % 2]][:], selb[:, i * P:(i + 1) * P], grow[:], start=True, stop=True).then_inc(gate_ps, 1)

            def ring_free(b, n):
                m = n - RING
                if TPU <= m < TPU + NC:
                    pe.wait_ge(z_copied.sem, z_copied.done(b, m - TPU))
                else:
                    t = m if m < TPU else m - NC
                    pe.wait_ge(uv_ready.sem, uv_ready.done(b, t))

            def turn_h(b, n):
                pe.wait_ge(xn_ready[n].sem, xn_ready[n].done(b, NC - 1))
                for k in range(KD):
                    if n == 0 and k == 0:
                        pe.wait_ge(btok_ready.sem, btok_ready.done(b - 1, 5))
                    elif n == 0:
                        ring_free(b, 0)
                    elif k == 0:
                        pe.wait_ge(gated.sem, gated.done(b, 0))
                    else:
                        pe.wait_ge(yT_ready.sem, yT_ready.done(b, UNITS - 1))
                    for c in range(NC):
                        mm = pe.transpose(chunk(bank[H_BANKS[n][k]], c), xn[:, c * DM + k * P:c * DM + (k + 1) * P], ident[:])
                    mm.then_inc(hT_ps[n].sem, 2)

            def turn_last_h(b, cp):
                pe.wait_ge(xn_ready[1].sem, xn_ready[1].done(b, 2 * cp + 1))
                pe.wait_ge(btok_ready.sem, btok_ready.done(b, 2 * UNITS - 1))
                pe.wait_ge(yT_ready.sem, yT_ready.done(b, UNITS - 1))
                pe.wait_ge(toff_ready.sem, toff_ready.done(b, UNITS - 1))
                for k in range(KD):
                    for c in (2 * cp, 2 * cp + 1):
                        mm = pe.transpose(chunk(bank[LAST_H_BANKS[cp][k]], c), xn[:, c * DM + k * P:c * DM + (k + 1) * P],
                                          ident[:])
                    mm.then_inc(hT_ps[1].sem, 1)

            def project(b, t):
                g, j = divmod(t, TPU)
                n = ring_index(t)
                ring_free(b, n)
                ps = bank[n % RING][:]
                i = 0
                for w, hs in ((w_hi, (h_hi, h_lo)), (w_lo, (h_hi,))):
                    for k in range(KD):
                        for hx in hs:
                            mm = pe.matmul(ps, w_tile(w, g, k, j), hx[:, k * SEQ:(k + 1) * SEQ],
                                           start=(i == 0), stop=(i == 3 * KD - 1))
                            i += 1
                mm.then_inc(wide_ps.sem, 1)

            def project_z(b, chunks):
                for c in chunks:
                    n = TPU + c
                    ring_free(b, n)
                    i = 0
                    for hx, ws in ((h_hi, (w_hi, w_lo)), (h_lo, (w_hi,))):
                        for k in range(KD):
                            for w in ws:
                                mm = pe.matmul(bank[n % RING][:], hx[:, k * SEQ + c * P:k * SEQ + (c + 1) * P],
                                               w[:, WZ + k * DI:WZ + (k + 1) * DI], start=(i == 0), stop=(i == 3 * KD - 1))
                                i += 1
                    mm.then_inc(wide_ps.sem, 1)

            def project_dt(b):
                pe.wait_ge(h_ready[0].sem, h_ready[0].done(b, 2 * KD - 1))
                pe.wait_ge(ysum_ready.sem, ysum_ready.done(b, -2))
                for c in range(NC):
                    for k in range(KD):
                        mm = pe.matmul(bank[7][:, c * NH:(c + 1) * NH], h[:, k * SEQ + c * P:k * SEQ + (c + 1) * P],
                                       wdt[:, k * NH:(k + 1) * NH], start=(k == 0), stop=(k == KD - 1))
                mm.then_inc(dt_ps.sem, 1)

            def sum_a(b):
                pe.wait_ge(ysum_ready.sem, ysum_ready.done(b, -1))
                pe.wait_ge(adt_ready.sem, adt_ready.done(b, 1))
                pe.matmul(bank[7][0:2 * NQ, P:2 * P], adt[:], tri[:], start=True, stop=True)
                pe.matmul(bank[7][:, NQ:2 * NQ], tri[:], adt[:, 0:NQ], start=True, stop=True)
                pe.matmul(bank[7][:, 2 * NQ:3 * NQ], ones[:], adt[:, 0:NQ], start=True, stop=True).then_inc(acs_ps.sem, 1)

            def segments(b, heads):
                pe.wait_ge(acs_ready.sem, acs_ready.done(b, 1))
                for hh in heads:
                    if hh >= 2:
                        pe.wait_ge(e_ready.sem, e_ready.done(b, hh - 2))
                    elif hh == 0:
                        pe.wait_ge(prev_ready.sem, prev_ready.done(b, -1))
                        pe.wait_ge(toff_ready.sem, toff_ready.done(b, -1))
                    ps = bank[4 + hh % 2]
                    pe.matmul(ps[:].rearrange("p (c l) -> p c l", c=NC), identr[:],
                              neg[:].unsqueeze(1).broadcast_to([P, NC, P]), start=True, stop=False, skip_group_check=True)
                    for c in range(NC):
                        q = c * NH + hh
                        mm = pe.matmul(chunk(ps, c), pairs[:, q:q + 1].broadcast_to([2 * NQ, P]), acs[:],
                                       start=False, stop=(c == NC - 1), skip_group_check=True)
                    mm.then_inc(seg_ps.sem, 1)

            def turn_x(b, g, next_batch):
                xt = xbc_tile(g, 0)
                pe.wait_ge(xbc_ready.sem, xbc_ready.done(b, g * TPU))
                if g == 0:
                    pe.wait_ge(btok_ready.sem, btok_ready.done(b, -1))
                elif g == 1:
                    pe.wait_ge(btok_ready.sem, btok_ready.done(b, 1))
                    pe.wait_ge(ffn_gated.sem, ffn_gated.done(b - 1, 0))
                elif g == UNITS - 1 and next_batch is not None:
                    pe.wait_ge(h_ready[0].sem, h_ready[0].done(next_batch, 1))
                else:
                    pe.wait_ge(btok_ready.sem, btok_ready.done(b, 2 * g - 1))
                for c in range(NC):
                    mm = pe.transpose(chunk(bank[3], c), chunk(xt, c), ident[:])
                mm.then_inc(xT_ps.sem, 1)

            def turn_b(b, g, hh, next_batch):
                bt = xbc_tile(g, 1 + hh)
                pe.wait_ge(xbc_ready.sem, xbc_ready.done(b, g * TPU + 1 + hh))
                if hh:
                    pe.wait_ge(xtok_ready.sem, xtok_ready.done(b, g))
                elif g == 0:
                    pe.wait_ge(yT_ready.sem, yT_ready.done(b, -2))
                elif g == 1:
                    pe.wait_ge(btok_ready.sem, btok_ready.done(b, 0))
                    pe.wait_ge(ffn_gated.sem, ffn_gated.done(b - 1, 1))
                else:
                    pe.wait_ge(yT_ready.sem, yT_ready.done(b, g - 2))
                for c in range(NC):
                    mm = pe.transpose(chunk(bank[(6, 3)[hh]], c), chunk(bt, c), ident[:])
                mm.then_inc(bT_ps.sem, 1)

            def pair_tokens(b, g, hh):
                bt, ctl = xbc_tile(g, 1 + hh), xbc_tile(g, 3 + hh)
                pe.wait_ge(xbc_ready.sem, xbc_ready.done(b, g * TPU + 3 + hh))
                if g == 0:
                    pe.wait_ge(e_ready.sem, e_ready.done(b, NH - 1))
                elif hh == 0:
                    pe.wait_ge(prev_ready.sem, prev_ready.done(b, 3 * g - 1))
                else:
                    pe.wait_ge(toff_ready.sem, toff_ready.done(b, g - 1))
                for c in range(NC):
                    mm = pe.matmul(chunk(bank[4 + hh], c), chunk(bt, c), chunk(ctl, c), start=True, stop=True)
                mm.then_inc(g_ps.sem, 1)

            def states(b, g):
                pe.wait_ge(btok_ready.sem, btok_ready.done(b, 2 * g + 1))
                pe.wait_ge(xw_ready.sem, xw_ready.done(b, g))
                pe.wait_ge(m_ready.sem, m_ready.done(b, 2 * g))
                for hh in range(2):
                    for c in range(NC - 1):
                        at = c * P + hh * HD
                        mm = pe.matmul(bank[4][:, at:at + HD], btok[:, hh * SEQ + c * P:hh * SEQ + (c + 1) * P],
                                       xw[:, at:at + HD], start=True, stop=True)
                mm.then_inc(st_ps.sem, 1)

            def within_chunks(b, g, next_batch):
                pe.wait_ge(m_ready.sem, m_ready.done(b, 2 * g + 1))
                pe.wait_ge(xdt_ready.sem, xdt_ready.done(b, g))
                if g == 0:
                    pe.wait_ge(exin_ready.sem, exin_ready.done(b, 0))
                    pe.wait_ge(gated.sem, gated.done(b - 1, 1))
                elif g == UNITS - 1 and next_batch is not None:
                    pe.wait_ge(dt_step.sem, dt_step.done(next_batch, 0))
                else:
                    pe.wait_ge(ysum_ready.sem, ysum_ready.done(b, g - 1))
                for hh in range(2):
                    for c in range(NC):
                        at = c * P + hh * HD
                        mm = pe.matmul(bank[7][:, at:at + HD], M[:, (2 * g + hh) * SEQ + c * P:(2 * g + hh) * SEQ + (c + 1) * P],
                                       xdt[:, at:at + HD], start=True, stop=True)
                mm.then_inc(ydiag_ps.sem, 1)

            def from_states(b, g):
                ctl = (xbc_tile(g, 3), xbc_tile(g, 4))
                pe.wait_ge(m_ready.sem, m_ready.done(b, 2 * g + 1))
                pe.wait_ge(prev_ready.sem, prev_ready.done(b, 3 * g + 2))
                for hh in range(2):
                    for c in range(1, NC):
                        at = c * P + hh * HD
                        mm = pe.matmul(bank[5][:, at:at + HD], chunk(ctl[hh], c), prev[:, at - P:at - P + HD],
                                       start=True, stop=True)
                mm.then_inc(yoff_ps.sem, 1)

            def turn_y(b, g, next_batch=None):
                if g + 1 < UNITS:
                    pe.wait_ge(btok_ready.sem, btok_ready.done(b, 2 * (g + 1)))
                elif next_batch is not None:
                    pe.wait_ge(btok_ready.sem, btok_ready.done(next_batch, 0))
                else:
                    pe.wait_ge(yT_ready.sem, yT_ready.done(b, g - 1))
                pe.wait_ge(yn_ready.sem, yn_ready.done(b, g))
                for c in range(NC):
                    mm = pe.transpose(chunk(bank[6], c), yg[:, g * SEQ + c * P:g * SEQ + (c + 1) * P], ident[:])
                mm.then_inc(yT_ps.sem, 1)

            def project_out(b, cp, next_batch, units=range(UNITS)):
                pe.wait_ge(yT_ready.sem, yT_ready.done(b, units[-1]))
                if next_batch is None:
                    pe.wait_ge(uv_ready.sem, uv_ready.done(b, TILES - 1))
                elif cp == 0:
                    pe.wait_ge(btok_ready.sem, btok_ready.done(next_batch, 1))
                else:
                    pe.wait_ge(exin_ready.sem, exin_ready.done(next_batch, 0))
                for c in (2 * cp, 2 * cp + 1):
                    for g in units:
                        mm = pe.matmul(attn_bank(b, cp)[:, (c % 2) * DM:(c % 2 + 1) * DM],
                                       yT[:, g * SEQ + c * P:g * SEQ + (c + 1) * P], wo[:, g * DM:(g + 1) * DM],
                                       start=(g == 0 and c % 2 == 0), stop=(g == UNITS - 1), skip_group_check=True)
                if units[-1] == UNITS - 1:
                    mm.then_inc(attn_ps.sem, 1)

            def feed_forward(b, cp, parts):
                pe.wait_ge(h_ready[1].sem, h_ready[1].done(b, parts - 1))
                for c in (2 * cp, 2 * cp + 1):
                    for k in range(KD):
                        mm = pe.matmul(bank[(3, 6)[cp]][:, (c % 2) * DM:(c % 2 + 1) * DM],
                                       h[:, k * SEQ + c * P:k * SEQ + (c + 1) * P], fsum[:, k * DM:(k + 1) * DM],
                                       start=(k == 0), stop=(k == KD - 1))
                mm.then_inc(ffn_ps.sem, 1)

            def unit(b, g, nxt, next_batch):
                def proj(j):
                    if nxt and (g, j) != (1, 0):
                        project(nxt[0], nxt[1] * TPU + j)

                if g == UNITS - 1:
                    turn_x(b, g, next_batch)
                    turn_b(b, g, 0, next_batch)
                    if nxt:
                        pe.wait_ge(hlo_ready.sem, hlo_ready.done(nxt[0], KD - 1))
                    proj(0)
                    pair_tokens(b, g, 0)
                    pair_tokens(b, g, 1)
                    turn_b(b, g, 1, next_batch)
                    proj(1)
                    if nxt:
                        project_dt(nxt[0])
                else:
                    proj(0)
                    turn_x(b, g, next_batch)
                    turn_b(b, g, 0, next_batch)
                    proj(1)
                    turn_b(b, g, 1, next_batch)
                    pair_tokens(b, g, 0)
                    pair_tokens(b, g, 1)
                proj(2)
                states(b, g)
                proj(3)
                within_chunks(b, g, next_batch)
                proj(4)
                if g == UNITS - 2 and next_batch is not None:
                    turn_h(next_batch, 0)
                from_states(b, g)
                turn_y(b, g - 1)
                if g == UNITS - 1 and next_batch is None:
                    project_out(b, 0, None, range(UNITS - 1))
                    project_out(b, 1, None, range(UNITS - 1))

            def turn_to(b, old=None):
                if b is not None:
                    turn_x(b, 0, None)
                    turn_b(b, 0, 0, None)
                    project_z(b, (0, 1, 2))
                    turn_b(b, 0, 1, None)
                    project_z(b, (3,))
                    sum_a(b)
                    project(b, TPU)
                    segments(b, (0, 1))
                    project(b, TPU + 1)
                    segments(b, (2, 3))
                    project(b, TPU + 2)
                    if old is not None:
                        project_out(old, 0, b, (0,))
                    segments(b, (4, 5))
                if old is not None:
                    turn_y(old, UNITS - 1, b)
                if b is not None:
                    project(b, TPU + 3)
                    if old is not None:
                        project_out(old, 0, b, (1, 2))
                    segments(b, (6, 7))

                if old is not None:
                    project_out(old, 0, b, (UNITS - 1,))
                    if b is not None:
                        project_out(old, 1, b, (0, 1))
                if b is not None:
                    pair_tokens(b, 0, 0)
                    pair_tokens(b, 0, 1)
                if old is not None:
                    project_out(old, 1, b, (2, 3) if b is not None else (UNITS - 1,))
                if b is not None:
                    project(b, TPU + 4)
                    states(b, 0)
                    within_chunks(b, 0, None)
                    from_states(b, 0)
                if b is None:
                    for cp in range(2):
                        turn_last_h(old, cp)
                    for cp in range(2):
                        feed_forward(old, cp, 2 * (cp + 1))
                elif old is None:
                    project(b, 2 * TPU)
                else:
                    turn_h(old, 1)
                    project(b, 2 * TPU)
                    feed_forward(old, 0, 2 * KD)
                    feed_forward(old, 1, 2 * KD)

            modulation(0, (0, 1, 2, 3))
            pe.wait_ge(consts, CONSTS)
            turn_h(0, 0)
            pe.wait_ge(hlo_ready.sem, hlo_ready.done(0, KD - 1))
            pe.wait_ge(w_lo_done, 1)
            project(0, 0)
            project(0, 1)
            pe.wait_ge(ld_dt, 16)
            project_dt(0)
            for t in range(2, TPU):
                project(0, t)
            modulation(1, (6, 7, 8, 9))
            gates()
            pe.wait_ge(w_lo_done, 3)
            turn_to(0)
            pe.wait_ge(w_lo_done, 5)
            spread_gates()
            pe.wait_ge(gate_sb, BATCH)
            pe.wait_ge(wo_done, UNITS)
            pe.wait_ge(f_done, 1)

            def batch(b, nb):
                for g in range(1, UNITS):
                    unit(b, g, (b, g + 1) if g + 1 < UNITS else (nb, 0) if nb is not None else None, nb)
                turn_to(nb, b)

            with pe.Fori(0, BATCH - 1) as b:
                batch(b, b + 1)
            batch(BATCH - 1, None)


def kernel(**inputs):
    import numpy as np
    import concourse.bacc as bacc
    from concourse.bass_utils import run_bass_kernel_spmd

    a = {name: np.asarray(v) for name, v in inputs.items()}
    w_in_t = a["L0_attn_W_in"].T
    x0, b0, c0, dt0 = DI, 2 * DI, 2 * DI + NH * NS, 2 * DI + 2 * NH * NS

    def unit_columns(m, base):
        return [np.concatenate([m[..., base + g * P:base + (g + 1) * P],
                                m[..., base + b0 - x0 + g * 2 * P:base + b0 - x0 + (g + 1) * 2 * P],
                                m[..., base + c0 - x0 + g * 2 * P:base + c0 - x0 + (g + 1) * 2 * P]], axis=-1)
                for g in range(UNITS)]

    def rows(m):
        k = m.shape[0] // P
        return np.ascontiguousarray(m.reshape(k, P, -1).transpose(1, 0, 2).reshape(P, -1))

    conv_w = np.concatenate(unit_columns(a["L0_attn_conv_w"].T, 0), axis=-1)
    conv_b = np.concatenate(unit_columns(a["L0_attn_conv_b"][None], 0), axis=-1)
    arrays = {
        "x_in": np.ascontiguousarray(a["L0_attn_hidden_states"]),
        "w_xbc": np.stack([rows(m) for m in unit_columns(w_in_t, x0)]),
        "w_z": rows(w_in_t[:, 0:DI]),
        "w_dt": rows(w_in_t[:, dt0:dt0 + NH]),
        "conv_w": np.ascontiguousarray(conv_w.reshape(TAPS, TILES, P).transpose(2, 1, 0).reshape(P, -1)),
        "conv_b": np.ascontiguousarray(conv_b.reshape(TILES, P).T),
        "a_row": np.ascontiguousarray(np.broadcast_to(a["L0_attn_A"], (P, NH))),
        "d_row": np.ascontiguousarray(np.broadcast_to(a["L0_attn_D"], (P, NH))),
        "dtb_row": np.ascontiguousarray(np.broadcast_to(a["L0_attn_dt_bias"], (P, NH))),
        "norm_w": np.ascontiguousarray(a["L0_attn_norm_weight"].reshape(UNITS, P).T),
        "w_out": rows(a["L0_attn_W_out"].T),
        "factors": np.ascontiguousarray(a["L0_ffn_factors"].reshape(RANK, KD, P, DM).transpose(2, 0, 1, 3).reshape(P, -1)),
        "ffn_bias": np.ascontiguousarray(np.broadcast_to(a["L0_ffn_bias"], (P, DM))),
        "c_t": rows(a["L0_c"].T),
        "w_mod": rows(a["L0_wmod"]),
    }
    nc = bacc.Bacc("TRN2", target_bir_lowering=False, num_devices=1)
    args = [nc.dram_tensor(n, v.shape, mybir.dt.from_np(v.dtype), kind="ExternalInput").ap() for n, v in arrays.items()]
    out = nc.dram_tensor("out", (BATCH, SEQ, DM), F32, kind="ExternalOutput").ap()
    build(nc, *args, out)
    r = run_bass_kernel_spmd(nc, [arrays], core_ids=[0])
    return r.results[0]["out"]
```
